# Optimizing a Trainium2 kernel written in Bass

```python
import numpy as np
import jax
import jax.numpy as jnp

def _softmax(x, axis=-1):
    return jax.nn.softmax(x, axis=axis)

def _gelu(x):
    return jax.nn.gelu(x, approximate=True)

def _silu(x):
    return jax.nn.silu(x)

def _sigmoid(x):
    return jax.nn.sigmoid(x)

def _layernorm(x, axis=-1, eps=1e-05):
    m = jnp.mean(x, axis=axis, keepdims=True)
    v = jnp.var(x, axis=axis, keepdims=True)
    return (x - m) / jnp.sqrt(v + eps)

def _scatter_add(tgt, idx, src, axis=0):
    return tgt.at[idx].add(src)

def _segment_sum(src, seg, n):
    return jax.ops.segment_sum(src, seg, n)
kernel_name = 'mk_vit_tower_d2_tok_img1024_r4_121459'

def setup_inputs(seed: int=0):
    np.random.seed(seed)
    _w = jnp.asarray

    def _rec_inputs():
        import jax
        import jax.numpy as jnp
        _rk = jax.random.key(seed)
        x = -0.00016672 + 0.999947 * jax.random.normal(jax.random.fold_in(_rk, 1), (16, 3, 96, 96), jnp.float32)
        return x
    x = _rec_inputs()

    def _L0_tok_setup():
        import jax, jax.numpy as jnp
        import numpy as np
        PATCH = 16

        def _patchify(x, p):
            B, C, H, W = x.shape
            nh, nw = (H // p, W // p)
            x = x.reshape(B, C, nh, p, nw, p)
            x = x.transpose(0, 2, 4, 1, 3, 5)
            return x.reshape(B, nh * nw, C * p * p)
        key = jax.random.key(seed)
        k1, k2, k3, k4, k5 = jax.random.split(key, 5)
        B, C, H = (64, 3, 96)
        d_model = 256
        p = PATCH
        num_patches = (H // p) ** 2
        in_dim = p * p * C
        x = jax.random.normal(k1, (B, C, H, H), dtype=jnp.float32)
        bound = 1.0 / np.sqrt(in_dim)
        W = jax.random.uniform(k2, (d_model, in_dim), dtype=jnp.float32, minval=-bound, maxval=bound)
        b = jax.random.uniform(k3, (d_model,), dtype=jnp.float32, minval=-bound, maxval=bound)
        cls_token = jax.random.normal(k4, (1, 1, d_model), dtype=jnp.float32)
        pos_enc = jax.random.normal(k5, (1, num_patches + 1, d_model), dtype=jnp.float32)
        return {'x': x, 'W': W, 'b': b, 'cls_token': cls_token, 'pos_enc': pos_enc}
    _L0_tok_all = _L0_tok_setup()
    _L0_tok_in = {k: v for k, v in _L0_tok_all.items() if k in ('W', 'b', 'cls_token', 'pos_enc')}
    del _L0_tok_all

    def _L0_attn_setup():
        import jax, jax.numpy as jnp
        import numpy as np
        EMB = 256
        NH = 4
        INNER = 512
        DH = INNER // NH
        KS = 4
        QKV_BLK = 4
        NHP = INNER // QKV_BLK
        EPS = 1e-06
        LN_EPS = 1e-05

        def _headwise(x, w):
            B, S, _ = x.shape
            xh = x.reshape(B, S, NHP, QKV_BLK)
            return jnp.einsum('bshd,hod->bsho', xh, w).reshape(B, S, -1)

        def _forward(x, w_up, conv_w, conv_b, w_q, w_k, w_v, w_ig, b_ig, w_fg, b_fg, ln_w, skip, w_down):
            B, S, _ = x.shape
            x_inner = x @ w_up.T
            x_m, z = jnp.split(x_inner, 2, axis=-1)
            xc = jax.lax.conv_general_dilated(x_m.transpose(0, 2, 1), conv_w, (1,), [(KS - 1, 0)], dimension_numbers=('NCH', 'OIH', 'NCH'), feature_group_count=INNER)
            xc = (xc + conv_b[None, :, None]).transpose(0, 2, 1)
            xc = jax.nn.silu(xc)
            q = _headwise(xc, w_q)
            k = _headwise(xc, w_k)
            v = _headwise(x_m, w_v)
            ifg_in = jnp.concatenate([q, k, v], axis=-1)
            igp = (ifg_in @ w_ig.T + b_ig).transpose(0, 2, 1)
            fgp = (ifg_in @ w_fg.T + b_fg).transpose(0, 2, 1)
            qh = q.reshape(B, S, NH, DH).transpose(0, 2, 1, 3)
            kh = k.reshape(B, S, NH, DH).transpose(0, 2, 1, 3)
            vh = v.reshape(B, S, NH, DH).transpose(0, 2, 1, 3)
            log_f = jax.nn.log_sigmoid(fgp)
            lc = jnp.concatenate([jnp.zeros((B, NH, 1), x.dtype), jnp.cumsum(log_f, axis=-1)], axis=-1)
            log_fg_mat = lc[:, :, 1:, None] - lc[:, :, None, 1:]
            ltr = jnp.tril(jnp.ones((S, S), bool))
            log_fg_mat = jnp.where(ltr, log_fg_mat, -jnp.inf)
            log_D = log_fg_mat + igp[:, :, None, :]
            max_log_D = jnp.max(log_D, axis=-1, keepdims=True)
            D = jnp.exp(log_D - max_log_D)
            qk = jnp.einsum('bhsd,bhtd->bhst', qh, kh) / float(np.sqrt(DH))
            C = qk * D
            normalizer = jnp.maximum(jnp.abs(C.sum(-1, keepdims=True)), jnp.exp(-max_log_D))
            h = jnp.einsum('bhst,bhtd->bhsd', C / (normalizer + EPS), vh)
            mu = h.mean(-1, keepdims=True)
            var = h.var(-1, keepdims=True)
            hn = (h - mu) / jnp.sqrt(var + LN_EPS) * ln_w[None, :, None, :]
            h_flat = hn.transpose(0, 2, 1, 3).reshape(B, S, INNER)
            h_skip = h_flat + skip * xc
            h_state = h_skip * jax.nn.silu(z)
            return h_state @ w_down.T
        key = jax.random.key(seed)
        ks = jax.random.split(key, 10)
        B, S = (4, 512)
        small_std = float(np.sqrt(2.0 / (5.0 * EMB)))
        blk_std = float(np.sqrt(2.0 / (5.0 * QKV_BLK)))
        return {'x': jax.random.normal(ks[0], (B, S, EMB), jnp.float32), 'w_up': jax.random.normal(ks[1], (2 * INNER, EMB), jnp.float32) * small_std, 'conv_w': jax.random.normal(ks[2], (INNER, 1, KS), jnp.float32) * 0.3, 'conv_b': jnp.zeros((INNER,), jnp.float32), 'w_q': jax.random.normal(ks[3], (NHP, QKV_BLK, QKV_BLK), jnp.float32) * blk_std, 'w_k': jax.random.normal(ks[4], (NHP, QKV_BLK, QKV_BLK), jnp.float32) * blk_std, 'w_v': jax.random.normal(ks[5], (NHP, QKV_BLK, QKV_BLK), jnp.float32) * blk_std, 'w_ig': jax.random.normal(ks[6], (NH, 3 * INNER), jnp.float32) * 0.01, 'b_ig': jnp.full((NH,), -2.0, jnp.float32), 'w_fg': jnp.zeros((NH, 3 * INNER), jnp.float32), 'b_fg': jnp.linspace(3.0, 6.0, NH).astype(jnp.float32), 'ln_w': jnp.ones((NH, DH), jnp.float32), 'skip': jnp.ones((INNER,), jnp.float32), 'w_down': jax.random.normal(ks[7], (EMB, INNER), jnp.float32) * (2.0 / float(np.sqrt(INNER)))}
    _L0_attn_all = _L0_attn_setup()
    _L0_attn_in = {k: v for k, v in _L0_attn_all.items() if k in ('w_up', 'conv_w', 'conv_b', 'w_q', 'w_k', 'w_v', 'w_ig', 'b_ig', 'w_fg', 'b_fg', 'ln_w', 'skip', 'w_down')}
    del _L0_attn_all

    def _L0_ffn_setup():
        import jax, jax.numpy as jnp
        import numpy as np
        B, S, H, I, E, K = (2, 128, 256, 128, 64, 8)
        key = jax.random.key(seed)
        ks = jax.random.split(key, 8)
        return {'hidden_states': jax.random.normal(ks[0], (B, S, H), dtype=jnp.float32), 'router_w': jax.random.normal(ks[1], (H, E), dtype=jnp.float32) * 0.02, 'shared_gate_w': jax.random.normal(ks[2], (H, I), dtype=jnp.float32) * 0.02, 'shared_up_w': jax.random.normal(ks[3], (H, I), dtype=jnp.float32) * 0.02, 'shared_down_w': jax.random.normal(ks[4], (I, H), dtype=jnp.float32) * 0.02, 'expert_gate_k': jax.random.normal(ks[5], (E, H, I), dtype=jnp.float32) * 0.02, 'expert_up_k': jax.random.normal(ks[6], (E, H, I), dtype=jnp.float32) * 0.02, 'expert_down_k': jax.random.normal(ks[7], (E, I, H), dtype=jnp.float32) * 0.02}
    _L0_ffn_all = _L0_ffn_setup()
    _L0_ffn_in = {k: v for k, v in _L0_ffn_all.items() if k in ('router_w', 'shared_gate_w', 'shared_up_w', 'shared_down_w', 'expert_gate_k', 'expert_up_k', 'expert_down_k')}
    del _L0_ffn_all

    def _L1_attn_setup():
        import jax, jax.numpy as jnp
        import numpy as np
        NUM_HEADS = 16
        ROPE_THETA = 10000.0

        def _rope_cos_sin(head_dim, seq_len, theta=ROPE_THETA):
            exps = -jnp.arange(0, head_dim, 2)[:head_dim // 2].astype(jnp.float32) / head_dim
            freqs = theta ** exps
            ang = jnp.arange(seq_len, dtype=jnp.float32)[:, None] * freqs[None, :]
            return (jnp.cos(ang), jnp.sin(ang))

        def _apply_rope(x, cos, sin):
            x2 = x.reshape(*x.shape[:-1], -1, 2)
            xr, xi = (x2[..., 0], x2[..., 1])
            c = cos[None, None]
            s = sin[None, None]
            outr = xr * c - xi * s
            outi = xr * s + xi * c
            return jnp.stack([outr, outi], axis=-1).reshape(x.shape)
        key = jax.random.key(seed)
        ks = jax.random.split(key, 9)
        B, S, D = (2, 512, 256)
        scale = 0.02
        x = jax.random.normal(ks[0], (B, S, D), jnp.float32)
        Wq = jax.random.normal(ks[1], (D, D), jnp.float32) * scale
        bq = jax.random.normal(ks[2], (D,), jnp.float32) * scale
        Wk = jax.random.normal(ks[3], (D, D), jnp.float32) * scale
        bk = jax.random.normal(ks[4], (D,), jnp.float32) * scale
        Wv = jax.random.normal(ks[5], (D, D), jnp.float32) * scale
        bv = jax.random.normal(ks[6], (D,), jnp.float32) * scale
        Wo = jax.random.normal(ks[7], (D, D), jnp.float32) * scale
        return {'x': x, 'Wq': Wq, 'bq': bq, 'Wk': Wk, 'bk': bk, 'Wv': Wv, 'bv': bv, 'Wo': Wo}
    _L1_attn_all = _L1_attn_setup()
    _L1_attn_in = {k: v for k, v in _L1_attn_all.items() if k in ('Wq', 'bq', 'Wk', 'bk', 'Wv', 'bv', 'Wo')}
    del _L1_attn_all

    def _L1_ffn_setup():
        import jax, jax.numpy as jnp
        import numpy as np
        B, S, D_MODEL, D_HIDDEN = (4, 512, 256, 1024)

        def act_quant(x):
            scale = 127.0 / jnp.clip(jnp.max(jnp.abs(x), axis=-1, keepdims=True), 1e-05)
            return jnp.clip(jnp.round(x * scale), -128, 127) / scale

        def weight_quant(w):
            scale = 1.0 / jnp.clip(jnp.mean(jnp.abs(w)), 1e-05)
            return jnp.clip(jnp.round(w * scale), -1, 1) / scale

        def bit_linear(x, w):
            xq = x + jax.lax.stop_gradient(act_quant(x) - x)
            wq = w + jax.lax.stop_gradient(weight_quant(w) - w)
            return jnp.einsum('bsd,hd->bsh', xq, wq)

        def depthwise_conv1d(x_bcl, w, b):
            y = jax.lax.conv_general_dilated(x_bcl, w, window_strides=(1,), padding=[(1, 1)], dimension_numbers=('NCH', 'OIH', 'NCH'), feature_group_count=x_bcl.shape[1])
            return y + b[None, :, None]
        key = jax.random.key(seed)
        ks = jax.random.split(key, 5)
        lim1 = 1.0 / np.sqrt(D_MODEL)
        lim2 = 1.0 / np.sqrt(D_HIDDEN)
        limc = 1.0 / np.sqrt(3.0)
        return {'x': jax.random.normal(ks[0], (B, S, D_MODEL), dtype=jnp.float32), 'w1': jax.random.uniform(ks[1], (D_HIDDEN, D_MODEL), jnp.float32, -lim1, lim1), 'conv_w': jax.random.uniform(ks[2], (D_HIDDEN, 1, 3), jnp.float32, -limc, limc), 'conv_b': jax.random.uniform(ks[3], (D_HIDDEN,), jnp.float32, -limc, limc), 'w2': jax.random.uniform(ks[4], (D_MODEL, D_HIDDEN), jnp.float32, -lim2, lim2)}
    _L1_ffn_all = _L1_ffn_setup()
    _L1_ffn_in = {k: v for k, v in _L1_ffn_all.items() if k in ('w1', 'conv_w', 'conv_b', 'w2')}
    del _L1_ffn_all
    return {'x': x, 'L0_tok_W': _L0_tok_in['W'], 'L0_tok_b': _L0_tok_in['b'], 'L0_tok_cls_token': _L0_tok_in['cls_token'], 'L0_tok_pos_enc': _L0_tok_in['pos_enc'], 'L0_attn_w_up': _L0_attn_in['w_up'], 'L0_attn_conv_w': _L0_attn_in['conv_w'], 'L0_attn_conv_b': _L0_attn_in['conv_b'], 'L0_attn_w_q': _L0_attn_in['w_q'], 'L0_attn_w_k': _L0_attn_in['w_k'], 'L0_attn_w_v': _L0_attn_in['w_v'], 'L0_attn_w_ig': _L0_attn_in['w_ig'], 'L0_attn_b_ig': _L0_attn_in['b_ig'], 'L0_attn_w_fg': _L0_attn_in['w_fg'], 'L0_attn_b_fg': _L0_attn_in['b_fg'], 'L0_attn_ln_w': _L0_attn_in['ln_w'], 'L0_attn_skip': _L0_attn_in['skip'], 'L0_attn_w_down': _L0_attn_in['w_down'], 'L0_ffn_router_w': _L0_ffn_in['router_w'], 'L0_ffn_shared_gate_w': _L0_ffn_in['shared_gate_w'], 'L0_ffn_shared_up_w': _L0_ffn_in['shared_up_w'], 'L0_ffn_shared_down_w': _L0_ffn_in['shared_down_w'], 'L0_ffn_expert_gate_k': _L0_ffn_in['expert_gate_k'], 'L0_ffn_expert_up_k': _L0_ffn_in['expert_up_k'], 'L0_ffn_expert_down_k': _L0_ffn_in['expert_down_k'], 'L1_attn_Wq': _L1_attn_in['Wq'], 'L1_attn_bq': _L1_attn_in['bq'], 'L1_attn_Wk': _L1_attn_in['Wk'], 'L1_attn_bk': _L1_attn_in['bk'], 'L1_attn_Wv': _L1_attn_in['Wv'], 'L1_attn_bv': _L1_attn_in['bv'], 'L1_attn_Wo': _L1_attn_in['Wo'], 'L1_ffn_w1': _L1_ffn_in['w1'], 'L1_ffn_conv_w': _L1_ffn_in['conv_w'], 'L1_ffn_conv_b': _L1_ffn_in['conv_b'], 'L1_ffn_w2': _L1_ffn_in['w2']}

def reference(x, L0_tok_W, L0_tok_b, L0_tok_cls_token, L0_tok_pos_enc, L0_attn_w_up, L0_attn_conv_w, L0_attn_conv_b, L0_attn_w_q, L0_attn_w_k, L0_attn_w_v, L0_attn_w_ig, L0_attn_b_ig, L0_attn_w_fg, L0_attn_b_fg, L0_attn_ln_w, L0_attn_skip, L0_attn_w_down, L0_ffn_router_w, L0_ffn_shared_gate_w, L0_ffn_shared_up_w, L0_ffn_shared_down_w, L0_ffn_expert_gate_k, L0_ffn_expert_up_k, L0_ffn_expert_down_k, L1_attn_Wq, L1_attn_bq, L1_attn_Wk, L1_attn_bk, L1_attn_Wv, L1_attn_bv, L1_attn_Wo, L1_ffn_w1, L1_ffn_conv_w, L1_ffn_conv_b, L1_ffn_w2):
    import jax
    import jax.numpy as jnp

    def _L0_tok_ref(x, W, b, cls_token, pos_enc):
        import jax, jax.numpy as jnp
        import numpy as np
        PATCH = 16

        def _patchify(x, p):
            B, C, H, W = x.shape
            nh, nw = (H // p, W // p)
            x = x.reshape(B, C, nh, p, nw, p)
            x = x.transpose(0, 2, 4, 1, 3, 5)
            return x.reshape(B, nh * nw, C * p * p)
        B = x.shape[0]
        patches = _patchify(x, PATCH)
        proj = jnp.einsum('bnf,df->bnd', patches, W) + b
        cls = jnp.broadcast_to(cls_token, (B, 1, cls_token.shape[-1]))
        out = jnp.concatenate([cls, proj], axis=1) + pos_enc
        return out

    def _L0_attn_ref(x, w_up, conv_w, conv_b, w_q, w_k, w_v, w_ig, b_ig, w_fg, b_fg, ln_w, skip, w_down):
        import jax, jax.numpy as jnp
        import numpy as np
        EMB = 256
        NH = 4
        INNER = 512
        DH = INNER // NH
        KS = 4
        QKV_BLK = 4
        NHP = INNER // QKV_BLK
        EPS = 1e-06
        LN_EPS = 1e-05

        def _headwise(x, w):
            B, S, _ = x.shape
            xh = x.reshape(B, S, NHP, QKV_BLK)
            return jnp.einsum('bshd,hod->bsho', xh, w).reshape(B, S, -1)

        def _forward(x, w_up, conv_w, conv_b, w_q, w_k, w_v, w_ig, b_ig, w_fg, b_fg, ln_w, skip, w_down):
            B, S, _ = x.shape
            x_inner = x @ w_up.T
            x_m, z = jnp.split(x_inner, 2, axis=-1)
            xc = jax.lax.conv_general_dilated(x_m.transpose(0, 2, 1), conv_w, (1,), [(KS - 1, 0)], dimension_numbers=('NCH', 'OIH', 'NCH'), feature_group_count=INNER)
            xc = (xc + conv_b[None, :, None]).transpose(0, 2, 1)
            xc = jax.nn.silu(xc)
            q = _headwise(xc, w_q)
            k = _headwise(xc, w_k)
            v = _headwise(x_m, w_v)
            ifg_in = jnp.concatenate([q, k, v], axis=-1)
            igp = (ifg_in @ w_ig.T + b_ig).transpose(0, 2, 1)
            fgp = (ifg_in @ w_fg.T + b_fg).transpose(0, 2, 1)
            qh = q.reshape(B, S, NH, DH).transpose(0, 2, 1, 3)
            kh = k.reshape(B, S, NH, DH).transpose(0, 2, 1, 3)
            vh = v.reshape(B, S, NH, DH).transpose(0, 2, 1, 3)
            log_f = jax.nn.log_sigmoid(fgp)
            lc = jnp.concatenate([jnp.zeros((B, NH, 1), x.dtype), jnp.cumsum(log_f, axis=-1)], axis=-1)
            log_fg_mat = lc[:, :, 1:, None] - lc[:, :, None, 1:]
            ltr = jnp.tril(jnp.ones((S, S), bool))
            log_fg_mat = jnp.where(ltr, log_fg_mat, -jnp.inf)
            log_D = log_fg_mat + igp[:, :, None, :]
            max_log_D = jnp.max(log_D, axis=-1, keepdims=True)
            D = jnp.exp(log_D - max_log_D)
            qk = jnp.einsum('bhsd,bhtd->bhst', qh, kh) / float(np.sqrt(DH))
            C = qk * D
            normalizer = jnp.maximum(jnp.abs(C.sum(-1, keepdims=True)), jnp.exp(-max_log_D))
            h = jnp.einsum('bhst,bhtd->bhsd', C / (normalizer + EPS), vh)
            mu = h.mean(-1, keepdims=True)
            var = h.var(-1, keepdims=True)
            hn = (h - mu) / jnp.sqrt(var + LN_EPS) * ln_w[None, :, None, :]
            h_flat = hn.transpose(0, 2, 1, 3).reshape(B, S, INNER)
            h_skip = h_flat + skip * xc
            h_state = h_skip * jax.nn.silu(z)
            return h_state @ w_down.T
        return _forward(x, w_up, conv_w, conv_b, w_q, w_k, w_v, w_ig, b_ig, w_fg, b_fg, ln_w, skip, w_down)

    def _L0_ffn_ref(hidden_states, router_w, shared_gate_w, shared_up_w, shared_down_w, expert_gate_k, expert_up_k, expert_down_k):
        import jax, jax.numpy as jnp
        import numpy as np
        B, S, H, I, E, K = (2, 128, 256, 128, 64, 8)
        logits = jnp.einsum('bsh,he->bse', hidden_states.astype(jnp.float32), router_w)
        affinity = jax.nn.sigmoid(logits)
        top_scores, top_idx = jax.lax.top_k(affinity, K)
        top_w = top_scores / (jnp.sum(top_scores, axis=-1, keepdims=True) + 1e-09)
        one_hot = jax.nn.one_hot(top_idx, E, dtype=top_w.dtype)
        router_mask = jnp.einsum('bske,bsk->bse', one_hot, top_w).astype(hidden_states.dtype)
        shared = jnp.einsum('bsi,ih->bsh', jax.nn.silu(hidden_states @ shared_gate_w) * (hidden_states @ shared_up_w), shared_down_w)
        gate_out = jnp.einsum('bsh,ehi->bsei', hidden_states, expert_gate_k)
        up_out = jnp.einsum('bsh,ehi->bsei', hidden_states, expert_up_k)
        expert_act = jax.nn.silu(gate_out) * up_out
        routed = jnp.einsum('bsei,eih->bsh', expert_act * router_mask[..., None], expert_down_k)
        return shared + routed

    def _L1_attn_ref(x, Wq, bq, Wk, bk, Wv, bv, Wo):
        import jax, jax.numpy as jnp
        import numpy as np
        NUM_HEADS = 16
        ROPE_THETA = 10000.0

        def _rope_cos_sin(head_dim, seq_len, theta=ROPE_THETA):
            exps = -jnp.arange(0, head_dim, 2)[:head_dim // 2].astype(jnp.float32) / head_dim
            freqs = theta ** exps
            ang = jnp.arange(seq_len, dtype=jnp.float32)[:, None] * freqs[None, :]
            return (jnp.cos(ang), jnp.sin(ang))

        def _apply_rope(x, cos, sin):
            x2 = x.reshape(*x.shape[:-1], -1, 2)
            xr, xi = (x2[..., 0], x2[..., 1])
            c = cos[None, None]
            s = sin[None, None]
            outr = xr * c - xi * s
            outi = xr * s + xi * c
            return jnp.stack([outr, outi], axis=-1).reshape(x.shape)
        B, S, D = x.shape
        H = NUM_HEADS
        hd = D // H
        q = (x @ Wq.T + bq).reshape(B, S, H, hd).transpose(0, 2, 1, 3)
        k = (x @ Wk.T + bk).reshape(B, S, H, hd).transpose(0, 2, 1, 3)
        v = (x @ Wv.T + bv).reshape(B, S, H, hd).transpose(0, 2, 1, 3)
        cos, sin = _rope_cos_sin(hd, S)
        q = _apply_rope(q, cos, sin)
        k = _apply_rope(k, cos, sin)
        inv_scale = 1.0 / jnp.sqrt(jnp.asarray(D, jnp.float32))
        scores = jax.nn.softmax(jnp.einsum('bhqd,bhkd->bhqk', q, k) * inv_scale, axis=-1)
        out = jnp.einsum('bhqk,bhkd->bhqd', scores, v)
        out = out.transpose(0, 2, 1, 3).reshape(B, S, D)
        return out @ Wo.T

    def _L1_ffn_ref(x, w1, conv_w, conv_b, w2):
        import jax, jax.numpy as jnp
        import numpy as np
        B, S, D_MODEL, D_HIDDEN = (4, 512, 256, 1024)

        def act_quant(x):
            scale = 127.0 / jnp.clip(jnp.max(jnp.abs(x), axis=-1, keepdims=True), 1e-05)
            return jnp.clip(jnp.round(x * scale), -128, 127) / scale

        def weight_quant(w):
            scale = 1.0 / jnp.clip(jnp.mean(jnp.abs(w)), 1e-05)
            return jnp.clip(jnp.round(w * scale), -1, 1) / scale

        def bit_linear(x, w):
            xq = x + jax.lax.stop_gradient(act_quant(x) - x)
            wq = w + jax.lax.stop_gradient(weight_quant(w) - w)
            return jnp.einsum('bsd,hd->bsh', xq, wq)

        def depthwise_conv1d(x_bcl, w, b):
            y = jax.lax.conv_general_dilated(x_bcl, w, window_strides=(1,), padding=[(1, 1)], dimension_numbers=('NCH', 'OIH', 'NCH'), feature_group_count=x_bcl.shape[1])
            return y + b[None, :, None]
        h = bit_linear(x, w1)
        h = depthwise_conv1d(h.transpose(0, 2, 1), conv_w, conv_b)
        h = h.transpose(0, 2, 1)
        h = jax.nn.silu(h)
        return bit_linear(h, w2)
    h = _L0_tok_ref(x, L0_tok_W, L0_tok_b, L0_tok_cls_token, L0_tok_pos_enc)
    h = h + _L0_attn_ref(_layernorm(h, axis=-1), L0_attn_w_up, L0_attn_conv_w, L0_attn_conv_b, L0_attn_w_q, L0_attn_w_k, L0_attn_w_v, L0_attn_w_ig, L0_attn_b_ig, L0_attn_w_fg, L0_attn_b_fg, L0_attn_ln_w, L0_attn_skip, L0_attn_w_down)
    h = h + _L0_ffn_ref(_layernorm(h, axis=-1), L0_ffn_router_w, L0_ffn_shared_gate_w, L0_ffn_shared_up_w, L0_ffn_shared_down_w, L0_ffn_expert_gate_k, L0_ffn_expert_up_k, L0_ffn_expert_down_k)
    h = h + _L1_attn_ref(_layernorm(h, axis=-1), L1_attn_Wq, L1_attn_bq, L1_attn_Wk, L1_attn_bk, L1_attn_Wv, L1_attn_bv, L1_attn_Wo)
    h = h + _L1_ffn_ref(_layernorm(h, axis=-1), L1_ffn_w1, L1_ffn_conv_w, L1_ffn_conv_b, L1_ffn_w2)
    return h

_drawn_inputs = setup_inputs


def setup_inputs(seed=0):
    import zlib

    import numpy as np

    out = dict(_drawn_inputs(seed))
    spreads = {'L0_attn_conv_b': (0.0, 0.1),
     'L0_attn_b_ig': (-2.0, 0.2),
     'L0_attn_w_fg': (0.0, 0.1),
     'L0_attn_ln_w': (1.0, 0.2),
     'L0_attn_skip': (1.0, 0.6)}
    factors = {'L0_ffn_router_w': 8.0,
     'L0_ffn_shared_gate_w': 6.172,
     'L0_ffn_shared_up_w': 6.287,
     'L0_ffn_shared_down_w': 6.174,
     'L0_ffn_expert_gate_k': 8.0,
     'L0_ffn_expert_up_k': 8.0,
     'L0_ffn_expert_down_k': 8.0,
     'L1_attn_Wq': 8.0,
     'L1_attn_bq': 43.655,
     'L1_attn_Wk': 8.0,
     'L1_attn_bk': 64.0,
     'L1_attn_Wv': 4.299,
     'L1_attn_bv': 8.0,
     'L1_attn_Wo': 3.969,
     'L1_ffn_w1': 4.84,
     'L1_ffn_conv_w': 4.849,
     'L1_ffn_conv_b': 4.043,
     'L1_ffn_w2': 3.15}
    for name, (base, spread) in spreads.items():
        noise = np.random.default_rng([zlib.crc32(name.encode()), seed]).standard_normal(out[name].shape)
        drawn = base * np.exp(spread * noise) if base else spread * noise
        out[name] = jnp.asarray(drawn.astype(out[name].dtype))
    for name, factor in factors.items():
        out[name] = (out[name] * factor).astype(out[name].dtype)
    return out
```

```python
from contextlib import ExitStack

import concourse.bass as bass
from concourse import mybir

F32 = mybir.dt.float32
F16 = mybir.dt.float16
BF16 = mybir.dt.bfloat16
ALU = mybir.AluOpType
ACT = mybir.ActivationFunctionType
AX = mybir.AxisListType.X

B, PATCHES, POS = 16, 36, 37
T = B * POS
HB = B // 2
HT = HB * POS
G, GT = B // 2, 2 * POS
D, DC = 256, 2
TOK_K = 6
INNER_C = 4
DH = 128
CONV = 4
E = 64
WE = 768
H1, HD1 = 16, 16
H1C = 8
QH = 9
FC = 8
MAGIC = 1.5 * 2.0 ** 23
NEG = -1.0e30

COLS = {}
_n = 0
for _name, _w in (("tok_b", DC), ("cls", DC), ("conv_w", INNER_C * CONV), ("conv_b", INNER_C),
                  ("ln_w", INNER_C), ("skip", INNER_C), ("gate_b", 1), ("bq", DC), ("bq_swap", DC),
                  ("bk", DC), ("bk_swap", DC), ("bv", DC), ("ffn_conv_w", FC * 3), ("ffn_conv_b", FC)):
    COLS[_name] = (_n, _n + _w)
    _n += _w
NCOLS = _n


def vit_tower(nc: bass.Bass, patches, tok_w, pos, cols, w_up, blocks, blocks_t, w_gates, w_down,
              w_router, w_shared, w_experts, l1_w, rope, ffn_w1, ffn_w2, out):
    with ExitStack() as ctx:
        def sb(name, shape, dt=F32):
            return ctx.enter_context(nc.sbuf_tensor(name, shape, dt))

        def sem(name):
            return ctx.enter_context(nc.semaphore(name))

        bank = [ctx.enter_context(nc.psum_tensor(f"bank{i}", [128, 512], F32)) for i in range(8)]

        colp = sb("colp", [128, NCOLS])
        posw = sb("posw", [128, DC, POS])
        blk = sb("blk", [128, 12, 4])
        blk_t = sb("blk_t", [128, 12, 4])
        wg = sb("wg", [128, 12, 64])
        wup = sb("wup", [128, DC, 1024])
        wdn = sb("wdn", [128, INNER_C, D])
        wrt = sb("wrt", [128, DC, E])
        l1w = sb("l1w", [128, 6, DC, D])
        ropew = sb("ropew", [128, 2, POS])
        ident = sb("ident", [128, 128])
        zero_w = sb("zero_w", [128, 128], F16)
        ident_h = sb("ident_h", [128, 128], F16)
        mean_w = sb("mean_w", [128, 128])
        ones = sb("ones", [128, 128])
        in_block = sb("in_block", [128, 32])
        head_col = sb("head_col", [128, H1C])
        expert_sel = sb("expert_sel", [128, E], F16)
        head_row = sb("head_row", [INNER_C, INNER_C, GT])
        causal = sb("causal", [GT, INNER_C, GT])
        restart_mul = sb("restart_mul", [INNER_C, B, POS])
        restart_add = sb("restart_add", [INNER_C, B, POS])
        magic_col = sb("magic_col", [128, 1])
        eps_col = sb("eps_col", [128, 1])
        h = sb("h", [128, DC, T])
        xn = sb("xn", [128, DC, T])
        sq = sb("sq", [128, DC, T])
        rstd = sb("rstd", [128, T])
        posb = sb("posb", [128, DC, POS])
        cls0 = sb("cls0", [128, DC])
        w1q = sb("w1q", [128, DC, 1024], BF16)
        w2q = sb("w2q", [128, FC, D], BF16)
        wabs = sb("wabs", [128, 2])
        wscale = sb("wscale", [128, 2])
        wmean = sb("wmean", [128, 2])

        arena = sb("arena", [128, 24064])
        where = [0]

        def take(n, start=None):
            if start is not None:
                where[0] = start
            a = where[0]
            where[0] += n
            assert where[0] <= 24064, where
            return arena[:, a:a + n]

        xm = take(INNER_C * T, 0).rearrange("p (c t) -> p c t", c=INNER_C)
        zs = take(INNER_C * T).rearrange("p (c t) -> p c t", c=INNER_C)
        xc = take(INNER_C * T).rearrange("p (c t) -> p c t", c=INNER_C)
        bd = take(12 * 128).rearrange("p (n m) -> p n m", n=12)
        bd_t = take(12 * 128).rearrange("p (n m) -> p n m", n=12)
        qT = take(INNER_C * T).rearrange("p (c t) -> p c t", c=INNER_C)
        kT = take(INNER_C * T).rearrange("p (c t) -> p c t", c=INNER_C)
        v = take(G * 512).rearrange("p (g m) -> p g m", g=G)
        hraw = take(G * 512).rearrange("p (g m) -> p g m", g=G)
        lf = hraw.rearrange("p g m -> p (g m)")[0:INNER_C, 0:4 * T].rearrange("p (n t) -> p n t", n=4)
        hst = qT
        cacc = kT
        patch_sb = arena[:, where[0] - G * 1024:where[0] - G * 1024 + TOK_K * B * PATCHES].rearrange(
            "p (k t) -> p k t", k=TOK_K)
        tokw = arena[:, where[0] - G * 1024 + TOK_K * B * PATCHES:
                     where[0] - G * 1024 + TOK_K * B * PATCHES + TOK_K * D].rearrange("p (k m) -> p k m", k=TOK_K)
        wraw1 = sb("wraw1", [128, DC, 1024])
        wraw2 = wup[:, :, :].rearrange("p a b -> p (a b)").rearrange("p (k m) -> p k m", k=FC)
        aff = take(G * E, 0).rearrange("p (g e) -> p g e", g=G)[0:GT]
        rest = take(G * E).rearrange("p (g e) -> p g e", g=G)[0:GT]
        mask_hl = take(G * E).bitcast(F16).rearrange("p (g e) -> p g e", g=G)[0:GT]
        maskT = take(T // 2).bitcast(F16)
        xhi = take(DC * T // 2).bitcast(F16).rearrange("p (c t) -> p c t", c=DC)
        xlo = take(DC * T // 2).bitcast(F16).rearrange("p (c t) -> p c t", c=DC)
        sg = take(2 * HT).rearrange("p (s t) -> p s t", s=2)
        gu = take(2 * HT).rearrange("p (s t) -> p s t", s=2)
        act = take(2 * HT).rearrange("p (s t) -> p s t", s=2)
        ahi = take(HT).bitcast(F16).rearrange("p (s t) -> p s t", s=2)
        alo = take(HT).bitcast(F16).rearrange("p (s t) -> p s t", s=2)
        whi = take(2 * WE).bitcast(F16).rearrange("p (s m) -> p s m", s=4)
        wlo = take(2 * WE).bitcast(F16).rearrange("p (s m) -> p s m", s=4)
        qr = take(DC * T, 0).rearrange("p (c t) -> p c t", c=DC)
        kr = take(DC * T).rearrange("p (c t) -> p c t", c=DC)
        rt = take(4 * HT).rearrange("p (s c t) -> p s c t", s=2, c=2)
        qm = take(DC * B * QH * POS).rearrange("p (c b h t) -> p c b h t", c=DC, b=B, h=QH)
        vb = take(B * D).rearrange("p (b m) -> p b m", b=B)
        pr = take(2 * 2 * 6 * POS).rearrange("p (s n t) -> p s n t", s=2, n=12)
        pT = take(2 * 2 * 333).rearrange("p (s c m) -> p s c m", s=2, c=2)
        otok = vb
        oT = qr
        hid = take(FC * T, 0).rearrange("p (c t) -> p c t", c=FC)
        h2 = take(FC * T).rearrange("p (c t) -> p c t", c=FC)
        h2q = take(FC * T // 2).bitcast(BF16).rearrange("p (c t) -> p c t", c=FC)
        x4q = take(DC * T // 2).bitcast(BF16).rearrange("p (c t) -> p c t", c=DC)
        habs = take(FC * T).rearrange("p (c t) -> p c t", c=FC)
        amax = take(T)
        bscale = take(T)
        binv = take(T)
        gts = sb("gts", [64, T])
        arow = sb("arow", [INNER_C, T])
        mrow = sb("mrow", [INNER_C, T])
        lcum = sb("lcum", [INNER_C, T])
        nrow = sb("nrow", [INNER_C, T])
        geff = sb("geff", [128, 8, 64])
        dmat = sb("dmat", [GT, 2, INNER_C, GT])
        cmat = sb("cmat", [GT, 2, INNER_C, GT])
        floor_t = sb("floor_t", [GT, G * INNER_C])
        csum = sb("csum", [GT, G * INNER_C])
        stat = sb("stat", [GT, G * INNER_C, 6])
        mv = sb("mv", [GT, G * INNER_C, 2])
        tiny = sb("tiny", [GT, 6, G * INNER_C])
        top = sb("top", [GT, G, 8])
        den = sb("den", [GT, 3, G])
        stage = sb("stage", [128, 4, WE])
        shared_w = sb("shared_w", [128, WE])
        smx = sb("smx", [128, 2, 3, 12])
        tmx = sb("tmx", [GT, G])
        tsc = sb("tsc", [GT, 2, G])
        tscT = sb("tscT", [2 * G, GT])

        def col(name, i=0, rows=slice(0, 128)):
            a = COLS[name][0] + i
            return colp[rows, a:a + 1]

        ld_first = sem("ld_first")
        ld_attn = sem("ld_attn")
        ld_ffn = sem("ld_ffn")
        ld_bit = sem("ld_bit")
        ld_stage = [sem("ld_stage_a"), sem("ld_stage_b")]
        consts = sem("consts")
        pool_step = sem("pool_step")
        vec_step = sem("vec_step")
        act_step = sem("act_step")
        wscaled, wmean_done, wq_done = sem("wscaled"), sem("wmean_done"), sem("wq_done")
        wabs_done = sem("wabs_done")
        wmean_mm = sem("wmean_mm")
        bd_done = sem("bd_done")
        tok_mm = sem("tok_mm")
        h_ready = sem("h_ready")
        ln_mean, ln_cent, ln_sq = sem("ln_mean"), sem("ln_cent"), sem("ln_sq")
        ln_var, ln_std, xn_ready = sem("ln_var"), sem("ln_std"), sem("xn_ready")
        geff_mm, geff_done = sem("geff_mm"), sem("geff_done")
        up_mm, xm_done, zs_done = sem("up_mm"), sem("xm_done"), sem("zs_done")
        conv_first, conv_done, xc_ready = sem("conv_first"), sem("conv_done"), sem("xc_ready")
        qk_mm, q_done, k_done = sem("qk_mm"), sem("q_done"), sem("k_done")
        gates_mm, gts_done = sem("gates_mm"), sem("gts_done")
        v_mm, v_done = sem("v_mm"), sem("v_done")
        absf_done, lnf_done, arow_done = sem("absf_done"), sem("lnf_done"), sem("arow_done")
        nrow_in, nrow_done, floor_mm = sem("nrow_in"), sem("nrow_done"), sem("floor_mm")
        s_mm, e_mm, d_done, c_done = sem("s_mm"), sem("e_mm"), sem("d_done"), sem("c_done")
        hv_mm, hraw_done, hstat_done = sem("hv_mm"), sem("hraw_done"), sem("hstat_done")
        hvar_done, hstd_done, hn_done = sem("hvar_done"), sem("hstd_done"), sem("hn_done")
        skip_done, ht_mm, hst_done, down0_mm = sem("skip_done"), sem("ht_mm"), sem("hst_done"), sem("down0_mm")
        route_mm, aff_done, mask_done, maskt_mm, maskt_done = (
            sem("route_mm"), sem("aff_done"), sem("mask_done"), sem("maskt_mm"), sem("maskt_done"))
        xhi_done, xlo_done = sem("xhi_done"), sem("xlo_done")
        whi_done, wlo_done = sem("whi_done"), sem("wlo_done")
        gate_mm, uproj_mm, mask_mm, down_mm = sem("gate_mm"), sem("uproj_mm"), sem("mask_mm"), sem("down_mm")
        silu_done, gu_done, act_done, alo_done = (
            sem("silu_done"), sem("gu_done"), sem("act_done"), sem("alo_done"))
        ahi_done = sem("ahi_done")
        rope_mm, rope_t, rope_done, qm_done = sem("rope_mm"), sem("rope_t"), sem("rope_done"), sem("qm_done")
        vb_mm, vb_done = sem("vb_mm"), sem("vb_done")
        sc_mm, sc_sub, sc_exp, p_done = sem("sc_mm"), sem("sc_sub"), sem("sc_exp"), sem("p_done")
        pt_mm, pt_done, pv_mm, ot_done = sem("pt_mm"), sem("pt_done"), sem("pv_mm"), sem("ot_done")
        ott_mm, oT_done, wo_mm = sem("ott_mm"), sem("oT_done"), sem("wo_mm")
        amax_done, amaxt_mm, tsc_done, tsct_mm, tsct_done, bc_mm, bc_done = (
            sem("amax_done"), sem("amaxt_mm"), sem("tsc_done"), sem("tsct_mm"), sem("tsct_done"),
            sem("bc_mm"), sem("bc_done"))
        quant_mul, xq_done = sem("quant_mul"), sem("xq_done")
        w1_mm, hid_done, fconv_first, fconv_done, h2_done, habs_done, w2_mm = (
            sem("w1_mm"), sem("hid_done"), sem("fconv_first"), sem("fconv_done"), sem("h2_done"), sem("habs_done"), sem("w2_mm"))
        stored = sem("stored")

        block = ctx.enter_context(nc.Block())

        def half(x, c, hf):
            return x[:, c, hf * HT:(hf + 1) * HT]

        def images(ap):
            return ap.rearrange("p (b t) -> p b t", t=POS)

        LOOPS = E // 4 - 1

        @block.sync
        def _(sp):
            sp.dma_start(patch_sb, patches).then_inc(ld_first, 16)
            sp.dma_start(tokw, tok_w).then_inc(ld_first, 16)
            sp.dma_start(posw[:, :, :], pos).then_inc(ld_first, 16)
            sp.dma_start(colp[:, :], cols).then_inc(ld_first, 16)
            for dst, src in ((blk[:, :, :], blocks), (blk_t[:, :, :], blocks_t), (wg[:, :, :], w_gates),
                             (wup[:, :, :], w_up), (wdn[:, :, :], w_down)):
                sp.dma_start(dst, src).then_inc(ld_attn, 16)
            for dst, src in ((wrt[:, :, :], w_router), (shared_w[:, :], w_shared)):
                sp.dma_start(dst, src).then_inc(ld_ffn, 16)
            for s in range(2):
                sp.dma_start(stage[:, 2 * s:2 * s + 2, :], w_experts[:, 2 * s:2 * s + 2, :]).then_inc(ld_stage[s], 16)
            for dst, src in ((wraw1[:, :, :], ffn_w1), (l1w[:, :, :, :], l1_w), (ropew[:, :, :], rope)):
                sp.dma_start(dst, src).then_inc(ld_bit, 16)
            sp.wait_ge(up_mm, 16)
            sp.dma_start(wraw2, ffn_w2).then_inc(ld_bit, 16)
            with sp.Fori(0, LOOPS) as it:
                for s in range(2):
                    sp.wait_ge(wlo_done, it * 4 + 2 * s + 3)
                    sp.dma_start(stage[:, 2 * s:2 * s + 2, :],
                                 w_experts[:, bass.ds(it * 4 + 4 + 2 * s, 2), :]).then_inc(ld_stage[s], 16)
            sp.wait_ge(h_ready, 20)
            sp.dma_start(out, h[:, :, :]).then_inc(stored, 16)
            sp.wait_ge(stored, 16)

        @block.gpsimd
        def _(pool):
            pool.memset(ones[:, :], 1.0).then_inc(pool_step, 1)
            pool.memset(mean_w[:, :], 1.0 / D)
            pool.memset(eps_col[:, :], 1e-5)
            pool.memset(magic_col[:, :], MAGIC)
            pool.memset(zero_w[:, :], 0.0)
            pool.wait_ge(pool_step, 1)
            pool.affine_select(out=ident[:, :], in_=ones[:, :], compare_op=ALU.is_equal, fill=0.0,
                               base=0, pattern=[[-1, 128]], channel_multiplier=1).then_inc(pool_step, 1)
            pool.affine_select(out=in_block[:, :], in_=ones[:, 0:32], compare_op=ALU.is_ge, fill=0.0,
                               base=0, pattern=[[-4, 32]], channel_multiplier=1).then_inc(pool_step, 1)
            pool.wait_ge(pool_step, 3)
            pool.affine_select(out=in_block[:, :], in_=in_block[:, :], compare_op=ALU.is_ge, fill=0.0,
                               base=3, pattern=[[4, 32]], channel_multiplier=-1).then_inc(consts, 1)
            pool.memset(head_row[:, :, :], 1.0)
            pool.memset(causal[:, :, :], 0.0).then_inc(pool_step, 1)
            pool.wait_ge(pool_step, 4)
            pool.affine_select(out=head_row[:, :, :], in_=head_row[:, :, :], compare_op=ALU.is_equal, fill=0.0,
                               base=0, pattern=[[-1, INNER_C], [0, GT]], channel_multiplier=1)
            pool.affine_select(out=causal[:, :, :], in_=causal[:, :, :], compare_op=ALU.is_ge, fill=NEG,
                               base=0, pattern=[[0, INNER_C], [1, GT]], channel_multiplier=-1).then_inc(pool_step, 1)
            pool.wait_ge(pool_step, 5)
            pool.affine_select(out=causal[:, :, POS:GT], in_=causal[:, :, POS:GT], compare_op=ALU.is_ge, fill=NEG,
                               base=-POS, pattern=[[0, INNER_C], [0, POS]], channel_multiplier=1)
            pool.memset(restart_mul[:, :, :], 1.0)
            pool.memset(restart_add[:, :, :], 0.0).then_inc(pool_step, 1)
            pool.wait_ge(pool_step, 6)
            pool.memset(restart_mul[:, :, 0:1], 0.0)
            pool.memset(restart_add[:, :, 0:1], NEG).then_inc(consts, 1)
            pool.affine_select(out=head_col[:, :], in_=ones[:, 0:H1C], compare_op=ALU.is_ge, fill=0.0,
                               base=0, pattern=[[-HD1, H1C]], channel_multiplier=1).then_inc(pool_step, 1)
            pool.wait_ge(pool_step, 7)
            pool.affine_select(out=head_col[:, :], in_=head_col[:, :], compare_op=ALU.is_ge, fill=0.0,
                               base=HD1 - 1, pattern=[[HD1, H1C]], channel_multiplier=-1)
            pool.tensor_copy(ident_h[:, :], ident[:, :])
            pool.tensor_tensor(expert_sel[:, :], ident[:, 0:E], ident[:, E:2 * E], ALU.add).then_inc(consts, 1)
            pool.wait_ge(ld_attn, 80)
            for dst, src in ((bd_t, blk_t), (bd, blk)):
                pool.tensor_tensor(dst.rearrange("p n (a b) -> p n a b", b=4),
                                   src[:, :, :].unsqueeze(2).broadcast_to([128, 12, 32, 4]),
                                   in_block[:, :].unsqueeze(1).unsqueeze(3).broadcast_to([128, 12, 32, 4]),
                                   ALU.mult).then_inc(bd_done, 1)

            for i, (raw, ints) in enumerate(((wraw1, w1q), (wraw2, w2q))):
                pool.wait_ge(wscaled, i + 1)
                pool.tensor_scalar(raw[:, :, :], raw[:, :, :], MAGIC, 1.0, ALU.subtract, ALU.min).then_inc(pool_step, 1)
                pool.wait_ge(pool_step, 8 + i)
                pool.tensor_scalar(ints[:, :, :], raw[:, :, :], -1.0, None, ALU.max).then_inc(wq_done, 1)

            def split_low(w, slot, n):
                pool.wait_ge(whi_done, n + 1)
                pool.tensor_tensor(wlo[:, slot, :], w, whi[:, slot, :], ALU.subtract).then_inc(wlo_done, 1)

            split_low(shared_w[:, :], 3, 0)
            for e in range(3):
                split_low(stage[:, e, :], e, e + 1)
            with pool.Fori(0, LOOPS) as it:
                for j in range(4):
                    s = (j + 3) % 4
                    split_low(stage[:, s, :], s, it * 4 + (j + 4))
            split_low(stage[:, 3, :], 3, E)

        @block.tensor
        def _(pe):
            pe.wait_ge(consts, 3)

            def layer_norm(n):
                for hf in range(2):
                    pe.wait_ge(h_ready, 4 * n + 2 * hf + 2)
                    for c in range(DC):
                        mm = pe.matmul(bank[4 + hf][:, 0:HT], mean_w[:, :], half(h, c, hf), start=c == 0, stop=c == DC - 1)
                    mm.then_inc(ln_mean, 1)
                for hf in range(2):
                    pe.wait_ge(ln_sq, 2 * n + hf + 1)
                    for c in range(DC):
                        mm = pe.matmul(bank[6 + hf][:, 0:HT], mean_w[:, :], half(sq, c, hf), start=c == 0, stop=c == DC - 1)
                    mm.then_inc(ln_var, 1)

            pe.wait_ge(ld_first, 64)
            for hf in range(2):
                for m in range(DC):
                    for k in range(TOK_K):
                        mm = pe.matmul(bank[2 * hf + m][:, 0:HB * PATCHES], tokw[:, k, m * 128:(m + 1) * 128],
                                       patch_sb[:, k, hf * HB * PATCHES:(hf + 1) * HB * PATCHES],
                                       start=k == 0, stop=k == TOK_K - 1)
                    mm.then_inc(tok_mm, 1)
            layer_norm(0)

            pe.wait_ge(ld_attn, 80)
            for n in range(16):
                hf, m = n // 8, (n % 8) // 2 + 4 * (n % 2)
                if n % 8 == 0:
                    pe.wait_ge(xn_ready, hf + 1)
                if n >= 4:
                    pe.wait_ge((xm_done, zs_done)[n % 2], n // 2 - 1)
                for k in range(DC):
                    mm = pe.matmul(bank[n % 4][:, 0:HT], wup[:, k, m * 128:(m + 1) * 128], half(xn, k, hf),
                                   start=k == 0, stop=k == DC - 1)
                mm.then_inc(up_mm, 1)

            pe.wait_ge(bd_done, 1)
            for c in range(INNER_C):
                pe.matmul(bank[4][:, c * 64:(c + 1) * 64], bd_t[:, c, :], wg[:, c, :], start=True, stop=False)
                pe.matmul(bank[4][:, c * 64:(c + 1) * 64], bd_t[:, 4 + c, :], wg[:, 4 + c, :], start=False, stop=True)
            for c in range(INNER_C):
                mm = pe.matmul(bank[4][:, (4 + c) * 64:(5 + c) * 64], bd_t[:, 8 + c, :], wg[:, 8 + c, :],
                               start=True, stop=True)
            mm.then_inc(geff_mm, 1)

            pe.wait_ge(bd_done, 2)
            pe.wait_ge(xm_done, 8)
            pe.wait_ge(zs_done, 8)
            for n in range(8):
                g = n
                b2 = 5 + n % 2
                if n >= 2:
                    pe.wait_ge(v_done, n - 1)
                for c in range(INNER_C):
                    mm = pe.matmul(bank[b2][0:GT, c * DH:(c + 1) * DH], xm[:, c, g * GT:(g + 1) * GT],
                                   bd[:, 8 + c, :], start=True, stop=True)
                mm.then_inc(v_mm, 1)
            for n in range(16):
                c, hf, kind = n // 4, (n // 2) % 2, n % 2
                pe.wait_ge(xc_ready, c + 1)
                if n >= 4:
                    pe.wait_ge((q_done, k_done)[kind], n // 2 - 1)
                pe.matmul(bank[n % 4][:, 0:HT], bd[:, 4 * kind + c, :], half(xc, c, hf),
                          start=True, stop=True).then_inc(qk_mm, 1)
            pe.wait_ge(geff_done, 1)
            pe.wait_ge(v_done, 8)
            for hf in range(2):
                for c in range(INNER_C):
                    pe.matmul(bank[4 + hf][0:64, 0:HT], geff[:, c, :], half(xc, c, hf), start=c == 0, stop=False)
                for c in range(INNER_C):
                    mm = pe.matmul(bank[4 + hf][0:64, 0:HT], geff[:, 4 + c, :],
                                   half(xm, c, hf), start=False, stop=c == INNER_C - 1)
                mm.then_inc(gates_mm, 1)

            def scores(g):
                if g == 0:
                    pe.wait_ge(q_done, 8)
                    pe.wait_ge(k_done, 8)
                if g >= 2:
                    pe.wait_ge(c_done, g - 1)
                tok = slice(g * GT, (g + 1) * GT)
                for c in range(INNER_C):
                    mm = pe.matmul(bank[g % 2][0:GT, c * GT:(c + 1) * GT], kT[:, c, tok], qT[:, c, tok],
                                   start=True, stop=True)
                mm.then_inc(s_mm, 1)
                if g == 0:
                    pe.wait_ge(arow_done, 1)
                dst = bank[2 + g % 2]
                pe.matmul(dst[0:GT, 0:INNER_C * GT], arow[:, tok], head_row[:, :, :], start=True, stop=False)
                for c in range(INNER_C):
                    pe.matmul(dst[0:GT, c * GT:(c + 1) * GT], head_row[:, c, :], mrow[:, tok], start=False, stop=False)
                pe.matmul(dst[0:GT, 0:INNER_C * GT], ident[0:GT, 0:GT], causal[:, :, :],
                          start=False, stop=True).then_inc(e_mm, 1)

            pe.wait_ge(consts, 2)
            scores(0)
            for g in range(G):
                if g + 1 < G:
                    scores(g + 1)
                if g == 0:
                    pe.wait_ge(nrow_done, 1)
                    for gg in range(G):
                        mm = pe.matmul(bank[7][0:GT, gg * INNER_C:(gg + 1) * INNER_C], nrow[:, gg * GT:(gg + 1) * GT],
                                       ident[0:INNER_C, 0:INNER_C], start=True, stop=True)
                    mm.then_inc(floor_mm, 1)
                    pe.wait_ge(gts_done, 2)
                pe.wait_ge(c_done, g + 1)
                if g >= 2:
                    pe.wait_ge(hstat_done, g - 1)
                    pe.wait_ge(hraw_done, g - 1)
                for c in range(INNER_C):
                    pe.matmul(bank[6][0:GT, g * INNER_C + c:g * INNER_C + c + 1], cmat[:, g % 2, c, :], ones[0:GT, 0:1],
                              start=True, stop=True)
                    mm = pe.matmul(bank[4 + g % 2][0:GT, c * DH:(c + 1) * DH], cmat[:, g % 2, c, :],
                                   v[0:GT, g, c * DH:(c + 1) * DH], start=True, stop=True)
                mm.then_inc(hv_mm, 1)
            pe.wait_ge(wabs_done, 2)
            pe.matmul(bank[3][:, 0:2], ones[:, :], wabs[:, :], start=True, stop=True).then_inc(wmean_mm, 1)
            for g in range(G):
                pe.wait_ge(hn_done, g + 1)
                if g >= 2:
                    pe.wait_ge(hst_done, g - 1)
                for c in range(INNER_C):
                    mm = pe.transpose(bank[g % 2][:, c * GT:(c + 1) * GT], hraw[0:GT, g, c * DH:(c + 1) * DH],
                                      ident[0:GT, 0:GT])
                mm.then_inc(ht_mm, 1)
            for hf in range(2):
                if hf == 0:
                    pe.wait_ge(hst_done, G)
                for m in range(DC):
                    for k in range(INNER_C):
                        mm = pe.matmul(bank[2 * hf + m][:, 0:HT], wdn[:, k, m * 128:(m + 1) * 128], half(hst, k, hf),
                                       start=k == 0, stop=k == INNER_C - 1)
                    mm.then_inc(down0_mm, 1)

            layer_norm(1)

            pe.wait_ge(ld_ffn, 32)
            pe.wait_ge(xn_ready, 4)
            for g in range(G):
                for k in range(DC):
                    mm = pe.matmul(bank[7][0:GT, g * E:(g + 1) * E], xn[:, k, g * GT:(g + 1) * GT], wrt[:, k, :],
                                   start=k == 0, stop=k == DC - 1)
            mm.then_inc(route_mm, 1)

            def into_hidden(dst, slot, at, hf, done):
                n = 0
                for k in range(DC):
                    w_at = slice(at + k * 128, at + (k + 1) * 128)
                    for w, x in ((whi, xhi), (whi, xlo), (wlo, xhi)):
                        mm = pe.matmul(dst[:, 0:HT], w[:, slot, w_at], half(x, k, hf), start=n == 0, stop=n == 5)
                        n += 1
                mm.then_inc(done, 1)

            def down(slot, hf, n, last=False):
                pe.wait_ge(alo_done, n + 1)
                s = hf
                for m in range(DC):
                    w_at = slice(512 + m * 128, 512 + (m + 1) * 128)
                    for i, (w, x) in enumerate(((whi, ahi), (whi, alo), (wlo, ahi))):
                        mm = pe.matmul(bank[2 * hf + m][:, 0:HT], w[:, slot, w_at], x[:, s, :],
                                       start=False, stop=last and i == 2, skip_group_check=True)
                mm.then_inc(down_mm, 1)

            pe.wait_ge(wlo_done, 1)
            pe.wait_ge(xlo_done, 2)
            for i in range(4):
                pe.matmul(bank[i][:, 0:HT], zero_w[:, :], half(xhi, 0, 0), start=True, stop=False, skip_group_check=True)
            into_hidden(bank[4], 3, 0, 0, gate_mm)
            into_hidden(bank[5], 3, 256, 0, uproj_mm)
            pe.wait_ge(aff_done, 1)
            into_hidden(bank[6], 3, 0, 1, gate_mm)
            into_hidden(bank[7], 3, 256, 1, uproj_mm)
            down(3, 0, 0)
            pe.wait_ge(mask_done, 1)
            pe.wait_ge(act_done, 1)
            for g in range(G):
                mm = pe.transpose(bank[4][:, g * 64:g * 64 + 64].bitcast(F16)[:, 0:GT], mask_hl[:, g, :], ident_h[0:GT, 0:GT])
            mm.then_inc(maskt_mm, 1)
            pe.wait_ge(maskt_done, 1)

            def four_experts(it, last=False):
                r = 0
                for j in range(4):
                    for hf in range(2):
                        n = it * 8 + (2 * j + hf + 2)
                        if hf == 0:
                            pe.wait_ge(wlo_done, it * 4 + (j + 2))
                        for kind in range(3):
                            old = r - 4
                            steps = n - (2 * j + hf) + old // 3
                            pe.wait_ge((silu_done, gu_done, act_done)[old % 3], steps + 1)
                            b = bank[4 + r % 4]
                            if kind == 0:
                                into_hidden(b, j, 0, hf, gate_mm)
                            elif kind == 1:
                                into_hidden(b, j, 256, hf, uproj_mm)
                            else:
                                e = it * 4 + j
                                pe.matmul(b[:, 0:HT], expert_sel[:, bass.ds(e, 1)].broadcast_to([128, 128]),
                                          maskT[:, hf * HT:(hf + 1) * HT], start=True, stop=True).then_inc(mask_mm, 1)
                            r += 1
                        down((j - 1 + hf) % 4, 1 - hf, n - 1, last=last and j == 3 and hf == 1)

            with pe.Fori(0, LOOPS) as it:
                four_experts(it)
            four_experts(LOOPS, last=True)
            down(3, 1, 2 * E + 1, last=True)

            layer_norm(2)

            pe.wait_ge(ld_bit, 64)
            n = 0
            for hf in range(2):
                pe.wait_ge(xn_ready, 4 + hf + 1)
                for qk in range(2):
                    for m in range(DC):
                        if n >= 2:
                            pe.wait_ge(rope_t, n - 1)
                        for sw in range(2):
                            b = bank[2 * (n % 2) + sw]
                            for k in range(DC):
                                mm = pe.matmul(b[:, 0:HT], l1w[:, 2 * qk + sw, k, m * 128:(m + 1) * 128], half(xn, k, hf),
                                               start=k == 0, stop=k == DC - 1)
                        mm.then_inc(rope_mm, 1)
                        n += 1
            for n in range(G):
                if n >= 2:
                    pe.wait_ge(vb_done, n - 1)
                for i in range(2):
                    b = 2 * n + i
                    for k in range(DC):
                        mm = pe.matmul(bank[4 + n % 2][0:POS, i * D:(i + 1) * D], xn[:, k, b * POS:(b + 1) * POS],
                                       l1w[:, 4, k, :], start=k == 0, stop=k == DC - 1)
                mm.then_inc(vb_mm, 1)

            U = 3 * POS

            def att_scores(n):
                if n == 0:
                    pe.wait_ge(qm_done, 16)
                    pe.wait_ge(rope_done, 8)
                if n >= 2:
                    pe.wait_ge(sc_sub, n - 1)
                for i in range(2):
                    b = 2 * n + i
                    for c in range(DC):
                        for u in range(3):
                            o = (i * 6 + c * 3 + u) * POS
                            mm = pe.matmul(bank[n % 2][0:U, o:o + POS], qm[:, c, b, 3 * u:3 * u + 3, :],
                                           kr[:, c, b * POS:(b + 1) * POS], start=True, stop=True)
                mm.then_inc(sc_mm, 1)

            att_scores(0)
            pe.wait_ge(vb_done, 8)
            for n in range(G):
                if n + 1 < G:
                    att_scores(n + 1)
                pe.wait_ge(p_done, n + 1)
                for i in range(2):
                    b = 2 * n + i
                    if b >= 1:
                        pe.wait_ge(pt_done, 2 * b)
                    for c in range(DC):
                        for u in range(3):
                            mm = pe.transpose(bank[2 + c][0:POS, u * U:(u + 1) * U],
                                              pr[0:U, n % 2, i * 6 + c * 3 + u, :], ident[0:U, 0:U])
                        mm.then_inc(pt_mm, 1)
                    pe.wait_ge(pt_done, 2 * b + 2)
                    if b >= 2:
                        pe.wait_ge(ot_done, b - 1)
                    for hh in range(H1):
                        c, q = hh // H1C, hh % H1C
                        mm = pe.matmul(bank[4 + b % 2][0:POS, hh * HD1:(hh + 1) * HD1], pT[0:POS, b % 2, c, q * POS:(q + 1) * POS],
                                       vb[0:POS, b, hh * HD1:(hh + 1) * HD1], start=True, stop=True)
                    mm.then_inc(pv_mm, 1)
            for c in range(DC):
                for hf in range(2):
                    for b in range(HB):
                        if c == 0:
                            pe.wait_ge(ot_done, hf * HB + b + 1)
                        mm = pe.transpose(bank[2 * c + hf][:, b * POS:(b + 1) * POS],
                                          otok[0:POS, hf * HB + b, c * 128:(c + 1) * 128], ident[0:POS, 0:POS])
                    mm.then_inc(ott_mm, 1)
            for hf in range(2):
                pe.wait_ge(oT_done, 4)
                for m in range(DC):
                    for k in range(DC):
                        mm = pe.matmul(bank[4 + 2 * hf + m][:, 0:HT], l1w[:, 5, k, m * 128:(m + 1) * 128], half(oT, k, hf),
                                       start=k == 0, stop=k == DC - 1)
                    mm.then_inc(wo_mm, 1)

            layer_norm(3)

            def token_scales(n):
                pe.wait_ge(amax_done, n + 1)
                for g in range(G):
                    b = bank[(4, 5)[g // 4]]
                    mm = pe.transpose(b[0:GT, (g % 4) * 128:(g % 4 + 1) * 128], amax[:, g * GT:(g + 1) * GT], ident[:, :])
                mm.then_inc(amaxt_mm, 1)
                pe.wait_ge(tsc_done, n + 1)
                pe.transpose(bank[6][0:2 * G, 0:GT], tsc[:, :, :].rearrange("p a g -> p (a g)"),
                             ident[0:GT, 0:GT]).then_inc(tsct_mm, 1)
                pe.wait_ge(tsct_done, n + 1)
                for kind in range(2):
                    for g in range(G):
                        b = bank[4 + 2 * kind + g // 4]
                        mm = pe.matmul(b[:, (g % 4) * GT:(g % 4 + 1) * GT], ident[0:2 * G, kind * G + g:kind * G + g + 1].broadcast_to([2 * G, 128]),
                                       tscT[:, :], start=True, stop=True)
                    mm.then_inc(bc_mm, 1)

            token_scales(0)
            pe.wait_ge(wq_done, 2)
            for n in range(16):
                hf, m = n // 8, n % 8
                pe.wait_ge(xq_done, 2 * hf + 2)
                if n >= 4:
                    pe.wait_ge(hid_done, n - 3)
                for k in range(DC):
                    mm = pe.matmul(bank[n % 4][:, 0:HT], w1q[:, k, m * 128:(m + 1) * 128], half(x4q, k, hf),
                                   start=k == 0, stop=k == DC - 1)
                mm.then_inc(w1_mm, 1)
            token_scales(1)
            for hf in range(2):
                for m in range(DC):
                    for k in range(FC):
                        if m == 0 and k % 4 == 0:
                            pe.wait_ge(xq_done, 4 + 2 * hf + k // 4 + 1)
                        mm = pe.matmul(bank[2 * hf + m][:, 0:HT], w2q[:, k, m * 128:(m + 1) * 128], half(h2q, k, hf),
                                       start=k == 0, stop=k == FC - 1)
                    mm.then_inc(w2_mm, 1)

        @block.scalar
        def _(a):
            def layer_norm(n):
                for hf in range(2):
                    a.wait_ge(ln_cent, 2 * n + hf + 1)
                    a.activation(sq[:, :, hf * HT:(hf + 1) * HT], xn[:, :, hf * HT:(hf + 1) * HT], ACT.Square).then_inc(ln_sq, 1)
                for hf in range(2):
                    a.wait_ge(ln_var, 2 * n + hf + 1)
                    a.activation(rstd[:, hf * HT:(hf + 1) * HT], bank[6 + hf][:, 0:HT], ACT.Sqrt,
                                 bias=eps_col[:, :]).then_inc(ln_std, 1)

            a.wait_ge(consts, 3)
            layer_norm(0)
            for n in range(8):
                a.wait_ge(up_mm, 2 * n + 2)
                hf, c = n // 4, n % 4
                a.activation(half(zs, c, hf), bank[(2 * n + 1) % 4][:, 0:HT], ACT.Silu).then_inc(zs_done, 1)
            for c in range(INNER_C):
                a.wait_ge(xm_done, 5 + c)
                a.activation(cacc[:, c, :], xm[:, c, :], ACT.Identity, bias=col("conv_b", c),
                             scale=col("conv_w", c * CONV + CONV - 1)).then_inc(conv_first, 1)
            for c in range(INNER_C):
                a.wait_ge(conv_done, c + 1)
                a.activation(xc[:, c, :], cacc[:, c, :], ACT.Silu).then_inc(xc_ready, 1)
            for g in range(G):
                a.wait_ge(v_mm, g + 1)
                if g == 0:
                    a.wait_ge(tok_mm, 4)
                a.activation(v[0:GT, g, :], bank[5 + g % 2][0:GT, :], ACT.Copy).then_inc(v_done, 1)
            for n in range(8):
                c, hf = n // 2, n % 2
                a.wait_ge(qk_mm, 2 * n + 1)
                a.activation(half(qT, c, hf), bank[(2 * n) % 4][:, 0:HT], ACT.Copy, scale=float(DH) ** -0.5).then_inc(q_done, 1)
            a.wait_ge(absf_done, 1)
            a.activation(lf[:, 1, :], lf[:, 0, :], ACT.Exp, scale=-1.0).then_inc(act_step, 1)
            a.wait_ge(act_step, 1)
            a.activation(lf[:, 1, :], lf[:, 1, :], ACT.Ln, bias=ones[0:INNER_C, 0:1]).then_inc(lnf_done, 1)
            a.wait_ge(nrow_in, 1)
            a.activation(nrow[:, :], nrow[:, :], ACT.Exp, scale=-1.0).then_inc(nrow_done, 1)

            def decay(g):
                a.wait_ge(e_mm, g + 1)
                if g >= 2:
                    a.wait_ge(c_done, g - 1)
                a.activation(dmat[:, g % 2, :, :], bank[2 + g % 2][0:GT, 0:INNER_C * GT], ACT.Exp).then_inc(d_done, 1)

            decay(0)
            for g in range(G):
                if g + 1 < G:
                    decay(g + 1)
                a.wait_ge(hstat_done, g + 1)
                a.activation(hraw[0:GT, g, :], bank[4 + g % 2][0:GT, :], ACT.Copy).then_inc(hraw_done, 1)
            for c in range(INNER_C):
                a.activation(xc[:, c, :], xc[:, c, :], ACT.Copy, scale=col("skip", c)).then_inc(skip_done, 1)
            a.wait_ge(ld_bit, 64)
            for i, (raw, free) in enumerate(((wraw1, kT), (wraw2, qT))):
                a.activation(free.rearrange("p c t -> p (c t)")[:, 0:2048], raw[:, :, :].rearrange("p a b -> p (a b)"), ACT.Abs,
                             accum_out=wabs[:, i:i + 1]).then_inc(wabs_done, 1)
            a.wait_ge(hvar_done, 1)
            a.activation(tiny[:, 3, :], tiny[:, 2, :], ACT.Sqrt, bias=eps_col[0:GT, :]).then_inc(hstd_done, 1)

            a.wait_ge(wmean_done, 1)
            for i, raw in enumerate((wraw1, wraw2)):
                a.activation(raw[:, :, :], raw[:, :, :], ACT.Identity, bias=magic_col[:, :],
                             scale=wscale[:, i:i + 1]).then_inc(wscaled, 1)
            layer_norm(1)
            a.wait_ge(ld_ffn, 32)
            a.activation(whi[:, 3, :], shared_w[:, :], ACT.Copy).then_inc(whi_done, 1)
            for hf in range(2):
                a.wait_ge(xn_ready, 2 + hf + 1)
                a.activation(xhi[:, :, hf * HT:(hf + 1) * HT], xn[:, :, hf * HT:(hf + 1) * HT], ACT.Copy).then_inc(xhi_done, 1)
            a.wait_ge(route_mm, 1)
            a.activation(aff[:, :, :].rearrange("p g e -> p (g e)"), bank[7][0:GT, :], ACT.Sigmoid).then_inc(aff_done, 1)

            def split_high(slot, reads):
                a.activation(whi[:, slot, :], stage[:, slot, :], ACT.Copy).then_inc(whi_done, 1)

            for e in range(3):
                if e % 2 == 0:
                    a.wait_ge(ld_stage[e // 2], 16)
                split_high(e, e)

            def silu(b, s, n):
                a.wait_ge(gate_mm, n + 1)
                a.activation(sg[:, s, :], b[:, 0:HT], ACT.Silu).then_inc(silu_done, 1)

            silu(bank[4], 0, 0)
            silu(bank[6], 1, 1)

            def four_experts(it, last=False):
                for j in range(4):
                    for hf in range(2):
                        n = it * 8 + (2 * j + hf + 2)
                        r = 3 * (2 * j + hf)
                        a.wait_ge(gu_done, n - 1)
                        silu(bank[4 + r % 4], hf, n)
                    if last and j > 0:
                        continue
                    s = (j + 3) % 4
                    if s == 0:
                        a.wait_ge(ld_stage[0], it * 16 + 32)
                    if s == 2:
                        a.wait_ge(ld_stage[1], it * 16 + 32)
                    a.wait_ge(down_mm, it * 8 + (2 * j + 2))
                    split_high(s, None)

            with a.Fori(0, LOOPS) as it:
                four_experts(it)
            four_experts(LOOPS, last=True)

            layer_norm(2)
            for n in range(G):
                a.wait_ge(vb_mm, n + 1)
                a.activation(vb[0:POS, 2 * n:2 * n + 2, :], bank[4 + n % 2][0:POS, :].rearrange("p (b m) -> p b m", b=2),
                             ACT.Copy).then_inc(vb_done, 1)
            U = 3 * POS

            def exps(n):
                a.wait_ge(sc_sub, n + 1)
                a.activation(pr[0:U, n % 2, :, :], pr[0:U, n % 2, :, :], ACT.Exp, scale=1.0 / 16.0).then_inc(sc_exp, 1)

            exps(0)
            for n in range(G):
                if n + 1 < G:
                    exps(n + 1)
                for i in range(2):
                    b = 2 * n + i
                    if b >= 2:
                        a.wait_ge(pv_mm, b - 1)
                    for c in range(DC):
                        a.wait_ge(pt_mm, 2 * b + c + 1)
                        a.activation(pT[0:POS, b % 2, c, :], bank[2 + c][0:POS, 0:3 * U], ACT.Copy).then_inc(pt_done, 1)
                    a.wait_ge(pv_mm, b + 1)
                    a.activation(otok[0:POS, b, :], bank[4 + b % 2][0:POS, 0:D], ACT.Copy).then_inc(ot_done, 1)
            for c in range(DC):
                for hf in range(2):
                    a.wait_ge(ott_mm, 2 * c + hf + 1)
                    a.activation(half(oT, c, hf), bank[2 * c + hf][:, 0:HT], ACT.Identity, bias=col("bv", c)).then_inc(oT_done, 1)

            layer_norm(3)
            for c in range(FC):
                a.wait_ge(hid_done, 9 + c)
                a.activation(h2[:, c, :], hid[:, c, :], ACT.Identity, bias=col("ffn_conv_b", c),
                             scale=col("ffn_conv_w", 3 * c + 1)).then_inc(fconv_first, 1)
            for c in range(FC):
                a.wait_ge(fconv_done, c + 1)
                a.activation(h2[:, c, :], h2[:, c, :], ACT.Silu).then_inc(h2_done, 1)
                a.wait_ge(h2_done, c + 1)
                a.activation(habs[:, c, :], h2[:, c, :], ACT.Abs).then_inc(habs_done, 1)

        @block.vector
        def _(d):
            steps = [0]

            def link(ins):
                steps[0] += 1
                ins.then_inc(vec_step, 1)
                d.wait_ge(vec_step, steps[0])

            def magnitude(out, x):
                return d.scalar_tensor_tensor(out=out, in0=x, scalar=-1.0, in1=x, op0=ALU.mult, op1=ALU.max)

            def layer_norm(n):
                for hf in range(2):
                    tok = slice(hf * HT, (hf + 1) * HT)
                    d.wait_ge(h_ready, 4 * n + 2 * hf + 2)
                    d.wait_ge(ln_mean, 2 * n + hf + 1)
                    d.tensor_tensor(xn[:, :, tok], h[:, :, tok],
                                    bank[4 + hf][:, 0:HT].unsqueeze(1).broadcast_to([128, DC, HT]), ALU.subtract).then_inc(ln_cent, 1)
                for hf in range(2):
                    tok = slice(hf * HT, (hf + 1) * HT)
                    d.wait_ge(ln_std, 2 * n + hf + 1)
                    link(d.reciprocal(rstd[:, tok], rstd[:, tok]))
                    d.tensor_tensor(xn[:, :, tok], xn[:, :, tok],
                                    rstd[:, tok].unsqueeze(1).broadcast_to([128, DC, HT]), ALU.mult).then_inc(xn_ready, 1)

            def add_to_h(banks, done, first):
                for hf in range(2):
                    for m in range(DC):
                        d.wait_ge(done, first + 2 * hf + m + 1)
                        d.tensor_tensor(half(h, m, hf), half(h, m, hf), banks[2 * hf + m][:, 0:HT], ALU.add).then_inc(h_ready, 1)

            d.wait_ge(consts, 3)
            d.wait_ge(ld_first, 64)
            for m in range(DC):
                d.tensor_scalar(posb[:, m, :], posw[:, m, :], col("tok_b", m), None, ALU.add)
                link(d.tensor_tensor(cls0[:, m:m + 1], col("cls", m), posw[:, m, 0:1], ALU.add))
                d.tensor_copy(images(h[:, m, :])[:, :, 0:1], cls0[:, m:m + 1].unsqueeze(1).broadcast_to([128, B, 1]))
            for hf in range(2):
                for m in range(DC):
                    d.wait_ge(tok_mm, 2 * hf + m + 1)
                    d.tensor_tensor(images(half(h, m, hf))[:, :, 1:POS],
                                    bank[2 * hf + m][:, 0:HB * PATCHES].rearrange("p (b t) -> p b t", t=PATCHES),
                                    posb[:, m, 1:POS].unsqueeze(1).broadcast_to([128, HB, PATCHES]), ALU.add).then_inc(h_ready, 1)
            layer_norm(0)

            for n in range(8):
                hf, c = n // 4, n % 4
                d.wait_ge(up_mm, 2 * n + 1)
                d.tensor_copy(half(xm, c, hf), bank[(2 * n) % 4][:, 0:HT]).then_inc(xm_done, 1)
            d.wait_ge(geff_mm, 1)
            d.tensor_copy(geff[:, :, :].rearrange("p a b -> p (a b)"), bank[4][:, :]).then_inc(geff_done, 1)
            for c in range(INNER_C):
                d.wait_ge(conv_first, c + 1)
                for back in range(1, CONV):
                    into = images(cacc[:, c, :])[:, :, back:POS]
                    ins = d.scalar_tensor_tensor(out=into, in0=images(xm[:, c, :])[:, :, 0:POS - back],
                                                 scalar=col("conv_w", c * CONV + CONV - 1 - back), in1=into,
                                                 op0=ALU.mult, op1=ALU.add)
                    if back < CONV - 1:
                        link(ins)
                ins.then_inc(conv_done, 1)
            for n in range(8):
                c, hf = n // 2, n % 2
                d.wait_ge(qk_mm, 2 * n + 2)
                if n == 0:
                    d.wait_ge(xc_ready, 4)
                d.tensor_copy(half(kT, c, hf), bank[(2 * n + 1) % 4][:, 0:HT]).then_inc(k_done, 1)

            for hf in range(2):
                d.wait_ge(gates_mm, hf + 1)
                d.tensor_scalar(gts[:, hf * HT:(hf + 1) * HT], bank[4 + hf][0:64, 0:HT], col("gate_b", 0, slice(0, 64)),
                                None, ALU.add).then_inc(gts_done, 1)
            d.wait_ge(gts_done, 2)
            d.tensor_scalar(lf[:, 2, :], gts[32:32 + INNER_C, :], 0.0, None, ALU.min)
            magnitude(lf[:, 0, :], gts[32:32 + INNER_C, :]).then_inc(absf_done, 1)
            d.wait_ge(lnf_done, 1)
            link(d.tensor_tensor(lf[:, 3, :], lf[:, 2, :], lf[:, 1, :], ALU.subtract))
            d.wait_ge(consts, 2)
            link(d.tensor_tensor_scan(lcum[:, :], restart_mul[:, :, :].rearrange("p b t -> p (b t)"), lf[:, 3, :], 0.0,
                                      ALU.mult, ALU.add))
            link(d.tensor_tensor(arow[:, :], gts[0:INNER_C, :], lcum[:, :], ALU.subtract))
            link(d.tensor_tensor_scan(mrow[:, :], restart_add[:, :, :].rearrange("p b t -> p (b t)"), arow[:, :], NEG,
                                      ALU.add, ALU.max))
            d.tensor_tensor(nrow[:, :], mrow[:, :], lcum[:, :], ALU.add).then_inc(nrow_in, 1)
            d.tensor_scalar(mrow[:, :], mrow[:, :], -1.0, None, ALU.mult).then_inc(arow_done, 1)

            def weights(g):
                d.wait_ge(d_done, g + 1)
                d.wait_ge(s_mm, g + 1)
                if g >= 2:
                    d.wait_ge(hv_mm, g - 1)
                d.tensor_tensor(cmat[:, g % 2, :, :], bank[g % 2][0:GT, 0:INNER_C * GT].rearrange("p (c s) -> p c s", c=INNER_C),
                                dmat[:, g % 2, :, :], ALU.mult).then_inc(c_done, 1)

            weights(0)
            for g in range(G):
                if g + 1 < G:
                    weights(g + 1)
                d.wait_ge(hv_mm, g + 1)
                for c in range(INNER_C):
                    ins = d.bn_stats(stat[:, g * INNER_C + c, :], bank[4 + g % 2][0:GT, c * DH:(c + 1) * DH])
                ins.then_inc(hstat_done, 1)
            d.wait_ge(hstat_done, G)
            for n in range(G * INNER_C):
                ins = d.bn_aggr(mv[:, n, :], stat[:, n, :])
            d.wait_ge(floor_mm, 1)
            d.tensor_copy(floor_t[:, :], bank[7][0:GT, 0:G * INNER_C])
            link(d.tensor_copy(csum[:, :], bank[6][0:GT, 0:G * INNER_C]))
            link(magnitude(csum[:, :], csum[:, :]))
            link(d.tensor_tensor(csum[:, :], csum[:, :], floor_t[:, :], ALU.max))
            link(d.tensor_scalar(csum[:, :], csum[:, :], 1e-6, None, ALU.add))
            link(d.reciprocal(tiny[:, 0, :], csum[:, :]))
            link(d.tensor_tensor(tiny[:, 1, :], tiny[:, 0, :], tiny[:, 0, :], ALU.mult))
            d.tensor_tensor(tiny[:, 2, :], tiny[:, 1, :], mv[:, :, 1], ALU.mult).then_inc(hvar_done, 1)
            d.wait_ge(hstd_done, 1)
            link(d.reciprocal(tiny[:, 4, :], tiny[:, 3, :]))
            link(d.tensor_tensor(tiny[:, 5, :], tiny[:, 4, :], tiny[:, 0, :], ALU.mult))
            d.wait_ge(hraw_done, G)
            for g in range(G):
                for c in range(INNER_C):
                    n = g * INNER_C + c
                    ins = d.tensor_scalar(hraw[0:GT, g, c * DH:(c + 1) * DH], hraw[0:GT, g, c * DH:(c + 1) * DH],
                                          mv[:, n, 0:1], tiny[:, 5, n:n + 1], ALU.subtract, ALU.mult)
                ins.then_inc(hn_done, 1)
            d.wait_ge(wmean_mm, 1)
            link(d.tensor_scalar(wmean[:, :], bank[3][:, 0:2], 1.0 / (D * 1024), 1e-5, ALU.mult, ALU.max))
            d.reciprocal(wscale[:, :], wmean[:, :]).then_inc(wmean_done, 1)
            d.wait_ge(skip_done, INNER_C)
            for g in range(G):
                d.wait_ge(ht_mm, g + 1)
                tok = slice(g * GT, (g + 1) * GT)
                for c in range(INNER_C):
                    ins = d.scalar_tensor_tensor(out=hst[:, c, tok], in0=bank[g % 2][:, c * GT:(c + 1) * GT],
                                                 scalar=col("ln_w", c), in1=xc[:, c, tok], op0=ALU.mult, op1=ALU.add)
                link(ins)
                d.tensor_tensor(hst[:, :, tok], hst[:, :, tok], zs[:, :, tok], ALU.mult).then_inc(hst_done, 1)
            add_to_h(bank[0:4], down0_mm, 0)
            layer_norm(1)

            for hf in range(2):
                tok = slice(hf * HT, (hf + 1) * HT)
                d.wait_ge(xhi_done, hf + 1)
                d.tensor_tensor(xlo[:, :, tok], xn[:, :, tok], xhi[:, :, tok], ALU.subtract).then_inc(xlo_done, 1)
            d.wait_ge(aff_done, 1)
            for g in range(G):
                ins = d.max(top[:, g, :], aff[:, g, :])
            link(ins)
            for g in range(G):
                d.match_replace(rest[:, g, :], top[:, g, :], aff[:, g, :], 0.0)
            link(d.tensor_reduce(den[:, 0, :], top[:, :, :], AX, ALU.add))
            link(d.tensor_scalar(den[:, 1, :], den[:, 0, :], 1e-9, None, ALU.add))
            link(d.reciprocal(den[:, 2, :], den[:, 1, :]))
            link(d.tensor_tensor(rest[:, :, :], aff[:, :, :], rest[:, :, :], ALU.subtract))
            link(d.tensor_tensor(rest[:, :, :], rest[:, :, :], den[:, 2, :].unsqueeze(2).broadcast_to([GT, G, E]), ALU.mult))
            link(d.tensor_copy(mask_hl[:, :, 0:E], rest[:, :, :]))
            d.tensor_tensor(mask_hl[:, :, E:2 * E], rest[:, :, :], mask_hl[:, :, 0:E], ALU.subtract).then_inc(mask_done, 1)

            def hidden(up_bank, mask_bank, s, n):
                d.wait_ge(silu_done, n + 1)
                d.wait_ge(uproj_mm, n + 1)
                d.tensor_tensor(gu[:, s, :], sg[:, s, :], up_bank[:, 0:HT], ALU.mult).then_inc(gu_done, 1)
                d.wait_ge(gu_done, n + 1)
                if mask_bank is None:
                    d.tensor_copy(act[:, s, :], gu[:, s, :]).then_inc(act_done, 1)
                else:
                    d.wait_ge(mask_mm, n - 1)
                    d.tensor_tensor(act[:, s, :], gu[:, s, :], mask_bank[:, 0:HT], ALU.mult).then_inc(act_done, 1)
                    d.wait_ge(down_mm, n - 1)
                d.wait_ge(act_done, n + 1)
                d.tensor_copy(ahi[:, s, :], act[:, s, :]).then_inc(ahi_done, 1)
                d.wait_ge(ahi_done, n + 1)
                d.tensor_tensor(alo[:, s, :], act[:, s, :], ahi[:, s, :], ALU.subtract).then_inc(alo_done, 1)

            hidden(bank[5], None, 0, 0)
            hidden(bank[7], None, 1, 1)
            d.wait_ge(maskt_mm, 1)
            d.tensor_copy(maskT[:, :].rearrange("p (g t) -> p g t", g=G),
                          bank[4][:, :].bitcast(F16).rearrange("p (g t) -> p g t", g=G)[:, :, 0:GT]).then_inc(maskt_done, 1)

            def four_experts(it):
                for j in range(4):
                    for hf in range(2):
                        r = 3 * (2 * j + hf)
                        hidden(bank[4 + (r + 1) % 4], bank[4 + (r + 2) % 4], hf, it * 8 + (2 * j + hf + 2))

            with d.Fori(0, LOOPS) as it:
                four_experts(it)
            four_experts(LOOPS)
            for hf in range(2):
                d.wait_ge(down_mm, 2 * E + 1 + hf)
                for m in range(DC):
                    d.tensor_tensor(half(h, m, hf), half(h, m, hf), bank[2 * hf + m][:, 0:HT], ALU.add).then_inc(h_ready, 1)
            layer_norm(2)

            n = 0
            for hf in range(2):
                for qk in range(2):
                    for m in range(DC):
                        d.wait_ge(rope_mm, n + 1)
                        if n >= 2:
                            d.wait_ge(rope_done, n - 1)
                        for sw in range(2):
                            if n + sw == 0:
                                d.wait_ge(ld_bit, 64)
                            ins = d.scalar_tensor_tensor(
                                out=images(rt[:, n % 2, sw, :]), in0=images(bank[2 * (n % 2) + sw][:, 0:HT]),
                                scalar=col(("bq", "bq_swap", "bk", "bk_swap")[2 * qk + sw], m),
                                in1=ropew[:, sw, :].unsqueeze(1).broadcast_to([128, HB, POS]), op0=ALU.add, op1=ALU.mult)
                        ins.then_inc(rope_t, 1)
                        d.wait_ge(rope_t, n + 1)
                        d.tensor_tensor(half((qr, kr)[qk], m, hf), rt[:, n % 2, 0, :], rt[:, n % 2, 1, :], ALU.add).then_inc(rope_done, 1)
                        n += 1
            d.wait_ge(rope_done, 8)
            d.memset(qm[:, :, :, H1C, :], 0.0)
            for c in range(DC):
                for hh in range(H1C):
                    d.tensor_scalar(qm[:, c, :, hh, :], images(qr[:, c, :]), head_col[:, hh:hh + 1], None, ALU.mult).then_inc(qm_done, 1)
            U = 3 * POS
            for n in range(G):
                def scores_of(n):
                    return bank[n % 2][0:U, 0:12 * POS].rearrange("p (n t) -> p n t", t=POS)

                def subtract_max(n):
                    d.wait_ge(sc_mm, n + 1)
                    if n >= 2:
                        d.wait_ge(pt_mm, 4 * (n - 1))
                    link(d.tensor_reduce(smx[0:U, n % 2, 0, :], scores_of(n), AX, ALU.max))
                    d.tensor_tensor(pr[0:U, n % 2, :, :], scores_of(n),
                                    smx[0:U, n % 2, 0, :].unsqueeze(2).broadcast_to([U, 12, POS]), ALU.subtract).then_inc(sc_sub, 1)

                if n == 0:
                    subtract_max(0)
                if n + 1 < G:
                    subtract_max(n + 1)
                d.wait_ge(sc_exp, n + 1)
                link(d.tensor_reduce(smx[0:U, n % 2, 1, :], pr[0:U, n % 2, :, :], AX, ALU.add))
                link(d.reciprocal(smx[0:U, n % 2, 2, :], smx[0:U, n % 2, 1, :]))
                d.tensor_tensor(pr[0:U, n % 2, :, :], pr[0:U, n % 2, :, :],
                                smx[0:U, n % 2, 2, :].unsqueeze(2).broadcast_to([U, 12, POS]), ALU.mult).then_inc(p_done, 1)
            add_to_h(bank[4:8], wo_mm, 0)
            layer_norm(3)

            def token_scales(n):
                for i in range(2):
                    if i == 0:
                        d.wait_ge(amaxt_mm, n + 1)
                    ins = d.tensor_reduce(tmx[:, 4 * i:4 * i + 4], bank[4 + i][0:GT, :].rearrange("p (g f) -> p g f", g=4), AX, ALU.max)
                link(ins)
                link(d.tensor_scalar(tmx[:, :], tmx[:, :], 1e-5, None, ALU.max))
                link(d.reciprocal(tsc[:, 0, :], tmx[:, :]))
                d.tensor_scalar(tsc[:, 1, :], tmx[:, :], 1.0 / 127.0, None, ALU.mult)
                d.tensor_scalar(tsc[:, 0, :], tsc[:, 0, :], 127.0, None, ALU.mult).then_inc(tsc_done, 1)
                d.wait_ge(tsct_mm, n + 1)
                d.tensor_copy(tscT[:, :], bank[6][0:2 * G, 0:GT]).then_inc(tsct_done, 1)

            def inverse_scales(n):
                d.wait_ge(bc_mm, 2 * n + 2)
                for i in range(2):
                    ins = d.tensor_scalar(binv[:, i * HT:(i + 1) * HT], bank[6 + i][:, 0:HT], wmean[:, n:n + 1], None, ALU.mult)
                ins.then_inc(bc_done, 1)

            def quantize(dst, src, hf, done, by):
                n = src.shape[1]
                link(d.tensor_tensor(src, src, bank[4 + hf][:, 0:HT].unsqueeze(1).broadcast_to([128, n, HT]), ALU.mult))
                link(d.tensor_scalar(src, src, 127.0, -128.0, ALU.min, ALU.max))
                d.tensor_scalar(dst, src, MAGIC, MAGIC, ALU.add, ALU.subtract).then_inc(done, by)

            d.wait_ge(xn_ready, 8)
            magnitude(habs[:, 0, :], xn[:, 0, :])
            link(magnitude(habs[:, 1, :], xn[:, 1, :]))
            d.tensor_tensor(amax, habs[:, 0, :], habs[:, 1, :], ALU.max).then_inc(amax_done, 1)
            token_scales(0)
            d.wait_ge(bc_mm, 1)
            for hf in range(2):
                tok = slice(hf * HT, (hf + 1) * HT)
                quantize(x4q[:, :, tok], xn[:, :, tok], hf, xq_done, 2)
            inverse_scales(0)
            d.wait_ge(bc_done, 1)
            for n in range(16):
                hf, c = n // 8, n % 8
                d.wait_ge(w1_mm, n + 1)
                d.tensor_tensor(half(hid, c, hf), bank[n % 4][:, 0:HT], binv[:, hf * HT:(hf + 1) * HT], ALU.mult).then_inc(hid_done, 1)
            for c in range(FC):
                d.wait_ge(fconv_first, c + 1)
                for k in (0, 2):
                    to, of = (slice(1, POS), slice(0, POS - 1)) if k == 0 else (slice(0, POS - 1), slice(1, POS))
                    into = images(h2[:, c, :])[:, :, to]
                    ins = d.scalar_tensor_tensor(out=into, in0=images(hid[:, c, :])[:, :, of],
                                                 scalar=col("ffn_conv_w", 3 * c + k), in1=into,
                                                 op0=ALU.mult, op1=ALU.add)
                    if k == 0:
                        link(ins)
                ins.then_inc(fconv_done, 1)
            d.wait_ge(habs_done, 2)
            link(d.tensor_tensor(amax, habs[:, 0, :], habs[:, 1, :], ALU.max))
            for c in range(2, FC):
                d.wait_ge(habs_done, c + 1)
                ins = d.tensor_tensor(amax, amax, habs[:, c, :], ALU.max)
                if c < FC - 1:
                    link(ins)
            ins.then_inc(amax_done, 1)
            token_scales(1)
            d.wait_ge(bc_mm, 3)
            for hf in range(2):
                tok = slice(hf * HT, (hf + 1) * HT)
                for c in (0, 4):
                    quantize(h2q[:, c:c + 4, tok], h2[:, c:c + 4, tok], hf, xq_done, 1)
            inverse_scales(1)
            d.wait_ge(bc_done, 2)
            for hf in range(2):
                for m in range(DC):
                    tok = slice(hf * HT, (hf + 1) * HT)
                    d.wait_ge(w2_mm, 2 * hf + m + 1)
                    link(d.tensor_tensor(half(sq, m, hf), bank[2 * hf + m][:, 0:HT], binv[:, tok], ALU.mult))
                    d.tensor_tensor(half(h, m, hf), half(h, m, hf), half(sq, m, hf), ALU.add).then_inc(h_ready, 1)


def _kmajor(w):
    k, m = w.shape
    return w.reshape(k // 128, 128, m).transpose(1, 0, 2)


def _columns(v):
    return v.reshape(-1, 128).T


def _rope_tables():
    import numpy as np
    freqs = np.float32(10000.0) ** (-np.arange(0, HD1, 2).astype(np.float32) / np.float32(HD1))
    ang = np.arange(POS, dtype=np.float32)[None, :] * freqs[:, None].astype(np.float32)
    f = (np.arange(128) % HD1) // 2
    sign = np.where(np.arange(128) % 2 == 0, -1.0, 1.0).astype(np.float32)[:, None]
    return np.stack([np.cos(ang)[f], np.sin(ang)[f] * sign], axis=1).astype(np.float32)


def _layouts(i):
    import numpy as np
    x = i["x"].reshape(B, 3, 6, 16, 6, 16).transpose(1, 3, 5, 0, 2, 4).reshape(TOK_K * 128, B * PATCHES)
    swap = np.arange(D) ^ 1
    gate_b = np.zeros((128, 1), np.float32)
    gate_b[0:4, 0], gate_b[32:36, 0] = i["L0_attn_b_ig"], i["L0_attn_b_fg"]
    w_gates = np.zeros((1536, 64), np.float32)
    w_gates[:, 0:4], w_gates[:, 32:36] = i["L0_attn_w_ig"].T, i["L0_attn_w_fg"].T
    cw = i["L0_attn_conv_w"].reshape(INNER_C, 128, CONV).transpose(1, 0, 2).reshape(128, -1)
    fw = i["L1_ffn_conv_w"].reshape(FC, 128, 3).transpose(1, 0, 2).reshape(128, -1)
    cols = np.concatenate([
        _columns(i["L0_tok_b"]), _columns(i["L0_tok_cls_token"].reshape(-1)), cw, _columns(i["L0_attn_conv_b"]),
        _columns(i["L0_attn_ln_w"].reshape(-1)), _columns(i["L0_attn_skip"]), gate_b,
        _columns(i["L1_attn_bq"]), _columns(i["L1_attn_bq"][swap]), _columns(i["L1_attn_bk"]),
        _columns(i["L1_attn_bk"][swap]), _columns(i["L1_attn_bv"]), fw, _columns(i["L1_ffn_conv_b"])], axis=1)
    heads = [i[f"L0_attn_w_{n}"] for n in "qkv"]
    blocks = np.concatenate([_kmajor(w.transpose(0, 2, 1).reshape(512, 4)) for w in heads], axis=1)
    blocks_t = np.concatenate([_kmajor(w.reshape(512, 4)) for w in heads], axis=1)

    def expert(gate, up, down):
        n = gate.shape[0]
        rows = [w.reshape(n, 2, 128, 128).transpose(0, 2, 1, 3).reshape(n, 128, 256) for w in (gate, up)]
        return np.concatenate([*rows, down], axis=2)

    shared = expert(*(i[f"L0_ffn_shared_{n}_w"][None] for n in ("gate", "up", "down")))[0]
    experts = expert(*(i[f"L0_ffn_expert_{n}_k"] for n in ("gate", "up", "down"))).transpose(1, 0, 2)
    wq, wk = i["L1_attn_Wq"], i["L1_attn_Wk"]
    l1_w = np.stack([_kmajor(w.T) for w in (wq, wq[swap], wk, wk[swap], i["L1_attn_Wv"], i["L1_attn_Wo"])], axis=1)
    return {
        "patches": _kmajor(x), "tok_w": _kmajor(i["L0_tok_W"].T), "pos": _kmajor(i["L0_tok_pos_enc"][0].T),
        "cols": cols, "w_up": _kmajor(i["L0_attn_w_up"].T), "blocks": blocks, "blocks_t": blocks_t,
        "w_gates": _kmajor(w_gates), "w_down": _kmajor(i["L0_attn_w_down"].T),
        "w_router": _kmajor(i["L0_ffn_router_w"]), "w_shared": shared, "w_experts": experts, "l1_w": l1_w,
        "rope": _rope_tables(), "ffn_w1": _kmajor(i["L1_ffn_w1"].T), "ffn_w2": _kmajor(i["L1_ffn_w2"].T),
    }


def kernel(**inputs):
    import numpy as np
    import concourse.bacc as bacc
    from concourse.bass_utils import run_bass_kernel_spmd

    nc = bacc.Bacc("TRN2", target_bir_lowering=False, num_devices=1)
    arrays = {k: np.ascontiguousarray(v) for k, v in _layouts({k: np.asarray(v) for k, v in inputs.items()}).items()}
    args = {k: nc.dram_tensor(k, v.shape, mybir.dt.from_np(v.dtype), kind="ExternalInput").ap() for k, v in arrays.items()}
    out = nc.dram_tensor("out", (128, DC, T), F32, kind="ExternalOutput").ap()
    vit_tower(nc, out=out, **args)
    r = run_bass_kernel_spmd(nc, [arrays], core_ids=[0])
    return r.results[0]["out"].transpose(2, 1, 0).reshape(B, POS, D)
```

```python
from contextlib import ExitStack

import concourse.bass as bass
from concourse import mybir

F32 = mybir.dt.float32
F16 = mybir.dt.float16
BF16 = mybir.dt.bfloat16
ALU = mybir.AluOpType
ACT = mybir.ActivationFunctionType
AX = mybir.AxisListType.X

B, PATCHES, POS = 16, 36, 37
T = B * POS
HB = B // 2
HT = HB * POS
G, GT = B // 2, 2 * POS
D, DC = 256, 2
TOK_K = 6
INNER_C = 4
DH = 128
CONV = 4
E = 64
WE = 768
H1, HD1 = 16, 16
H1C = 8
SPILL = 64
PTW = 112
QH = 9
FC = 8
PARTS = ((0, 0), (0, 1), (1, 0))
MAGIC = 1.5 * 2.0 ** 23
NEG = -1.0e30
QK_SCALE = float(DH) ** -0.5

COLS = {}
_n = 0
for _name, _w in (("tok_b", DC), ("cls", DC), ("conv_w", INNER_C * CONV), ("conv_b", INNER_C),
                  ("ln_w", INNER_C), ("skip", INNER_C), ("gate_b", 1), ("bq", DC), ("bq_swap", DC),
                  ("bk", DC), ("bk_swap", DC), ("bv", DC), ("ffn_conv_w", FC * 3), ("ffn_conv_b", FC)):
    COLS[_name] = (_n, _n + _w)
    _n += _w
NCOLS = _n


def vit_tower(nc: bass.Bass, patches, tok_w, pos, cols, w_up, blocks, blocks_t, w_gates, w_down,
              w_router, w_shared, w_experts, l1_w, rope, ffn_w1, ffn_w2, out):
    with ExitStack() as ctx:
        def sb(name, shape, dt=F32):
            return ctx.enter_context(nc.sbuf_tensor(name, shape, dt))

        def sem(name):
            return ctx.enter_context(nc.semaphore(name))

        bank = [ctx.enter_context(nc.psum_tensor(f"bank{i}", [128, 512], F32)) for i in range(8)]

        colp = sb("colp", [128, NCOLS])
        posw = sb("posw", [128, DC, POS])
        blk = sb("blk", [128, 12, 4])
        blk_t = sb("blk_t", [128, 12, 4])
        wg = sb("wg", [128, 12, 64])
        wup = sb("wup", [128, DC, 1024])
        wdn = sb("wdn", [128, INNER_C, D])
        wrt = sb("wrt", [128, DC, E])
        l1w = sb("l1w", [128, 6, DC, D])
        ropew = sb("ropew", [128, 2, POS])
        ident = sb("ident", [128, 128])
        zero_w = sb("zero_w", [128, 128], F16)
        ident_h = sb("ident_h", [128, 128], F16)
        mean_w = sb("mean_w", [128, 128])
        ones = sb("ones", [128, 128])
        in_block = sb("in_block", [128, 32])
        head_col = sb("head_col", [128, H1C])
        expert_sel = sb("expert_sel", [128, E], F16)
        causal = sb("causal", [GT, INNER_C, GT], BF16)
        restart_mul = sb("restart_mul", [INNER_C, B, POS])
        restart_add = sb("restart_add", [INNER_C, B, POS])
        magic_col = sb("magic_col", [128, 1])
        eps_col = sb("eps_col", [128, 1])
        h = sb("h", [128, DC, T])
        xn = sb("xn", [128, DC, T])
        sq = sb("sq", [128, DC, T])
        rstd = sb("rstd", [128, T])
        posb = sb("posb", [128, DC, POS])
        cls0 = sb("cls0", [128, DC])
        w1q = sb("w1q", [128, DC, 1024], BF16)
        w2q = sb("w2q", [128, FC, D], BF16)
        wabs = sb("wabs", [128, 2])
        wscale = sb("wscale", [128, 2])
        wmean = sb("wmean", [128, 2])

        arena = sb("arena", [128, 24064])
        where = [0]

        def take(n, start=None):
            if start is not None:
                where[0] = start
            a = where[0]
            where[0] += n
            assert where[0] <= 24064, where
            return arena[:, a:a + n]

        xm = take(INNER_C * T, 0).rearrange("p (c t) -> p c t", c=INNER_C)
        zs = take(INNER_C * T).rearrange("p (c t) -> p c t", c=INNER_C)
        xc = take(INNER_C * T).rearrange("p (c t) -> p c t", c=INNER_C)
        bd = take(12 * 128).rearrange("p (n m) -> p n m", n=12)
        bd_t = take(12 * 128).rearrange("p (n m) -> p n m", n=12)
        hst = take(INNER_C * T).rearrange("p (c t) -> p c t", c=INNER_C)
        q_hl = hst.rearrange("p c t -> p (c t)").bitcast(F16)
        k_hl = take(INNER_C * T + SPILL // 2).bitcast(F16)
        cacc = k_hl.bitcast(F32)[:, 0:INNER_C * T].rearrange("p (c t) -> p c t", c=INNER_C)
        v = take(G * 512).bitcast(F16).rearrange("p (w g m) -> p w g m", w=2, g=G)
        hraw = take(G * 512).rearrange("p (g m) -> p g m", g=G)
        lf = hraw.rearrange("p g m -> p (g m)")[0:INNER_C, 0:4 * T].rearrange("p (n t) -> p n t", n=4)
        patch_sb = arena[:, where[0] - G * 1024:where[0] - G * 1024 + TOK_K * B * PATCHES].rearrange(
            "p (k t) -> p k t", k=TOK_K)
        tokw = arena[:, where[0] - G * 1024 + TOK_K * B * PATCHES:
                     where[0] - G * 1024 + TOK_K * B * PATCHES + TOK_K * D].rearrange("p (k m) -> p k m", k=TOK_K)
        wraw1 = sb("wraw1", [128, DC, 1024])
        wraw2 = wup[:, :, :].rearrange("p a b -> p (a b)").rearrange("p (k m) -> p k m", k=FC)
        aff = take(G * E, 0).rearrange("p (g e) -> p g e", g=G)[0:GT]
        rest = take(G * E).rearrange("p (g e) -> p g e", g=G)[0:GT]
        mask_hl = take(G * E).bitcast(F16).rearrange("p (g e) -> p g e", g=G)[0:GT]
        maskT = take(T // 2).bitcast(F16)
        xhi = take(DC * T // 2).bitcast(F16).rearrange("p (c t) -> p c t", c=DC)
        xlo = take(DC * T // 2).bitcast(F16).rearrange("p (c t) -> p c t", c=DC)
        sg = take(2 * HT).rearrange("p (s t) -> p s t", s=2)
        gu = take(2 * HT).rearrange("p (s t) -> p s t", s=2)
        act = take(2 * HT).rearrange("p (s t) -> p s t", s=2)
        ahi = take(HT).bitcast(F16).rearrange("p (s t) -> p s t", s=2)
        alo = take(HT).bitcast(F16).rearrange("p (s t) -> p s t", s=2)
        whi = take(2 * WE).bitcast(F16).rearrange("p (s m) -> p s m", s=4)
        wlo = take(2 * WE).bitcast(F16).rearrange("p (s m) -> p s m", s=4)
        otok = take(B * D, 0).rearrange("p (b m) -> p b m", b=B)
        q1_hl = take(DC * T, 0).bitcast(F16).rearrange("p (w c t) -> p w c t", w=2, c=DC)
        rsum = take(2 * HT).rearrange("p (s t) -> p s t", s=2)
        rt = take(4 * HT).rearrange("p (s c t) -> p s c t", s=2, c=2)
        xdup = take(2 * DC * T).rearrange("p (c b i t) -> p c b i t", c=DC, b=B, i=2)
        oT = xdup.rearrange("p c b i t -> p (c b i t)")[:, DC * T:2 * DC * T].rearrange("p (c t) -> p c t", c=DC)
        k1_hl = take(DC * T).bitcast(F16).rearrange("p (w c t) -> p w c t", w=2, c=DC)
        qm_flat = take(DC * B * QH * POS + SPILL // 2).bitcast(F16)
        qm = qm_flat[:, 0:2 * DC * B * QH * POS].rearrange("p (w c b h t) -> p w c b h t", w=2, c=DC, b=B, h=QH)
        v1 = take(B * D).bitcast(F16).rearrange("p (w b m) -> p w b m", w=2, b=B)
        pr = take(2 * 2 * 6 * POS).rearrange("p (s n t) -> p s n t", s=2, n=12)
        ph = take(2 * 6 * 2 * POS).bitcast(F16).rearrange("p (s n w t) -> p s n w t", s=2, n=12, w=2)
        pT = take(6 * PTW).bitcast(F16).rearrange("p (s m) -> p s m", s=2)
        hid = take(FC * T, 0).rearrange("p (c t) -> p c t", c=FC)
        h2 = take(FC * T).rearrange("p (c t) -> p c t", c=FC)
        h2q = take(FC * T // 2).bitcast(BF16).rearrange("p (c t) -> p c t", c=FC)
        x4q = take(DC * T // 2).bitcast(BF16).rearrange("p (c t) -> p c t", c=DC)
        habs = take(FC * T).rearrange("p (c t) -> p c t", c=FC)
        amax = take(T)
        bscale = take(T)
        binv = take(T)
        gts = sb("gts", [64, T])
        arow = sb("arow", [INNER_C, T])
        rrow = sb("rrow", [INNER_C, 2, T])
        a3 = sb("a3", [96, T + SPILL], BF16)
        m3 = sb("m3", [96, T], BF16)
        sel3 = sb("sel3", [96, INNER_C, 128], BF16)
        ident_b = sb("ident_b", [GT, 128], BF16)
        ones_h = sb("ones_h", [128, 1], F16)
        mrow = sb("mrow", [INNER_C, T])
        lcum = sb("lcum", [INNER_C, T])
        nrow = sb("nrow", [INNER_C, T])
        geff = sb("geff", [128, 8, 64])
        dmat = sb("dmat", [GT, 2, INNER_C, GT])
        cmat = sb("cmat", [GT, 2, INNER_C * GT])
        c_hl = sb("c_hl", [GT, 2, 2, INNER_C * GT + SPILL], F16)
        floor_t = sb("floor_t", [GT, G * INNER_C])
        csum = sb("csum", [GT, G * INNER_C])
        stat = sb("stat", [GT, G * INNER_C, 6])
        mv = sb("mv", [GT, G * INNER_C, 2])
        tiny = sb("tiny", [GT, 6, G * INNER_C])
        top = sb("top", [GT, G, 8])
        den = sb("den", [GT, 3, G])
        stage = sb("stage", [128, 4, WE])
        shared_w = wg[:, :, :].rearrange("p a b -> p (a b)")
        smx = sb("smx", [128, 2, 3, 12])
        tmx = sb("tmx", [GT, G])
        tsc = sb("tsc", [GT, 2, G])
        tscT = sb("tscT", [2 * G, GT])

        def col(name, i=0, rows=slice(0, 128)):
            a = COLS[name][0] + i
            return colp[rows, a:a + 1]

        ld_first = sem("ld_first")
        ld_attn = sem("ld_attn")
        ld_ffn = sem("ld_ffn")
        ld_bit = sem("ld_bit")
        ld_stage = [sem("ld_stage_a"), sem("ld_stage_b")]
        consts = sem("consts")
        pool_step = sem("pool_step")
        vec_step = sem("vec_step")
        act_step = sem("act_step")
        wscaled, wmean_done, wq_done = sem("wscaled"), sem("wmean_done"), sem("wq_done")
        wabs_done = sem("wabs_done")
        wmean_mm = sem("wmean_mm")
        bd_done = sem("bd_done")
        tok_mm = sem("tok_mm")
        h_ready = sem("h_ready")
        ln_mean, ln_cent, ln_sq = sem("ln_mean"), sem("ln_cent"), sem("ln_sq")
        ln_var, ln_std, xn_ready = sem("ln_var"), sem("ln_std"), sem("xn_ready")
        geff_mm, geff_done = sem("geff_mm"), sem("geff_done")
        up_mm, xm_done, zs_done = sem("up_mm"), sem("xm_done"), sem("zs_done")
        conv_first, conv_done, xc_ready = sem("conv_first"), sem("conv_done"), sem("xc_ready")
        qk_mm, qkhi_done, qklo_done = sem("qk_mm"), sem("qkhi_done"), sem("qklo_done")
        gates_mm, gts_done = sem("gates_mm"), sem("gts_done")
        v_mm, v_done, vlo_done = sem("v_mm"), sem("v_done"), sem("vlo_done")
        absf_done, lnf_done, arow_done = sem("absf_done"), sem("lnf_done"), sem("arow_done")
        nrow_in, nrow_done, floor_mm = sem("nrow_in"), sem("nrow_done"), sem("floor_mm")
        s_mm, e_mm, d_done, c_done, c_split = sem("s_mm"), sem("e_mm"), sem("d_done"), sem("c_done"), sem("c_split")
        hv_mm, hraw_done, hstat_done = sem("hv_mm"), sem("hraw_done"), sem("hstat_done")
        hvar_done, hstd_done, hn_done = sem("hvar_done"), sem("hstd_done"), sem("hn_done")
        skip_done, ht_mm, hst_done, down0_mm = sem("skip_done"), sem("ht_mm"), sem("hst_done"), sem("down0_mm")
        route_mm, aff_done, mask_done, maskt_mm, maskt_done = (
            sem("route_mm"), sem("aff_done"), sem("mask_done"), sem("maskt_mm"), sem("maskt_done"))
        xhi_done, xlo_done = sem("xhi_done"), sem("xlo_done")
        whi_done, wlo_done = sem("whi_done"), sem("wlo_done")
        gate_mm, uproj_mm, mask_mm, down_mm = sem("gate_mm"), sem("uproj_mm"), sem("mask_mm"), sem("down_mm")
        silu_done, gu_done, act_done, alo_done = (
            sem("silu_done"), sem("gu_done"), sem("act_done"), sem("alo_done"))
        ahi_done = sem("ahi_done")
        rope_mm, rope_t, rope_sum, rope_hi, rope_done, qm_done = (
            sem("rope_mm"), sem("rope_t"), sem("rope_sum"), sem("rope_hi"), sem("rope_done"), sem("qm_done"))
        vb_mm, v1hi_done, v1lo_done, xdup_done = sem("vb_mm"), sem("v1hi_done"), sem("v1lo_done"), sem("xdup_done")
        sc_mm, sc_sub, sc_exp, p_done = sem("sc_mm"), sem("sc_sub"), sem("sc_exp"), sem("p_done")
        pt_mm, pt_done, pv_mm, ot_done = sem("pt_mm"), sem("pt_done"), sem("pv_mm"), sem("ot_done")
        ott_mm, oT_done, wo_mm = sem("ott_mm"), sem("oT_done"), sem("wo_mm")
        amax_done, amaxt_mm, tsc_done, tsct_mm, tsct_done, bc_mm, bc_done = (
            sem("amax_done"), sem("amaxt_mm"), sem("tsc_done"), sem("tsct_mm"), sem("tsct_done"),
            sem("bc_mm"), sem("bc_done"))
        quant_mul, xq_done = sem("quant_mul"), sem("xq_done")
        w1_mm, hid_done, fconv_first, fconv_done, h2_done, habs_done, w2_mm = (
            sem("w1_mm"), sem("hid_done"), sem("fconv_first"), sem("fconv_done"), sem("h2_done"), sem("habs_done"), sem("w2_mm"))
        stored = sem("stored")

        block = ctx.enter_context(nc.Block())

        def half(x, c, hf):
            return x[:, c, hf * HT:(hf + 1) * HT]

        def images(ap):
            return ap.rearrange("p (b t) -> p b t", t=POS)

        LOOPS = E // 4 - 1

        @block.sync
        def _(sp):
            sp.dma_start(patch_sb, patches).then_inc(ld_first, 16)
            sp.dma_start(tokw, tok_w).then_inc(ld_first, 16)
            sp.dma_start(posw[:, :, :], pos).then_inc(ld_first, 16)
            sp.dma_start(colp[:, :], cols).then_inc(ld_first, 16)
            for dst, src in ((blk[:, :, :], blocks), (blk_t[:, :, :], blocks_t), (wg[:, :, :], w_gates),
                             (wup[:, :, :], w_up), (wdn[:, :, :], w_down)):
                sp.dma_start(dst, src).then_inc(ld_attn, 16)
            sp.dma_start(wrt[:, :, :], w_router).then_inc(ld_ffn, 16)
            for s in range(2):
                sp.dma_start(stage[:, 2 * s:2 * s + 2, :], w_experts[:, 2 * s:2 * s + 2, :]).then_inc(ld_stage[s], 16)
            for dst, src in ((wraw1[:, :, :], ffn_w1), (l1w[:, :, :, :], l1_w), (ropew[:, :, :], rope)):
                sp.dma_start(dst, src).then_inc(ld_bit, 16)
            sp.wait_ge(up_mm, 16)
            sp.dma_start(wraw2, ffn_w2).then_inc(ld_bit, 16)
            sp.wait_ge(geff_mm, 1)
            sp.dma_start(shared_w, w_shared).then_inc(ld_ffn, 16)
            with sp.Fori(0, LOOPS) as it:
                for s in range(2):
                    sp.wait_ge(wlo_done, it * 4 + 2 * s + 3)
                    sp.dma_start(stage[:, 2 * s:2 * s + 2, :],
                                 w_experts[:, bass.ds(it * 4 + 4 + 2 * s, 2), :]).then_inc(ld_stage[s], 16)
            sp.wait_ge(h_ready, 20)
            sp.dma_start(out, h[:, :, :]).then_inc(stored, 16)
            sp.wait_ge(stored, 16)

        @block.gpsimd
        def _(pool):
            steps = [0]

            def link(ins):
                steps[0] += 1
                ins.then_inc(pool_step, 1)
                pool.wait_ge(pool_step, steps[0])

            def select(x, compare, fill, base, pattern, by, source=None):
                return pool.affine_select(out=x, in_=x if source is None else source, compare_op=compare, fill=fill,
                                          base=base, pattern=pattern, channel_multiplier=by)

            pool.memset(mean_w[:, :], 1.0 / D)
            pool.memset(eps_col[:, :], 1e-5)
            pool.memset(magic_col[:, :], MAGIC)
            pool.memset(zero_w[:, :], 0.0)
            link(pool.memset(ones[:, :], 1.0))
            select(ident[:, :], ALU.is_equal, 0.0, 0, [[-1, 128]], 1, ones[:, :])
            link(select(in_block[:, :], ALU.is_ge, 0.0, 0, [[-4, 32]], 1, ones[:, 0:32]))
            select(in_block[:, :], ALU.is_ge, 0.0, 3, [[4, 32]], -1).then_inc(consts, 1)
            link(select(head_col[:, :], ALU.is_ge, 0.0, 0, [[-HD1, H1C]], 1, ones[:, 0:H1C]))
            select(head_col[:, :], ALU.is_ge, 0.0, HD1 - 1, [[HD1, H1C]], -1)
            pool.tensor_copy(ident_h[:, :], ident[:, :])
            pool.tensor_tensor(expert_sel[:, :], ident[:, 0:E], ident[:, E:2 * E], ALU.add)
            link(pool.memset(ones_h[:, :], 1.0))
            link(pool.memset(sel3[:, :, :], 0.0))
            for part in range(3):
                link(select(sel3[:, :, :], ALU.not_equal, 1.0, -32 * part, [[-1, INNER_C], [0, 128]], 1))
            link(pool.memset(a3[:, :], 0.0))
            link(pool.memset(m3[:, :], 0.0))
            pool.tensor_copy(ident_b[:, :], ident[0:GT, :])
            pool.memset(c_hl[:, :, :, :], 0.0)
            link(pool.memset(causal[:, :, :], 0.0))
            link(select(causal[:, :, :], ALU.is_ge, NEG, 0, [[0, INNER_C], [1, GT]], -1))
            link(select(causal[:, :, POS:GT], ALU.is_ge, NEG, -POS, [[0, INNER_C], [0, POS]], 1))
            pool.memset(restart_mul[:, :, :], 1.0)
            link(pool.memset(restart_add[:, :, :], 0.0))
            pool.memset(restart_mul[:, :, 0:1], 0.0)
            link(pool.memset(restart_add[:, :, 0:1], NEG))
            pool.drain().then_inc(consts, 2)

            pool.wait_ge(ld_attn, 80)
            for dst, src in ((bd_t, blk_t), (bd, blk)):
                pool.tensor_tensor(dst.rearrange("p n (a b) -> p n a b", b=4),
                                   src[:, :, :].unsqueeze(2).broadcast_to([128, 12, 32, 4]),
                                   in_block[:, :].unsqueeze(1).unsqueeze(3).broadcast_to([128, 12, 32, 4]),
                                   ALU.mult).then_inc(bd_done, 1)

            for i, (raw, ints) in enumerate(((wraw1, w1q), (wraw2, w2q))):
                pool.wait_ge(wscaled, i + 1)
                link(pool.tensor_scalar(raw[:, :, :], raw[:, :, :], MAGIC, 1.0, ALU.subtract, ALU.min))
                pool.tensor_scalar(ints[:, :, :], raw[:, :, :], -1.0, None, ALU.max).then_inc(wq_done, 1)

            def split_low(w, slot, n):
                pool.wait_ge(whi_done, n + 1)
                pool.tensor_tensor(wlo[:, slot, :], w, whi[:, slot, :], ALU.subtract).then_inc(wlo_done, 1)

            split_low(shared_w[:, :], 3, 0)
            for e in range(3):
                split_low(stage[:, e, :], e, e + 1)
            with pool.Fori(0, LOOPS) as it:
                for j in range(4):
                    s = (j + 3) % 4
                    split_low(stage[:, s, :], s, it * 4 + (j + 4))
            split_low(stage[:, 3, :], 3, E)

        @block.tensor
        def _(pe):
            pe.wait_ge(consts, 3)

            def layer_norm(n):
                for hf in range(2):
                    pe.wait_ge(h_ready, 4 * n + 2 * hf + 2)
                    for c in range(DC):
                        mm = pe.matmul(bank[4 + hf][:, 0:HT], mean_w[:, :], half(h, c, hf), start=c == 0, stop=c == DC - 1)
                    mm.then_inc(ln_mean, 1)
                for hf in range(2):
                    pe.wait_ge(ln_sq, 2 * n + hf + 1)
                    for c in range(DC):
                        mm = pe.matmul(bank[6 + hf][:, 0:HT], mean_w[:, :], half(sq, c, hf), start=c == 0, stop=c == DC - 1)
                    mm.then_inc(ln_var, 1)

            pe.wait_ge(ld_first, 64)
            for hf in range(2):
                for m in range(DC):
                    for k in range(TOK_K):
                        mm = pe.matmul(bank[2 * hf + m][:, 0:HB * PATCHES], tokw[:, k, m * 128:(m + 1) * 128],
                                       patch_sb[:, k, hf * HB * PATCHES:(hf + 1) * HB * PATCHES],
                                       start=k == 0, stop=k == TOK_K - 1)
                    mm.then_inc(tok_mm, 1)
            layer_norm(0)

            pe.wait_ge(ld_attn, 80)
            for n in range(16):
                hf, m = n // 8, (n % 8) // 2 + 4 * (n % 2)
                if n % 8 == 0:
                    pe.wait_ge(xn_ready, hf + 1)
                if n >= 4:
                    pe.wait_ge((xm_done, zs_done)[n % 2], n // 2 - 1)
                for k in range(DC):
                    mm = pe.matmul(bank[n % 4][:, 0:HT], wup[:, k, m * 128:(m + 1) * 128], half(xn, k, hf),
                                   start=k == 0, stop=k == DC - 1)
                mm.then_inc(up_mm, 1)

            pe.wait_ge(bd_done, 1)
            for c in range(INNER_C):
                pe.matmul(bank[4][:, c * 64:(c + 1) * 64], bd_t[:, c, :], wg[:, c, :], start=True, stop=False)
                pe.matmul(bank[4][:, c * 64:(c + 1) * 64], bd_t[:, 4 + c, :], wg[:, 4 + c, :], start=False, stop=True)
            for c in range(INNER_C):
                mm = pe.matmul(bank[4][:, (4 + c) * 64:(5 + c) * 64], bd_t[:, 8 + c, :], wg[:, 8 + c, :],
                               start=True, stop=True)
            mm.then_inc(geff_mm, 1)

            pe.wait_ge(bd_done, 2)
            pe.wait_ge(xm_done, 8)
            pe.wait_ge(zs_done, 8)
            for n in range(8):
                g = n
                b2 = 5 + n % 2
                if n >= 2:
                    pe.wait_ge(vlo_done, n - 1)
                for c in range(INNER_C):
                    mm = pe.matmul(bank[b2][0:GT, c * DH:(c + 1) * DH], xm[:, c, g * GT:(g + 1) * GT],
                                   bd[:, 8 + c, :], start=True, stop=True)
                mm.then_inc(v_mm, 1)
            for n in range(16):
                c, hf, kind = n // 4, (n // 2) % 2, n % 2
                pe.wait_ge(xc_ready, c + 1)
                if n >= 4:
                    pe.wait_ge(qklo_done, n - 3)
                pe.matmul(bank[n % 4][:, 0:HT], bd[:, 4 * kind + c, :], half(xc, c, hf),
                          start=True, stop=True).then_inc(qk_mm, 1)
            pe.wait_ge(geff_done, 1)
            pe.wait_ge(vlo_done, 8)
            for hf in range(2):
                for c in range(INNER_C):
                    pe.matmul(bank[4 + hf][0:64, 0:HT], geff[:, c, :], half(xc, c, hf), start=c == 0, stop=False)
                for c in range(INNER_C):
                    mm = pe.matmul(bank[4 + hf][0:64, 0:HT], geff[:, 4 + c, :],
                                   half(xm, c, hf), start=False, stop=c == INNER_C - 1)
                mm.then_inc(gates_mm, 1)

            def scores(g):
                if g == 0:
                    pe.wait_ge(qklo_done, 16)
                if g >= 2:
                    pe.wait_ge(c_done, g - 1)
                tok = slice(g * GT, (g + 1) * GT)
                for c in range(INNER_C):
                    for i, (kw, qw) in enumerate(PARTS):
                        k_at = (kw * INNER_C + c) * T + g * GT
                        q_at = (qw * INNER_C + c) * T + g * GT
                        mm = pe.matmul(bank[g % 2][:, c * GT:(c + 1) * GT], k_hl[:, k_at:k_at + 128],
                                       q_hl[:, q_at:q_at + GT], start=i == 0, stop=i == 2)
                mm.then_inc(s_mm, 1)
                if g == 0:
                    pe.wait_ge(arow_done, 1)
                dst = bank[2 + g % 2]
                pe.matmul(dst[:, 0:INNER_C * GT], a3[0:68, g * GT:g * GT + 128], sel3[0:68, :, 0:GT], start=True, stop=False)
                for c in range(INNER_C):
                    pe.matmul(dst[:, c * GT:(c + 1) * GT], sel3[0:68, c, :], m3[0:68, tok], start=False, stop=False)
                pe.matmul(dst[:, 0:INNER_C * GT], ident_b[:, :], causal[:, :, :],
                          start=False, stop=True).then_inc(e_mm, 1)

            pe.wait_ge(consts, 2)
            scores(0)
            for g in range(G):
                if g + 1 < G:
                    scores(g + 1)
                if g == 0:
                    pe.wait_ge(nrow_done, 1)
                    for gg in range(G):
                        mm = pe.matmul(bank[7][0:GT, gg * INNER_C:(gg + 1) * INNER_C], nrow[:, gg * GT:(gg + 1) * GT],
                                       ident[0:INNER_C, 0:INNER_C], start=True, stop=True)
                    mm.then_inc(floor_mm, 1)
                    pe.wait_ge(gts_done, 2)
                pe.wait_ge(c_split, g + 1)
                if g >= 2:
                    pe.wait_ge(hstat_done, g - 1)
                    pe.wait_ge(hraw_done, g - 1)
                for c in range(INNER_C):
                    high, low = (c_hl[:, g % 2, w, c * GT:c * GT + 128] for w in range(2))
                    total = bank[6][:, g * INNER_C + c:g * INNER_C + c + 1]
                    pe.matmul(total, high, ones_h[0:GT, :], start=True, stop=False)
                    pe.matmul(total, low, ones_h[0:GT, :], start=False, stop=True)
                    for i, (cw, vw) in enumerate(PARTS):
                        mm = pe.matmul(bank[4 + g % 2][:, c * DH:(c + 1) * DH], (high, low)[cw],
                                       v[0:GT, vw, g, c * DH:(c + 1) * DH], start=i == 0, stop=i == 2)
                mm.then_inc(hv_mm, 1)
            pe.wait_ge(wabs_done, 2)
            pe.matmul(bank[3][:, 0:2], ones[:, :], wabs[:, :], start=True, stop=True).then_inc(wmean_mm, 1)
            for g in range(G):
                pe.wait_ge(hn_done, g + 1)
                if g >= 2:
                    pe.wait_ge(hst_done, g - 1)
                for c in range(INNER_C):
                    mm = pe.transpose(bank[g % 2][:, c * GT:(c + 1) * GT], hraw[0:GT, g, c * DH:(c + 1) * DH],
                                      ident[0:GT, 0:GT])
                mm.then_inc(ht_mm, 1)
            for hf in range(2):
                if hf == 0:
                    pe.wait_ge(hst_done, G)
                for m in range(DC):
                    for k in range(INNER_C):
                        mm = pe.matmul(bank[2 * hf + m][:, 0:HT], wdn[:, k, m * 128:(m + 1) * 128], half(hst, k, hf),
                                       start=k == 0, stop=k == INNER_C - 1)
                    mm.then_inc(down0_mm, 1)

            layer_norm(1)

            pe.wait_ge(ld_ffn, 32)
            pe.wait_ge(xn_ready, 4)
            for g in range(G):
                for k in range(DC):
                    mm = pe.matmul(bank[7][0:GT, g * E:(g + 1) * E], xn[:, k, g * GT:(g + 1) * GT], wrt[:, k, :],
                                   start=k == 0, stop=k == DC - 1)
            mm.then_inc(route_mm, 1)

            def into_hidden(dst, slot, at, hf, done):
                n = 0
                for k in range(DC):
                    w_at = slice(at + k * 128, at + (k + 1) * 128)
                    for w, x in ((whi, xhi), (whi, xlo), (wlo, xhi)):
                        mm = pe.matmul(dst[:, 0:HT], w[:, slot, w_at], half(x, k, hf), start=n == 0, stop=n == 5)
                        n += 1
                mm.then_inc(done, 1)

            def down(slot, hf, n, last=False):
                pe.wait_ge(alo_done, n + 1)
                s = hf
                for m in range(DC):
                    w_at = slice(512 + m * 128, 512 + (m + 1) * 128)
                    for i, (w, x) in enumerate(((whi, ahi), (whi, alo), (wlo, ahi))):
                        mm = pe.matmul(bank[2 * hf + m][:, 0:HT], w[:, slot, w_at], x[:, s, :],
                                       start=False, stop=last and i == 2, skip_group_check=True)
                mm.then_inc(down_mm, 1)

            pe.wait_ge(wlo_done, 1)
            pe.wait_ge(xlo_done, 2)
            for i in range(4):
                pe.matmul(bank[i][:, 0:HT], zero_w[:, :], half(xhi, 0, 0), start=True, stop=False, skip_group_check=True)
            into_hidden(bank[4], 3, 0, 0, gate_mm)
            into_hidden(bank[5], 3, 256, 0, uproj_mm)
            pe.wait_ge(aff_done, 1)
            into_hidden(bank[6], 3, 0, 1, gate_mm)
            into_hidden(bank[7], 3, 256, 1, uproj_mm)
            down(3, 0, 0)
            pe.wait_ge(mask_done, 1)
            pe.wait_ge(act_done, 1)
            for g in range(G):
                mm = pe.transpose(bank[4][:, g * 64:g * 64 + 64].bitcast(F16)[:, 0:GT], mask_hl[:, g, :], ident_h[0:GT, 0:GT])
            mm.then_inc(maskt_mm, 1)
            pe.wait_ge(maskt_done, 1)

            def four_experts(it, last=False):
                r = 0
                for j in range(4):
                    for hf in range(2):
                        n = it * 8 + (2 * j + hf + 2)
                        if hf == 0:
                            pe.wait_ge(wlo_done, it * 4 + (j + 2))
                        for kind in range(3):
                            old = r - 4
                            steps = n - (2 * j + hf) + old // 3
                            pe.wait_ge((silu_done, gu_done, act_done)[old % 3], steps + 1)
                            b = bank[4 + r % 4]
                            if kind == 0:
                                into_hidden(b, j, 0, hf, gate_mm)
                            elif kind == 1:
                                into_hidden(b, j, 256, hf, uproj_mm)
                            else:
                                e = it * 4 + j
                                pe.matmul(b[:, 0:HT], expert_sel[:, bass.ds(e, 1)].broadcast_to([128, 128]),
                                          maskT[:, hf * HT:(hf + 1) * HT], start=True, stop=True).then_inc(mask_mm, 1)
                            r += 1
                        down((j - 1 + hf) % 4, 1 - hf, n - 1, last=last and j == 3 and hf == 1)

            with pe.Fori(0, LOOPS) as it:
                four_experts(it)
            four_experts(LOOPS, last=True)
            down(3, 1, 2 * E + 1, last=True)

            layer_norm(2)

            pe.wait_ge(ld_bit, 64)
            n = 0
            for hf in range(2):
                pe.wait_ge(xn_ready, 4 + hf + 1)
                for qk in range(2):
                    for m in range(DC):
                        if n >= 2:
                            pe.wait_ge(rope_t, n - 1)
                        for sw in range(2):
                            b = bank[2 * (n % 2) + sw]
                            for k in range(DC):
                                mm = pe.matmul(b[:, 0:HT], l1w[:, 2 * qk + sw, k, m * 128:(m + 1) * 128], half(xn, k, hf),
                                               start=k == 0, stop=k == DC - 1)
                        mm.then_inc(rope_mm, 1)
                        n += 1
            pe.wait_ge(xdup_done, 2)
            for n in range(G):
                if n >= 2:
                    pe.wait_ge(v1lo_done, n - 1)
                for i in range(2):
                    b = 2 * n + i
                    for k in range(DC):
                        mm = pe.matmul(bank[4 + n % 2][0:GT, i * D:(i + 1) * D],
                                       xdup[:, k, b, :, :].rearrange("p i t -> p (i t)"),
                                       l1w[:, 4, k, :], start=k == 0, stop=k == DC - 1)
                mm.then_inc(vb_mm, 1)

            U = 3 * POS

            def att_scores(n):
                if n == 0:
                    pe.wait_ge(qm_done, 8)
                    pe.wait_ge(rope_done, 8)
                if n >= 2:
                    pe.wait_ge(sc_sub, n - 1)
                for i in range(2):
                    b = 2 * n + i
                    for c in range(DC):
                        for u in range(3):
                            o = (i * 6 + c * 3 + u) * POS
                            for j, (qw, kw) in enumerate(PARTS):
                                at = ((qw * DC + c) * B + b) * QH * POS + u * U
                                mm = pe.matmul(bank[n % 2][:, o:o + POS], qm_flat[:, at:at + 128],
                                               k1_hl[:, kw, c, b * POS:(b + 1) * POS], start=j == 0, stop=j == 2)
                mm.then_inc(sc_mm, 1)

            def turn(b):
                pe.wait_ge(p_done, b // 2 + 1)
                if b >= 2:
                    pe.wait_ge(pt_done, b - 1)
                for u in range(6):
                    mm = pe.transpose(bank[2 + b % 2][0:2 * POS, 56 * u:56 * (u + 1)].bitcast(F16)[:, 0:U],
                                      ph[0:U, (b // 2) % 2, (b % 2) * 6 + u, :, :].rearrange("p w t -> p (w t)"),
                                      ident_h[0:U, 0:U])
                mm.then_inc(pt_mm, 1)

            att_scores(0)
            att_scores(1)
            pe.wait_ge(v1lo_done, 8)
            turn(0)
            for b in range(B):
                if b % 2 == 0 and b // 2 + 2 < G:
                    att_scores(b // 2 + 2)
                if b + 1 < B:
                    turn(b + 1)
                pe.wait_ge(pt_done, b + 1)
                if b >= 2:
                    pe.wait_ge(ot_done, b - 1)
                for hh in range(H1):
                    c, q = hh // H1C, hh % H1C
                    at = (3 * c + q // 3) * PTW + q % 3 * POS
                    dst = bank[4 + b % 2][0:POS, hh * HD1:(hh + 1) * HD1]
                    feat = slice(hh * HD1, (hh + 1) * HD1)
                    pe.matmul(dst, pT[0:2 * POS, b % 2, at:at + POS], v1[0:2 * POS, 0, b, feat], start=True, stop=False)
                    mm = pe.matmul(dst, pT[0:POS, b % 2, at:at + POS], v1[0:POS, 1, b, feat], start=False, stop=True)
                mm.then_inc(pv_mm, 1)
            for c in range(DC):
                for hf in range(2):
                    for b in range(HB):
                        if c == 0:
                            pe.wait_ge(ot_done, hf * HB + b + 1)
                        mm = pe.transpose(bank[2 * c + hf][:, b * POS:(b + 1) * POS],
                                          otok[0:POS, hf * HB + b, c * 128:(c + 1) * 128], ident[0:POS, 0:POS])
                    mm.then_inc(ott_mm, 1)
            for hf in range(2):
                pe.wait_ge(oT_done, 4)
                for m in range(DC):
                    for k in range(DC):
                        mm = pe.matmul(bank[4 + 2 * hf + m][:, 0:HT], l1w[:, 5, k, m * 128:(m + 1) * 128], half(oT, k, hf),
                                       start=k == 0, stop=k == DC - 1)
                    mm.then_inc(wo_mm, 1)

            layer_norm(3)

            def token_scales(n):
                pe.wait_ge(amax_done, n + 1)
                for g in range(G):
                    b = bank[(4, 5)[g // 4]]
                    mm = pe.transpose(b[0:GT, (g % 4) * 128:(g % 4 + 1) * 128], amax[:, g * GT:(g + 1) * GT], ident[:, :])
                mm.then_inc(amaxt_mm, 1)
                pe.wait_ge(tsc_done, n + 1)
                pe.transpose(bank[6][0:2 * G, 0:GT], tsc[:, :, :].rearrange("p a g -> p (a g)"),
                             ident[0:GT, 0:GT]).then_inc(tsct_mm, 1)
                pe.wait_ge(tsct_done, n + 1)
                for kind in range(2):
                    for g in range(G):
                        b = bank[4 + 2 * kind + g // 4]
                        mm = pe.matmul(b[:, (g % 4) * GT:(g % 4 + 1) * GT], ident[0:2 * G, kind * G + g:kind * G + g + 1].broadcast_to([2 * G, 128]),
                                       tscT[:, :], start=True, stop=True)
                    mm.then_inc(bc_mm, 1)

            token_scales(0)
            pe.wait_ge(wq_done, 2)
            for n in range(16):
                hf, m = n // 8, n % 8
                pe.wait_ge(xq_done, 2 * hf + 2)
                if n >= 4:
                    pe.wait_ge(hid_done, n - 3)
                for k in range(DC):
                    mm = pe.matmul(bank[n % 4][:, 0:HT], w1q[:, k, m * 128:(m + 1) * 128], half(x4q, k, hf),
                                   start=k == 0, stop=k == DC - 1)
                mm.then_inc(w1_mm, 1)
            token_scales(1)
            for hf in range(2):
                for m in range(DC):
                    for k in range(FC):
                        if m == 0 and k % 4 == 0:
                            pe.wait_ge(xq_done, 4 + 2 * hf + k // 4 + 1)
                        mm = pe.matmul(bank[2 * hf + m][:, 0:HT], w2q[:, k, m * 128:(m + 1) * 128], half(h2q, k, hf),
                                       start=k == 0, stop=k == FC - 1)
                    mm.then_inc(w2_mm, 1)

        @block.scalar
        def _(a):
            def layer_norm(n):
                for hf in range(2):
                    a.wait_ge(ln_cent, 2 * n + hf + 1)
                    a.activation(sq[:, :, hf * HT:(hf + 1) * HT], xn[:, :, hf * HT:(hf + 1) * HT], ACT.Square).then_inc(ln_sq, 1)
                for hf in range(2):
                    a.wait_ge(ln_var, 2 * n + hf + 1)
                    a.activation(rstd[:, hf * HT:(hf + 1) * HT], bank[6 + hf][:, 0:HT], ACT.Sqrt,
                                 bias=eps_col[:, :]).then_inc(ln_std, 1)

            a.wait_ge(consts, 3)
            layer_norm(0)
            for n in range(8):
                a.wait_ge(up_mm, 2 * n + 2)
                hf, c = n // 4, n % 4
                a.activation(half(zs, c, hf), bank[(2 * n + 1) % 4][:, 0:HT], ACT.Silu).then_inc(zs_done, 1)
            for c in range(INNER_C):
                a.wait_ge(xm_done, 5 + c)
                a.activation(cacc[:, c, :], xm[:, c, :], ACT.Identity, bias=col("conv_b", c),
                             scale=col("conv_w", c * CONV + CONV - 1)).then_inc(conv_first, 1)
            for c in range(INNER_C):
                a.wait_ge(conv_done, c + 1)
                a.activation(xc[:, c, :], cacc[:, c, :], ACT.Silu).then_inc(xc_ready, 1)
            for g in range(G):
                a.wait_ge(v_mm, g + 1)
                if g == 0:
                    a.wait_ge(tok_mm, 4)
                a.activation(v[0:GT, 0, g, :], bank[5 + g % 2][0:GT, :], ACT.Copy).then_inc(v_done, 1)
            for n in range(16):
                c, hf, kind = n // 4, (n // 2) % 2, n % 2
                a.wait_ge(qk_mm, n + 1)
                at = c * T + hf * HT
                if kind:
                    a.activation(k_hl[:, at:at + HT], bank[n % 4][:, 0:HT], ACT.Copy).then_inc(qkhi_done, 1)
                else:
                    a.activation(q_hl[:, at:at + HT], bank[n % 4][:, 0:HT], ACT.Copy, scale=QK_SCALE).then_inc(qkhi_done, 1)
            a.wait_ge(absf_done, 1)
            a.activation(lf[:, 1, :], lf[:, 0, :], ACT.Exp, scale=-1.0).then_inc(act_step, 1)
            a.wait_ge(act_step, 1)
            a.activation(lf[:, 1, :], lf[:, 1, :], ACT.Ln, bias=ones[0:INNER_C, 0:1]).then_inc(lnf_done, 1)
            a.wait_ge(nrow_in, 1)
            a.activation(nrow[:, :], nrow[:, :], ACT.Exp, scale=-1.0).then_inc(nrow_done, 1)

            def decay(g):
                a.wait_ge(e_mm, g + 1)
                if g >= 2:
                    a.wait_ge(c_done, g - 1)
                a.activation(dmat[:, g % 2, :, :], bank[2 + g % 2][0:GT, 0:INNER_C * GT], ACT.Exp).then_inc(d_done, 1)

            decay(0)
            for g in range(G):
                if g + 1 < G:
                    decay(g + 1)
                a.wait_ge(hstat_done, g + 1)
                a.activation(hraw[0:GT, g, :], bank[4 + g % 2][0:GT, :], ACT.Copy).then_inc(hraw_done, 1)
            for c in range(INNER_C):
                a.activation(xc[:, c, :], xc[:, c, :], ACT.Copy, scale=col("skip", c)).then_inc(skip_done, 1)
            a.wait_ge(ld_bit, 64)
            for i, (raw, free) in enumerate(((wraw1, k_hl), (wraw2, q_hl))):
                a.activation(free[:, 0:2048], raw[:, :, :].rearrange("p a b -> p (a b)"), ACT.Abs,
                             accum_out=wabs[:, i:i + 1]).then_inc(wabs_done, 1)
            a.wait_ge(hvar_done, 1)
            a.activation(tiny[:, 3, :], tiny[:, 2, :], ACT.Sqrt, bias=eps_col[0:GT, :]).then_inc(hstd_done, 1)

            a.wait_ge(wmean_done, 1)
            for i, raw in enumerate((wraw1, wraw2)):
                a.activation(raw[:, :, :], raw[:, :, :], ACT.Identity, bias=magic_col[:, :],
                             scale=wscale[:, i:i + 1]).then_inc(wscaled, 1)
            layer_norm(1)
            a.wait_ge(ld_ffn, 32)
            a.activation(whi[:, 3, :], shared_w[:, :], ACT.Copy).then_inc(whi_done, 1)
            for hf in range(2):
                a.wait_ge(xn_ready, 2 + hf + 1)
                a.activation(xhi[:, :, hf * HT:(hf + 1) * HT], xn[:, :, hf * HT:(hf + 1) * HT], ACT.Copy).then_inc(xhi_done, 1)
            a.wait_ge(route_mm, 1)
            a.activation(aff[:, :, :].rearrange("p g e -> p (g e)"), bank[7][0:GT, :], ACT.Sigmoid).then_inc(aff_done, 1)

            def split_high(slot, reads):
                a.activation(whi[:, slot, :], stage[:, slot, :], ACT.Copy).then_inc(whi_done, 1)

            for e in range(3):
                if e % 2 == 0:
                    a.wait_ge(ld_stage[e // 2], 16)
                split_high(e, e)

            def silu(b, s, n):
                a.wait_ge(gate_mm, n + 1)
                a.activation(sg[:, s, :], b[:, 0:HT], ACT.Silu).then_inc(silu_done, 1)

            silu(bank[4], 0, 0)
            silu(bank[6], 1, 1)

            def four_experts(it, last=False):
                for j in range(4):
                    for hf in range(2):
                        n = it * 8 + (2 * j + hf + 2)
                        r = 3 * (2 * j + hf)
                        a.wait_ge(gu_done, n - 1)
                        silu(bank[4 + r % 4], hf, n)
                    if last and j > 0:
                        continue
                    s = (j + 3) % 4
                    if s == 0:
                        a.wait_ge(ld_stage[0], it * 16 + 32)
                    if s == 2:
                        a.wait_ge(ld_stage[1], it * 16 + 32)
                    a.wait_ge(down_mm, it * 8 + (2 * j + 2))
                    split_high(s, None)

            with a.Fori(0, LOOPS) as it:
                four_experts(it)
            four_experts(LOOPS, last=True)

            layer_norm(2)
            for i in range(2):
                a.wait_ge(xn_ready, 6)
                a.activation(xdup[:, :, :, i, :].rearrange("p c b t -> p (c b) t"),
                             xn[:, :, :].rearrange("p c (b t) -> p (c b) t", t=POS), ACT.Copy).then_inc(xdup_done, 1)
            n = 0
            for hf in range(2):
                for qk in range(2):
                    for m in range(DC):
                        a.wait_ge(rope_sum, n + 1)
                        a.activation(half((q1_hl, k1_hl)[qk][:, 0], m, hf), rsum[:, n % 2, :], ACT.Copy).then_inc(rope_hi, 1)
                        n += 1
            for n in range(G):
                a.wait_ge(vb_mm, n + 1)
                a.activation(v1[0:GT, 0, 2 * n:2 * n + 2, :], bank[4 + n % 2][0:GT, :].rearrange("p (b m) -> p b m", b=2),
                             ACT.Copy).then_inc(v1hi_done, 1)
            U = 3 * POS

            def exps(n):
                a.wait_ge(sc_sub, n + 1)
                a.activation(pr[0:U, n % 2, :, :], pr[0:U, n % 2, :, :], ACT.Exp, scale=1.0 / 16.0).then_inc(sc_exp, 1)

            def outputs(b):
                a.wait_ge(pv_mm, b + 1)
                a.activation(otok[0:POS, b, :], bank[4 + b % 2][0:POS, 0:D], ACT.Copy).then_inc(ot_done, 1)

            exps(0)
            exps(1)
            for b in range(B):
                if b >= 2:
                    a.wait_ge(pv_mm, b - 1)
                a.wait_ge(pt_mm, b + 1)
                a.activation(pT[0:2 * POS, b % 2, :].rearrange("p (u m) -> p u m", u=6)[:, :, 0:U],
                             bank[2 + b % 2][0:2 * POS, 0:336].bitcast(F16).rearrange("p (u m) -> p u m", u=6)[:, :, 0:U],
                             ACT.Copy).then_inc(pt_done, 1)
                if b >= 1:
                    outputs(b - 1)
                if b % 2 == 0 and b // 2 + 2 < G:
                    exps(b // 2 + 2)
            outputs(B - 1)
            for c in range(DC):
                for hf in range(2):
                    a.wait_ge(ott_mm, 2 * c + hf + 1)
                    a.activation(half(oT, c, hf), bank[2 * c + hf][:, 0:HT], ACT.Identity, bias=col("bv", c)).then_inc(oT_done, 1)

            layer_norm(3)
            for c in range(FC):
                a.wait_ge(hid_done, 9 + c)
                a.activation(h2[:, c, :], hid[:, c, :], ACT.Identity, bias=col("ffn_conv_b", c),
                             scale=col("ffn_conv_w", 3 * c + 1)).then_inc(fconv_first, 1)
            for c in range(FC):
                a.wait_ge(fconv_done, c + 1)
                a.activation(h2[:, c, :], h2[:, c, :], ACT.Silu).then_inc(h2_done, 1)
                a.wait_ge(h2_done, c + 1)
                a.activation(habs[:, c, :], h2[:, c, :], ACT.Abs).then_inc(habs_done, 1)

        @block.vector
        def _(d):
            steps = [0]

            def link(ins):
                steps[0] += 1
                ins.then_inc(vec_step, 1)
                d.wait_ge(vec_step, steps[0])

            def magnitude(out, x):
                return d.scalar_tensor_tensor(out=out, in0=x, scalar=-1.0, in1=x, op0=ALU.mult, op1=ALU.max)

            def layer_norm(n):
                for hf in range(2):
                    tok = slice(hf * HT, (hf + 1) * HT)
                    d.wait_ge(h_ready, 4 * n + 2 * hf + 2)
                    d.wait_ge(ln_mean, 2 * n + hf + 1)
                    d.tensor_tensor(xn[:, :, tok], h[:, :, tok],
                                    bank[4 + hf][:, 0:HT].unsqueeze(1).broadcast_to([128, DC, HT]), ALU.subtract).then_inc(ln_cent, 1)
                for hf in range(2):
                    tok = slice(hf * HT, (hf + 1) * HT)
                    d.wait_ge(ln_std, 2 * n + hf + 1)
                    link(d.reciprocal(rstd[:, tok], rstd[:, tok]))
                    d.tensor_tensor(xn[:, :, tok], xn[:, :, tok],
                                    rstd[:, tok].unsqueeze(1).broadcast_to([128, DC, HT]), ALU.mult).then_inc(xn_ready, 1)

            def add_to_h(banks, done, first):
                for hf in range(2):
                    for m in range(DC):
                        d.wait_ge(done, first + 2 * hf + m + 1)
                        d.tensor_tensor(half(h, m, hf), half(h, m, hf), banks[2 * hf + m][:, 0:HT], ALU.add).then_inc(h_ready, 1)

            d.wait_ge(consts, 3)
            d.wait_ge(ld_first, 64)
            for m in range(DC):
                d.tensor_scalar(posb[:, m, :], posw[:, m, :], col("tok_b", m), None, ALU.add)
                link(d.tensor_tensor(cls0[:, m:m + 1], col("cls", m), posw[:, m, 0:1], ALU.add))
                d.tensor_copy(images(h[:, m, :])[:, :, 0:1], cls0[:, m:m + 1].unsqueeze(1).broadcast_to([128, B, 1]))
            for hf in range(2):
                for m in range(DC):
                    d.wait_ge(tok_mm, 2 * hf + m + 1)
                    d.tensor_tensor(images(half(h, m, hf))[:, :, 1:POS],
                                    bank[2 * hf + m][:, 0:HB * PATCHES].rearrange("p (b t) -> p b t", t=PATCHES),
                                    posb[:, m, 1:POS].unsqueeze(1).broadcast_to([128, HB, PATCHES]), ALU.add).then_inc(h_ready, 1)
            layer_norm(0)

            for n in range(8):
                hf, c = n // 4, n % 4
                d.wait_ge(up_mm, 2 * n + 1)
                d.tensor_copy(half(xm, c, hf), bank[(2 * n) % 4][:, 0:HT]).then_inc(xm_done, 1)
            d.wait_ge(geff_mm, 1)
            d.tensor_copy(geff[:, :, :].rearrange("p a b -> p (a b)"), bank[4][:, :]).then_inc(geff_done, 1)
            for c in range(INNER_C):
                d.wait_ge(conv_first, c + 1)
                for back in range(1, CONV):
                    into = images(cacc[:, c, :])[:, :, back:POS]
                    ins = d.scalar_tensor_tensor(out=into, in0=images(xm[:, c, :])[:, :, 0:POS - back],
                                                 scalar=col("conv_w", c * CONV + CONV - 1 - back), in1=into,
                                                 op0=ALU.mult, op1=ALU.add)
                    if back < CONV - 1:
                        link(ins)
                ins.then_inc(conv_done, 1)
            for n in range(G):
                d.wait_ge(v_done, n + 1)
                d.tensor_tensor(v[0:GT, 1, n, :], bank[5 + n % 2][0:GT, :], v[0:GT, 0, n, :], ALU.subtract).then_inc(vlo_done, 1)
            for n in range(16):
                c, hf, kind = n // 4, (n // 2) % 2, n % 2
                d.wait_ge(qkhi_done, n + 1)
                hi, lo = c * T + hf * HT, (INNER_C + c) * T + hf * HT
                if kind:
                    d.tensor_tensor(k_hl[:, lo:lo + HT], bank[n % 4][:, 0:HT], k_hl[:, hi:hi + HT], ALU.subtract).then_inc(qklo_done, 1)
                else:
                    d.scalar_tensor_tensor(out=q_hl[:, lo:lo + HT], in0=bank[n % 4][:, 0:HT], scalar=QK_SCALE,
                                           in1=q_hl[:, hi:hi + HT], op0=ALU.mult, op1=ALU.subtract).then_inc(qklo_done, 1)
            d.memset(k_hl[:, 2 * INNER_C * T:2 * INNER_C * T + SPILL], 0.0)

            for hf in range(2):
                d.wait_ge(gates_mm, hf + 1)
                d.tensor_scalar(gts[:, hf * HT:(hf + 1) * HT], bank[4 + hf][0:64, 0:HT], col("gate_b", 0, slice(0, 64)),
                                None, ALU.add).then_inc(gts_done, 1)
            d.wait_ge(gts_done, 2)
            d.tensor_scalar(lf[:, 2, :], gts[32:32 + INNER_C, :], 0.0, None, ALU.min)
            magnitude(lf[:, 0, :], gts[32:32 + INNER_C, :]).then_inc(absf_done, 1)
            d.wait_ge(lnf_done, 1)
            link(d.tensor_tensor(lf[:, 3, :], lf[:, 2, :], lf[:, 1, :], ALU.subtract))
            d.wait_ge(consts, 2)
            link(d.tensor_tensor_scan(lcum[:, :], restart_mul[:, :, :].rearrange("p b t -> p (b t)"), lf[:, 3, :], 0.0,
                                      ALU.mult, ALU.add))
            link(d.tensor_tensor(arow[:, :], gts[0:INNER_C, :], lcum[:, :], ALU.subtract))
            link(d.tensor_tensor_scan(mrow[:, :], restart_add[:, :, :].rearrange("p b t -> p (b t)"), arow[:, :], NEG,
                                      ALU.add, ALU.max))
            d.tensor_tensor(nrow[:, :], mrow[:, :], lcum[:, :], ALU.add).then_inc(nrow_in, 1)
            link(d.tensor_scalar(mrow[:, :], mrow[:, :], -1.0, None, ALU.mult))
            rows = ((arow, a3), (mrow, m3))
            for x, parts in rows:
                ins = d.tensor_copy(parts[0:INNER_C, 0:T], x[:, :])
            link(ins)
            for i, (x, parts) in enumerate(rows):
                ins = d.tensor_tensor(rrow[:, i, :], x[:, :], parts[0:INNER_C, 0:T], ALU.subtract)
            link(ins)
            for i, (x, parts) in enumerate(rows):
                ins = d.tensor_copy(parts[32:32 + INNER_C, 0:T], rrow[:, i, :])
            link(ins)
            for i, (x, parts) in enumerate(rows):
                link(d.tensor_copy(x[:, :], parts[32:32 + INNER_C, 0:T]))
                ins = d.tensor_tensor(parts[64:64 + INNER_C, 0:T], rrow[:, i, :], x[:, :], ALU.subtract)
            ins.then_inc(arow_done, 1)

            def weights(g):
                d.wait_ge(d_done, g + 1)
                d.wait_ge(s_mm, g + 1)
                d.tensor_tensor(cmat[:, g % 2, :], bank[g % 2][0:GT, 0:INNER_C * GT],
                                dmat[:, g % 2, :, :].rearrange("p c s -> p (c s)"), ALU.mult).then_inc(c_done, 1)
                d.wait_ge(c_done, g + 1)
                if g >= 2:
                    d.wait_ge(hv_mm, g - 1)
                high, low = (c_hl[:, g % 2, w, 0:INNER_C * GT] for w in range(2))
                link(d.tensor_copy(high, cmat[:, g % 2, :]))
                d.tensor_tensor(low, cmat[:, g % 2, :], high, ALU.subtract).then_inc(c_split, 1)

            weights(0)
            for g in range(G):
                if g + 1 < G:
                    weights(g + 1)
                d.wait_ge(hv_mm, g + 1)
                for c in range(INNER_C):
                    ins = d.bn_stats(stat[:, g * INNER_C + c, :], bank[4 + g % 2][0:GT, c * DH:(c + 1) * DH])
                ins.then_inc(hstat_done, 1)
            d.wait_ge(hstat_done, G)
            for n in range(G * INNER_C):
                ins = d.bn_aggr(mv[:, n, :], stat[:, n, :])
            d.wait_ge(floor_mm, 1)
            d.tensor_copy(floor_t[:, :], bank[7][0:GT, 0:G * INNER_C])
            link(d.tensor_copy(csum[:, :], bank[6][0:GT, 0:G * INNER_C]))
            link(magnitude(csum[:, :], csum[:, :]))
            link(d.tensor_tensor(csum[:, :], csum[:, :], floor_t[:, :], ALU.max))
            link(d.tensor_scalar(csum[:, :], csum[:, :], 1e-6, None, ALU.add))
            link(d.reciprocal(tiny[:, 0, :], csum[:, :]))
            link(d.tensor_tensor(tiny[:, 1, :], tiny[:, 0, :], tiny[:, 0, :], ALU.mult))
            d.tensor_tensor(tiny[:, 2, :], tiny[:, 1, :], mv[:, :, 1], ALU.mult).then_inc(hvar_done, 1)
            d.wait_ge(hstd_done, 1)
            link(d.reciprocal(tiny[:, 4, :], tiny[:, 3, :]))
            link(d.tensor_tensor(tiny[:, 5, :], tiny[:, 4, :], tiny[:, 0, :], ALU.mult))
            d.wait_ge(hraw_done, G)
            for g in range(G):
                for c in range(INNER_C):
                    n = g * INNER_C + c
                    ins = d.tensor_scalar(hraw[0:GT, g, c * DH:(c + 1) * DH], hraw[0:GT, g, c * DH:(c + 1) * DH],
                                          mv[:, n, 0:1], tiny[:, 5, n:n + 1], ALU.subtract, ALU.mult)
                ins.then_inc(hn_done, 1)
            d.wait_ge(wmean_mm, 1)
            link(d.tensor_scalar(wmean[:, :], bank[3][:, 0:2], 1.0 / (D * 1024), 1e-5, ALU.mult, ALU.max))
            d.reciprocal(wscale[:, :], wmean[:, :]).then_inc(wmean_done, 1)
            d.wait_ge(skip_done, INNER_C)
            for g in range(G):
                d.wait_ge(ht_mm, g + 1)
                tok = slice(g * GT, (g + 1) * GT)
                for c in range(INNER_C):
                    ins = d.scalar_tensor_tensor(out=hst[:, c, tok], in0=bank[g % 2][:, c * GT:(c + 1) * GT],
                                                 scalar=col("ln_w", c), in1=xc[:, c, tok], op0=ALU.mult, op1=ALU.add)
                link(ins)
                d.tensor_tensor(hst[:, :, tok], hst[:, :, tok], zs[:, :, tok], ALU.mult).then_inc(hst_done, 1)
            add_to_h(bank[0:4], down0_mm, 0)
            layer_norm(1)

            for hf in range(2):
                tok = slice(hf * HT, (hf + 1) * HT)
                d.wait_ge(xhi_done, hf + 1)
                d.tensor_tensor(xlo[:, :, tok], xn[:, :, tok], xhi[:, :, tok], ALU.subtract).then_inc(xlo_done, 1)
            d.wait_ge(aff_done, 1)
            for g in range(G):
                ins = d.max(top[:, g, :], aff[:, g, :])
            link(ins)
            for g in range(G):
                d.match_replace(rest[:, g, :], top[:, g, :], aff[:, g, :], 0.0)
            link(d.tensor_reduce(den[:, 0, :], top[:, :, :], AX, ALU.add))
            link(d.tensor_scalar(den[:, 1, :], den[:, 0, :], 1e-9, None, ALU.add))
            link(d.reciprocal(den[:, 2, :], den[:, 1, :]))
            link(d.tensor_tensor(rest[:, :, :], aff[:, :, :], rest[:, :, :], ALU.subtract))
            link(d.tensor_tensor(rest[:, :, :], rest[:, :, :], den[:, 2, :].unsqueeze(2).broadcast_to([GT, G, E]), ALU.mult))
            link(d.tensor_copy(mask_hl[:, :, 0:E], rest[:, :, :]))
            d.tensor_tensor(mask_hl[:, :, E:2 * E], rest[:, :, :], mask_hl[:, :, 0:E], ALU.subtract).then_inc(mask_done, 1)

            def hidden(up_bank, mask_bank, s, n):
                d.wait_ge(silu_done, n + 1)
                d.wait_ge(uproj_mm, n + 1)
                d.tensor_tensor(gu[:, s, :], sg[:, s, :], up_bank[:, 0:HT], ALU.mult).then_inc(gu_done, 1)
                d.wait_ge(gu_done, n + 1)
                if mask_bank is None:
                    d.tensor_copy(act[:, s, :], gu[:, s, :]).then_inc(act_done, 1)
                else:
                    d.wait_ge(mask_mm, n - 1)
                    d.tensor_tensor(act[:, s, :], gu[:, s, :], mask_bank[:, 0:HT], ALU.mult).then_inc(act_done, 1)
                    d.wait_ge(down_mm, n - 1)
                d.wait_ge(act_done, n + 1)
                d.tensor_copy(ahi[:, s, :], act[:, s, :]).then_inc(ahi_done, 1)
                d.wait_ge(ahi_done, n + 1)
                d.tensor_tensor(alo[:, s, :], act[:, s, :], ahi[:, s, :], ALU.subtract).then_inc(alo_done, 1)

            hidden(bank[5], None, 0, 0)
            hidden(bank[7], None, 1, 1)
            d.wait_ge(maskt_mm, 1)
            d.tensor_copy(maskT[:, :].rearrange("p (g t) -> p g t", g=G),
                          bank[4][:, :].bitcast(F16).rearrange("p (g t) -> p g t", g=G)[:, :, 0:GT]).then_inc(maskt_done, 1)

            def four_experts(it):
                for j in range(4):
                    for hf in range(2):
                        r = 3 * (2 * j + hf)
                        hidden(bank[4 + (r + 1) % 4], bank[4 + (r + 2) % 4], hf, it * 8 + (2 * j + hf + 2))

            with d.Fori(0, LOOPS) as it:
                four_experts(it)
            four_experts(LOOPS)
            for hf in range(2):
                d.wait_ge(down_mm, 2 * E + 1 + hf)
                for m in range(DC):
                    d.tensor_tensor(half(h, m, hf), half(h, m, hf), bank[2 * hf + m][:, 0:HT], ALU.add).then_inc(h_ready, 1)
            layer_norm(2)

            def low_part(n):
                hf, qk, m = n // 4, n // 2 % 2, n % 2
                hl = (q1_hl, k1_hl)[qk]
                d.wait_ge(rope_hi, n + 1)
                d.tensor_tensor(half(hl[:, 1], m, hf), rsum[:, n % 2, :], half(hl[:, 0], m, hf), ALU.subtract).then_inc(rope_done, 1)

            n = 0
            for hf in range(2):
                for qk in range(2):
                    for m in range(DC):
                        d.wait_ge(rope_mm, n + 1)
                        if n >= 2:
                            d.wait_ge(rope_done, n - 1)
                        for sw in range(2):
                            if n + sw == 0:
                                d.wait_ge(ld_bit, 64)
                            ins = d.scalar_tensor_tensor(
                                out=images(rt[:, n % 2, sw, :]), in0=images(bank[2 * (n % 2) + sw][:, 0:HT]),
                                scalar=col(("bq", "bq_swap", "bk", "bk_swap")[2 * qk + sw], m),
                                in1=ropew[:, sw, :].unsqueeze(1).broadcast_to([128, HB, POS]), op0=ALU.add, op1=ALU.mult)
                        ins.then_inc(rope_t, 1)
                        d.wait_ge(rope_t, n + 1)
                        d.tensor_tensor(rsum[:, n % 2, :], rt[:, n % 2, 0, :], rt[:, n % 2, 1, :], ALU.add).then_inc(rope_sum, 1)
                        if n >= 1:
                            low_part(n - 1)
                        n += 1
            low_part(7)
            d.wait_ge(rope_done, 8)
            d.memset(qm[:, :, :, :, H1C, :].rearrange("p w c b t -> p (w c b) t"), 0.0)
            d.memset(qm_flat[:, 2 * DC * B * QH * POS:2 * DC * B * QH * POS + SPILL], 0.0)
            for hh in range(H1C):
                for w in range(2):
                    ins = d.tensor_scalar(qm[:, w, :, :, hh, :].rearrange("p c b t -> p (c b) t"),
                                          q1_hl[:, w, :, :].rearrange("p c (b t) -> p (c b) t", t=POS),
                                          head_col[:, hh:hh + 1], None, ALU.mult)
                ins.then_inc(qm_done, 1)
            U = 3 * POS

            def scores_of(n):
                return bank[n % 2][0:U, 0:12 * POS].rearrange("p (n t) -> p n t", t=POS)

            def subtract_max(n):
                d.wait_ge(sc_mm, n + 1)
                link(d.tensor_reduce(smx[0:U, n % 2, 0, :], scores_of(n), AX, ALU.max))
                d.tensor_tensor(pr[0:U, n % 2, :, :], scores_of(n),
                                smx[0:U, n % 2, 0, :].unsqueeze(2).broadcast_to([U, 12, POS]), ALU.subtract).then_inc(sc_sub, 1)

            def v1_low(n):
                d.wait_ge(v1hi_done, n + 1)
                d.tensor_tensor(v1[0:POS, 1, 2 * n:2 * n + 2, :], bank[4 + n % 2][0:POS, :].rearrange("p (b m) -> p b m", b=2),
                                v1[0:POS, 0, 2 * n:2 * n + 2, :], ALU.subtract).then_inc(v1lo_done, 1)

            for n in range(G):
                v1_low(n)
            subtract_max(0)
            subtract_max(1)
            for n in range(G):
                d.wait_ge(sc_exp, n + 1)
                e = pr[0:U, n % 2, :, :]
                link(d.tensor_reduce(smx[0:U, n % 2, 1, :], e, AX, ALU.add))
                link(d.reciprocal(smx[0:U, n % 2, 2, :], smx[0:U, n % 2, 1, :]))
                link(d.tensor_tensor(e, e, smx[0:U, n % 2, 2, :].unsqueeze(2).broadcast_to([U, 12, POS]), ALU.mult))
                if n >= 2:
                    d.wait_ge(pt_mm, 2 * (n - 1))
                link(d.tensor_copy(ph[0:U, n % 2, :, 0, :], e))
                d.tensor_tensor(ph[0:U, n % 2, :, 1, :], e, ph[0:U, n % 2, :, 0, :], ALU.subtract).then_inc(p_done, 1)
                if n + 2 < G:
                    d.wait_ge(p_done, n + 1)
                    subtract_max(n + 2)
            add_to_h(bank[4:8], wo_mm, 0)
            layer_norm(3)

            def token_scales(n):
                for i in range(2):
                    if i == 0:
                        d.wait_ge(amaxt_mm, n + 1)
                    ins = d.tensor_reduce(tmx[:, 4 * i:4 * i + 4], bank[4 + i][0:GT, :].rearrange("p (g f) -> p g f", g=4), AX, ALU.max)
                link(ins)
                link(d.tensor_scalar(tmx[:, :], tmx[:, :], 1e-5, None, ALU.max))
                link(d.reciprocal(tsc[:, 0, :], tmx[:, :]))
                d.tensor_scalar(tsc[:, 1, :], tmx[:, :], 1.0 / 127.0, None, ALU.mult)
                d.tensor_scalar(tsc[:, 0, :], tsc[:, 0, :], 127.0, None, ALU.mult).then_inc(tsc_done, 1)
                d.wait_ge(tsct_mm, n + 1)
                d.tensor_copy(tscT[:, :], bank[6][0:2 * G, 0:GT]).then_inc(tsct_done, 1)

            def inverse_scales(n):
                d.wait_ge(bc_mm, 2 * n + 2)
                for i in range(2):
                    ins = d.tensor_scalar(binv[:, i * HT:(i + 1) * HT], bank[6 + i][:, 0:HT], wmean[:, n:n + 1], None, ALU.mult)
                ins.then_inc(bc_done, 1)

            def quantize(dst, src, hf, done, by):
                n = src.shape[1]
                link(d.tensor_tensor(src, src, bank[4 + hf][:, 0:HT].unsqueeze(1).broadcast_to([128, n, HT]), ALU.mult))
                link(d.tensor_scalar(src, src, 127.0, -128.0, ALU.min, ALU.max))
                d.tensor_scalar(dst, src, MAGIC, MAGIC, ALU.add, ALU.subtract).then_inc(done, by)

            d.wait_ge(xn_ready, 8)
            magnitude(habs[:, 0, :], xn[:, 0, :])
            link(magnitude(habs[:, 1, :], xn[:, 1, :]))
            d.tensor_tensor(amax, habs[:, 0, :], habs[:, 1, :], ALU.max).then_inc(amax_done, 1)
            token_scales(0)
            d.wait_ge(bc_mm, 1)
            for hf in range(2):
                tok = slice(hf * HT, (hf + 1) * HT)
                quantize(x4q[:, :, tok], xn[:, :, tok], hf, xq_done, 2)
            inverse_scales(0)
            d.wait_ge(bc_done, 1)
            for n in range(16):
                hf, c = n // 8, n % 8
                d.wait_ge(w1_mm, n + 1)
                d.tensor_tensor(half(hid, c, hf), bank[n % 4][:, 0:HT], binv[:, hf * HT:(hf + 1) * HT], ALU.mult).then_inc(hid_done, 1)
            for c in range(FC):
                d.wait_ge(fconv_first, c + 1)
                for k in (0, 2):
                    to, of = (slice(1, POS), slice(0, POS - 1)) if k == 0 else (slice(0, POS - 1), slice(1, POS))
                    into = images(h2[:, c, :])[:, :, to]
                    ins = d.scalar_tensor_tensor(out=into, in0=images(hid[:, c, :])[:, :, of],
                                                 scalar=col("ffn_conv_w", 3 * c + k), in1=into,
                                                 op0=ALU.mult, op1=ALU.add)
                    if k == 0:
                        link(ins)
                ins.then_inc(fconv_done, 1)
            d.wait_ge(habs_done, 2)
            link(d.tensor_tensor(amax, habs[:, 0, :], habs[:, 1, :], ALU.max))
            for c in range(2, FC):
                d.wait_ge(habs_done, c + 1)
                ins = d.tensor_tensor(amax, amax, habs[:, c, :], ALU.max)
                if c < FC - 1:
                    link(ins)
            ins.then_inc(amax_done, 1)
            token_scales(1)
            d.wait_ge(bc_mm, 3)
            for hf in range(2):
                tok = slice(hf * HT, (hf + 1) * HT)
                for c in (0, 4):
                    quantize(h2q[:, c:c + 4, tok], h2[:, c:c + 4, tok], hf, xq_done, 1)
            inverse_scales(1)
            d.wait_ge(bc_done, 2)
            for hf in range(2):
                for m in range(DC):
                    tok = slice(hf * HT, (hf + 1) * HT)
                    d.wait_ge(w2_mm, 2 * hf + m + 1)
                    link(d.tensor_tensor(half(sq, m, hf), bank[2 * hf + m][:, 0:HT], binv[:, tok], ALU.mult))
                    d.tensor_tensor(half(h, m, hf), half(h, m, hf), half(sq, m, hf), ALU.add).then_inc(h_ready, 1)


def _kmajor(w):
    k, m = w.shape
    return w.reshape(k // 128, 128, m).transpose(1, 0, 2)


def _columns(v):
    return v.reshape(-1, 128).T


def _rope_tables():
    import numpy as np
    freqs = np.float32(10000.0) ** (-np.arange(0, HD1, 2).astype(np.float32) / np.float32(HD1))
    ang = np.arange(POS, dtype=np.float32)[None, :] * freqs[:, None].astype(np.float32)
    f = (np.arange(128) % HD1) // 2
    sign = np.where(np.arange(128) % 2 == 0, -1.0, 1.0).astype(np.float32)[:, None]
    return np.stack([np.cos(ang)[f], np.sin(ang)[f] * sign], axis=1).astype(np.float32)


def _layouts(i):
    import numpy as np
    x = i["x"].reshape(B, 3, 6, 16, 6, 16).transpose(1, 3, 5, 0, 2, 4).reshape(TOK_K * 128, B * PATCHES)
    swap = np.arange(D) ^ 1
    gate_b = np.zeros((128, 1), np.float32)
    gate_b[0:4, 0], gate_b[32:36, 0] = i["L0_attn_b_ig"], i["L0_attn_b_fg"]
    w_gates = np.zeros((1536, 64), np.float32)
    w_gates[:, 0:4], w_gates[:, 32:36] = i["L0_attn_w_ig"].T, i["L0_attn_w_fg"].T
    cw = i["L0_attn_conv_w"].reshape(INNER_C, 128, CONV).transpose(1, 0, 2).reshape(128, -1)
    fw = i["L1_ffn_conv_w"].reshape(FC, 128, 3).transpose(1, 0, 2).reshape(128, -1)
    cols = np.concatenate([
        _columns(i["L0_tok_b"]), _columns(i["L0_tok_cls_token"].reshape(-1)), cw, _columns(i["L0_attn_conv_b"]),
        _columns(i["L0_attn_ln_w"].reshape(-1)), _columns(i["L0_attn_skip"]), gate_b,
        _columns(i["L1_attn_bq"]), _columns(i["L1_attn_bq"][swap]), _columns(i["L1_attn_bk"]),
        _columns(i["L1_attn_bk"][swap]), _columns(i["L1_attn_bv"]), fw, _columns(i["L1_ffn_conv_b"])], axis=1)
    heads = [i[f"L0_attn_w_{n}"] for n in "qkv"]
    blocks = np.concatenate([_kmajor(w.transpose(0, 2, 1).reshape(512, 4)) for w in heads], axis=1)
    blocks_t = np.concatenate([_kmajor(w.reshape(512, 4)) for w in heads], axis=1)

    def expert(gate, up, down):
        n = gate.shape[0]
        rows = [w.reshape(n, 2, 128, 128).transpose(0, 2, 1, 3).reshape(n, 128, 256) for w in (gate, up)]
        return np.concatenate([*rows, down], axis=2)

    shared = expert(*(i[f"L0_ffn_shared_{n}_w"][None] for n in ("gate", "up", "down")))[0]
    experts = expert(*(i[f"L0_ffn_expert_{n}_k"] for n in ("gate", "up", "down"))).transpose(1, 0, 2)
    wq, wk = i["L1_attn_Wq"], i["L1_attn_Wk"]
    l1_w = np.stack([_kmajor(w.T) for w in (wq, wq[swap], wk, wk[swap], i["L1_attn_Wv"], i["L1_attn_Wo"])], axis=1)
    return {
        "patches": _kmajor(x), "tok_w": _kmajor(i["L0_tok_W"].T), "pos": _kmajor(i["L0_tok_pos_enc"][0].T),
        "cols": cols, "w_up": _kmajor(i["L0_attn_w_up"].T), "blocks": blocks, "blocks_t": blocks_t,
        "w_gates": _kmajor(w_gates), "w_down": _kmajor(i["L0_attn_w_down"].T),
        "w_router": _kmajor(i["L0_ffn_router_w"]), "w_shared": shared, "w_experts": experts, "l1_w": l1_w,
        "rope": _rope_tables(), "ffn_w1": _kmajor(i["L1_ffn_w1"].T), "ffn_w2": _kmajor(i["L1_ffn_w2"].T),
    }


def kernel(**inputs):
    import numpy as np
    import concourse.bacc as bacc
    from concourse.bass_utils import run_bass_kernel_spmd

    nc = bacc.Bacc("TRN2", target_bir_lowering=False, num_devices=1)
    arrays = {k: np.ascontiguousarray(v) for k, v in _layouts({k: np.asarray(v) for k, v in inputs.items()}).items()}
    args = {k: nc.dram_tensor(k, v.shape, mybir.dt.from_np(v.dtype), kind="ExternalInput").ap() for k, v in arrays.items()}
    out = nc.dram_tensor("out", (128, DC, T), F32, kind="ExternalOutput").ap()
    vit_tower(nc, out=out, **args)
    r = run_bass_kernel_spmd(nc, [arrays], core_ids=[0])
    return r.results[0]["out"].transpose(2, 1, 0).reshape(B, POS, D)
```

```python
from contextlib import ExitStack

import concourse.bass as bass
from concourse import mybir

F32 = mybir.dt.float32
F16 = mybir.dt.float16
BF16 = mybir.dt.bfloat16
ALU = mybir.AluOpType
ACT = mybir.ActivationFunctionType
AX = mybir.AxisListType.X

B, PATCHES, POS = 16, 36, 37
T = B * POS
HB = B // 2
HT = HB * POS
G, GT = B // 2, 2 * POS
D, DC = 256, 2
TOK_K = 6
INNER_C = 4
DH = 128
CONV = 4
E = 64
WE = 768
H1, HD1 = 16, 16
H1C = 8
SPILL = 64
PTW = 112
REP = 3
UK = REP * POS
QH = 9
FC = 8
PARTS = ((0, 0), (0, 1), (1, 0))
TAP_ORDER, POOL_TAPS = (1, 2, 0, 4, 5, 3, 6, 7), (0, 3)
MAGIC = 1.5 * 2.0 ** 23
NEG = -1.0e30
QK_SCALE = float(DH) ** -0.5

COLS = {}
_n = 0
for _name, _w in (("tok_b", DC), ("cls", DC), ("conv_w", INNER_C * CONV), ("conv_b", INNER_C),
                  ("ln_w", INNER_C), ("skip", INNER_C), ("gate_b", 1), ("bq", DC), ("bq_swap", DC),
                  ("bk", DC), ("bk_swap", DC), ("bv", DC), ("ffn_conv_w", FC * 3), ("ffn_conv_b", FC)):
    COLS[_name] = (_n, _n + _w)
    _n += _w
NCOLS = _n


def vit_tower(nc: bass.Bass, patches, tok_w, pos, cols, w_up, blocks, blocks_t, w_gates, w_down,
              w_router, w_shared, w_experts, l1_w, rope, ffn_w1, ffn_w2, out):
    with ExitStack() as ctx:
        def sb(name, shape, dt=F32):
            return ctx.enter_context(nc.sbuf_tensor(name, shape, dt))

        def sem(name):
            return ctx.enter_context(nc.semaphore(name))

        bank = [ctx.enter_context(nc.psum_tensor(f"bank{i}", [128, 512], F32)) for i in range(8)]

        colp = sb("colp", [128, NCOLS])
        posw = sb("posw", [128, DC, POS])
        blk = sb("blk", [128, 12, 4])
        blk_t = sb("blk_t", [128, 12, 4])
        wg = sb("wg", [128, 12, 64])
        wup = sb("wup", [128, DC, 1024])
        wdn = sb("wdn", [128, INNER_C, D])
        wrt = sb("wrt", [128, DC, E])
        l1w = sb("l1w", [128, 6, DC, D])
        ropew = sb("ropew", [128, 2, POS])
        ident = sb("ident", [128, 128])
        zero_w = sb("zero_w", [128, 128], F16)
        ident_h = sb("ident_h", [128, 128], F16)
        mean_w = sb("mean_w", [128, 128])
        ones = sb("ones", [128, 128])
        in_block = sb("in_block", [128, 32])
        head_col = sb("head_col", [128, H1C])
        expert_sel = sb("expert_sel", [128, E], F16)
        causal = sb("causal", [GT, INNER_C, GT], BF16)
        restart_mul = sb("restart_mul", [INNER_C, B, POS])
        restart_add = sb("restart_add", [INNER_C, B, POS])
        magic_col = sb("magic_col", [128, 1])
        minus_magic = sb("minus_magic", [128, 1])
        eps_col = sb("eps_col", [128, 1])
        h = sb("h", [128, DC, T])
        xn = sb("xn", [128, DC, T])
        sq = sb("sq", [128, DC, T])
        var8 = sb("var8", [GT, 2, G])
        rstd = sb("rstd", [GT, G, GT])
        root_warm = sb("root_warm", [128, 6])
        posb = sb("posb", [128, DC, POS])
        cls0 = sb("cls0", [128, DC])
        w1q = sb("w1q", [128, DC, 1024], BF16)
        w2q = sb("w2q", [128, FC, D], BF16)
        wabs = sb("wabs", [128, 2])
        wscale = sb("wscale", [128, 2])
        wmean = sb("wmean", [128, 2])

        arena = sb("arena", [128, 24064])
        where = [0]

        def take(n, start=None):
            if start is not None:
                where[0] = start
            a = where[0]
            where[0] += n
            assert where[0] <= 24064, where
            return arena[:, a:a + n]

        xm = take(INNER_C * T, 0).rearrange("p (c t) -> p c t", c=INNER_C)
        zs = take(INNER_C * T).rearrange("p (c t) -> p c t", c=INNER_C)
        xc = take(INNER_C * T).rearrange("p (c t) -> p c t", c=INNER_C)
        bd = take(12 * 128).rearrange("p (n m) -> p n m", n=12)
        bd_t = take(12 * 128).rearrange("p (n m) -> p n m", n=12)
        hst = take(INNER_C * T).rearrange("p (c t) -> p c t", c=INNER_C)
        q_hl = hst.rearrange("p c t -> p (c t)").bitcast(F16)
        up_hl = q_hl[:, 0:4 * 1024].rearrange("p (w k m) -> p w k m", w=2, k=DC)
        EXPERTS_AT = where[0]
        k_hl = take(INNER_C * T + SPILL // 2).bitcast(F16)
        xu_hl = k_hl[:, 0:2 * DC * T].rearrange("p (w c t) -> p w c t", w=2, c=DC)
        cacc = k_hl.bitcast(F32)[:, 0:INNER_C * T].rearrange("p (c t) -> p c t", c=INNER_C)
        v = take(G * 512).bitcast(F16).rearrange("p (w g m) -> p w g m", w=2, g=G)
        hraw = take(G * 512).rearrange("p (g m) -> p g m", g=G)
        lf = hraw.rearrange("p g m -> p (g m)")[0:INNER_C, 0:4 * T].rearrange("p (n t) -> p n t", n=4)
        conv_tap = hraw.rearrange("p g m -> p (g m)")[:, 4 * T:5 * T]
        mid = lf[:, 0, :].bitcast(BF16).rearrange("p (n t) -> p n t", n=2)
        patch_sb = arena[:, where[0] - G * 1024:where[0] - G * 1024 + TOK_K * B * PATCHES].rearrange(
            "p (k t) -> p k t", k=TOK_K)
        tokw = arena[:, where[0] - G * 1024 + TOK_K * B * PATCHES:
                     where[0] - G * 1024 + TOK_K * B * PATCHES + TOK_K * D].rearrange("p (k m) -> p k m", k=TOK_K)
        wraw1 = sb("wraw1", [128, DC, 1024])
        wraw2 = wup[:, :, :].rearrange("p a b -> p (a b)").rearrange("p (k m) -> p k m", k=FC)
        whi = take(2 * WE, EXPERTS_AT).bitcast(F16).rearrange("p (s m) -> p s m", s=4)
        wlo = take(2 * WE).bitcast(F16).rearrange("p (s m) -> p s m", s=4)
        aff = take(G * E).rearrange("p (g e) -> p g e", g=G)[0:GT]
        rest = take(G * E).rearrange("p (g e) -> p g e", g=G)[0:GT]
        mask_hl = take(G * E).bitcast(F16).rearrange("p (g e) -> p g e", g=G)[0:GT]
        maskT = take(T // 2).bitcast(F16)
        xhi = take(DC * T // 2).bitcast(F16).rearrange("p (c t) -> p c t", c=DC)
        xlo = take(DC * T // 2).bitcast(F16).rearrange("p (c t) -> p c t", c=DC)
        sg = take(2 * HT).rearrange("p (s t) -> p s t", s=2)
        gu = take(2 * HT).rearrange("p (s t) -> p s t", s=2)
        act = take(2 * HT).rearrange("p (s t) -> p s t", s=2)
        ahi = take(HT).bitcast(F16).rearrange("p (s t) -> p s t", s=2)
        alo = take(HT).bitcast(F16).rearrange("p (s t) -> p s t", s=2)
        otok = take(B * D, 0).rearrange("p (b m) -> p b m", b=B)
        rsum = take(2 * HT, 0).rearrange("p (s t) -> p s t", s=2)
        rt = take(4 * HT).rearrange("p (s c t) -> p s c t", s=2, c=2)
        xd_flat = take(REP * DC * T + SPILL // 2)
        q1_hl = take(DC * T)
        oT = q1_hl.rearrange("p (c t) -> p c t", c=DC)
        q1_hl = q1_hl.bitcast(F16).rearrange("p (w c t) -> p w c t", w=2, c=DC)
        xd_flat = xd_flat.bitcast(F16)
        xdup = xd_flat[:, 0:2 * REP * DC * T].rearrange("p (w c b i t) -> p w c b i t", w=2, c=DC, b=B, i=REP)
        k1_hl = take(DC * T).bitcast(F16).rearrange("p (w c t) -> p w c t", w=2, c=DC)
        qm_flat = take(DC * B * QH * POS + SPILL // 2).bitcast(F16)
        qm = qm_flat[:, 0:2 * DC * B * QH * POS].rearrange("p (w c b h t) -> p w c b h t", w=2, c=DC, b=B, h=QH)
        v1 = take(B * D // 2).bitcast(F16).rearrange("p (b m) -> p b m", b=B)
        pr = take(2 * 2 * 6 * POS).rearrange("p (s n t) -> p s n t", s=2, n=12)
        ph = take(2 * 6 * REP * POS).bitcast(F16).rearrange("p (s n w t) -> p s n w t", s=2, n=12, w=REP)
        pT = take(6 * PTW).bitcast(F16).rearrange("p (s m) -> p s m", s=2)
        l1hi, l1lo = (w[:, :, :].rearrange("p a b -> p (a b)").bitcast(F16)[:, 0:6 * DC * D].rearrange(
            "p (n k m) -> p n k m", n=6, k=DC) for w in (wraw1, wraw2))
        hid = take(FC * T, 0).rearrange("p (c t) -> p c t", c=FC)
        h2 = take(FC * T).rearrange("p (c t) -> p c t", c=FC)
        h2q = take(FC * T // 2).bitcast(BF16).rearrange("p (c t) -> p c t", c=FC)
        x4q = take(DC * T // 2).bitcast(BF16).rearrange("p (c t) -> p c t", c=DC)
        habs = take(FC * T).rearrange("p (c t) -> p c t", c=FC)
        amax = take(T)
        tapped = take(T)
        bscale = take(T)
        binv = take(T)
        spread = take(2 * T).rearrange("p (n g t) -> p n g t", n=2, g=G)[0:2 * G]
        gts = sb("gts", [64, T])
        arow = sb("arow", [INNER_C, T])
        rrow = sb("rrow", [INNER_C, 2, T])
        a3 = sb("a3", [96, T + SPILL], BF16)
        m3 = sb("m3", [96, T], BF16)
        sel3 = sb("sel3", [96, INNER_C, 128], BF16)
        ident_b = sb("ident_b", [GT, 128], BF16)
        ones_h = sb("ones_h", [128, 1], F16)
        mrow = sb("mrow", [INNER_C, T])
        lcum = sb("lcum", [INNER_C, T])
        nrow = sb("nrow", [INNER_C, T])
        geff = sb("geff", [128, 8, 64])
        dmat = sb("dmat", [GT, 2, INNER_C, GT])
        cmat = sb("cmat", [GT, 2, INNER_C * GT])
        c_hl = sb("c_hl", [GT, 2, 2, INNER_C * GT + SPILL], F16)
        floor_t = sb("floor_t", [GT, G * INNER_C])
        csum = sb("csum", [GT, G * INNER_C])
        stat = sb("stat", [GT, G * INNER_C, 6])
        mv = sb("mv", [GT, G * INNER_C, 2])
        tiny = sb("tiny", [GT, 6, G * INNER_C])
        top = sb("top", [GT, G, 8])
        den = sb("den", [GT, 3, G])
        stage = sb("stage", [128, 4, WE])
        shared_w = wg[:, :, :].rearrange("p a b -> p (a b)")
        smx = sb("smx", [128, 2, 3, 12])
        tmx = sb("tmx", [GT, G])
        tsc = sb("tsc", [GT, 2, G])

        def col(name, i=0, rows=slice(0, 128)):
            a = COLS[name][0] + i
            return colp[rows, a:a + 1]

        ld_patch = [sem(f"ld_patch{i}") for i in range(3)]
        ld_first = sem("ld_first")
        ld_up = sem("ld_up")
        up_hi_done, up_lo_done, xuhi_done, xulo_done = sem("up_hi_done"), sem("up_lo_done"), sem("xuhi_done"), sem("xulo_done")
        ld_attn = sem("ld_attn")
        ld_ffn = sem("ld_ffn")
        ld_bit = sem("ld_bit")
        ld_w2 = sem("ld_w2")
        ld_stage = [sem("ld_stage_a"), sem("ld_stage_b")]
        consts = sem("consts")
        pool_step = sem("pool_step")
        vec_step = sem("vec_step")
        act_step = sem("act_step")
        wscaled, wmean_done, wq_done = sem("wscaled"), sem("wmean_done"), sem("wq_done")
        wabs_done = sem("wabs_done")
        wmean_mm = sem("wmean_mm")
        bd_done = sem("bd_done")
        tok_mm = sem("tok_mm")
        h_ready = sem("h_ready")
        ln_mean, ln_cent, ln_sq = sem("ln_mean"), sem("ln_cent"), sem("ln_sq")
        ln_diag, ln_rstd = sem("ln_diag"), sem("ln_rstd")
        ln_var, ln_std, xn_ready = sem("ln_var"), sem("ln_std"), sem("xn_ready")
        geff_mm, geff_done = sem("geff_mm"), sem("geff_done")
        up_mm, xm_done, zs_done = sem("up_mm"), sem("xm_done"), sem("zs_done")
        conv_first, conv_done, xc_ready = sem("conv_first"), sem("conv_done"), sem("xc_ready")
        qk_mm, qkhi_done, qlo_done, klo_done = sem("qk_mm"), sem("qkhi_done"), sem("qlo_done"), sem("klo_done")
        gates_mm, gts_done = sem("gates_mm"), sem("gts_done")
        v_mm, v_done, vlo_done = sem("v_mm"), sem("v_done"), sem("vlo_done")
        absf_done, lnf_done, arow_done = sem("absf_done"), sem("lnf_done"), sem("arow_done")
        hcoef_done, hnv_done = sem("hcoef_done"), sem("hnv_done")
        arow_in, mrow_in, gate_hi, gate_rest, gate_mid, mid_placed = (
            sem("arow_in"), sem("mrow_in"), sem("gate_hi"), sem("gate_rest"), sem("gate_mid"), sem("mid_placed"))
        nrow_in, nrow_done, floor_mm = sem("nrow_in"), sem("nrow_done"), sem("floor_mm")
        s_mm, e_mm, d_done, c_done, c_high, c_split = (
            sem("s_mm"), sem("e_mm"), sem("d_done"), sem("c_done"), sem("c_high"), sem("c_split"))
        hv_mm, hraw_done, hstat_done = sem("hv_mm"), sem("hraw_done"), sem("hstat_done")
        hvar_done, hstd_done, hn_done = sem("hvar_done"), sem("hstd_done"), sem("hn_done")
        skip_done, ht_mm, hst_done, down0_mm = sem("skip_done"), sem("ht_mm"), sem("hst_done"), sem("down0_mm")
        route_mm, aff_done, mask_done, maskt_mm, maskt_done = (
            sem("route_mm"), sem("aff_done"), sem("mask_done"), sem("maskt_mm"), sem("maskt_done"))
        xhi_done, xlo_done = sem("xhi_done"), sem("xlo_done")
        whi_done, wlo_done = sem("whi_done"), sem("wlo_done")
        gate_mm, uproj_mm, mask_mm, down_mm = sem("gate_mm"), sem("uproj_mm"), sem("mask_mm"), sem("down_mm")
        silu_done, gu_done, act_done, alo_done = (
            sem("silu_done"), sem("gu_done"), sem("act_done"), sem("alo_done"))
        ahi_done = sem("ahi_done")
        rope_mm, rope_t, rope_sum, rope_hi, rope_done, qm_done = (
            sem("rope_mm"), sem("rope_t"), sem("rope_sum"), sem("rope_hi"), sem("rope_done"), sem("qm_done"))
        vb_mm, v1hi_done, v1lo_done = sem("vb_mm"), sem("v1hi_done"), sem("v1lo_done")
        l1hi_done, l1lo_done, xdhi_done, xdlo_done, xdup_done, qm_pool = (
            sem("l1hi_done"), sem("l1lo_done"), sem("xdhi_done"), sem("xdlo_done"), sem("xdup_done"), sem("qm_pool"))
        max_done, conv_pool = sem("max_done"), sem("conv_pool")
        xdlast_done, p_again = sem("xdlast_done"), sem("p_again")
        quot_done, p_high, qm_act = sem("quot_done"), sem("p_high"), sem("qm_act")
        sc_mm, sc_sub, sc_exp, p_done = sem("sc_mm"), sem("sc_sub"), sem("sc_exp"), sem("p_done")
        pt_mm, pt_done, pv_mm, ot_done = sem("pt_mm"), sem("pt_done"), sem("pv_mm"), sem("ot_done")
        ott_mm, oT_done, wo_mm = sem("ott_mm"), sem("oT_done"), sem("wo_mm")
        amax_done, amaxt_mm, tsc_done, tsct_mm, tsct_done, bc_mm, bc_done = (
            sem("amax_done"), sem("amaxt_mm"), sem("tsc_done"), sem("tsct_mm"), sem("tsct_done"),
            sem("bc_mm"), sem("bc_done"))
        xq_done = sem("xq_done")
        w1_mm, hid_done, fconv_first, fconv_done, h2_done, habs_done, w2_mm = (
            sem("w1_mm"), sem("hid_done"), sem("fconv_first"), sem("fconv_done"), sem("h2_done"), sem("habs_done"), sem("w2_mm"))
        fconv_pool, clipped, rounded, h2q_done = sem("fconv_pool"), sem("clipped"), sem("rounded"), sem("h2q_done")
        last_rounded = sem("last_rounded")
        stored = sem("stored")

        block = ctx.enter_context(nc.Block())

        def half(x, c, hf):
            return x[:, c, hf * HT:(hf + 1) * HT]

        def images(ap):
            return ap.rearrange("p (b t) -> p b t", t=POS)

        IM = (slice(0, HB + 1), slice(HB + 1, B))

        def queries_at(x, part, head=None):
            if head is None:
                return x.rearrange("p c (b t) -> p c b t", t=POS)[:, :, IM[part], :]
            return x[:, :, IM[part], head, :]

        LOOPS = E // 4 - 1

        @block.sync
        def _(sp):
            for i in range(3):
                k = slice(2 * i, 2 * i + 2)
                sp.dma_start(tokw[:, k, :], tok_w[:, k, :]).then_inc(ld_patch[i], 16)
                sp.dma_start(patch_sb[:, k, :], patches[:, k, :]).then_inc(ld_patch[i], 16)
            sp.dma_start(posw[:, :, :], pos).then_inc(ld_first, 16)
            sp.dma_start(colp[:, :], cols).then_inc(ld_first, 16)
            sp.dma_start(wup[:, :, :], w_up).then_inc(ld_up, 16)
            for dst, src in ((blk[:, :, :], blocks), (blk_t[:, :, :], blocks_t), (wg[:, :, :], w_gates),
                             (wdn[:, :, :], w_down)):
                sp.dma_start(dst, src).then_inc(ld_attn, 16)
            sp.dma_start(wrt[:, :, :], w_router).then_inc(ld_ffn, 16)
            for s in range(2):
                sp.dma_start(stage[:, 2 * s:2 * s + 2, :], w_experts[:, 2 * s:2 * s + 2, :]).then_inc(ld_stage[s], 16)
            for dst, src in ((wraw1[:, :, :], ffn_w1), (l1w[:, :, :, :], l1_w), (ropew[:, :, :], rope)):
                sp.dma_start(dst, src).then_inc(ld_bit, 16)
            sp.wait_ge(up_mm, 16)
            sp.dma_start(wraw2, ffn_w2).then_inc(ld_w2, 16)
            sp.wait_ge(geff_mm, 1)
            sp.dma_start(shared_w, w_shared).then_inc(ld_ffn, 16)
            with sp.Fori(0, LOOPS) as it:
                for s in range(2):
                    sp.wait_ge(wlo_done, it * 4 + 2 * s + 3)
                    sp.dma_start(stage[:, 2 * s:2 * s + 2, :],
                                 w_experts[:, bass.ds(it * 4 + 4 + 2 * s, 2), :]).then_inc(ld_stage[s], 16)
            for hf in range(2):
                sp.wait_ge(h_ready, 16 + 2 * hf + 2)
                tok = slice(hf * HT, (hf + 1) * HT)
                sp.dma_start(out[:, :, tok], h[:, :, tok]).then_inc(stored, 16)
            sp.wait_ge(stored, 32)

        @block.gpsimd
        def _(pool):
            steps = [0]

            def link(ins):
                steps[0] += 1
                ins.then_inc(pool_step, 1)
                pool.wait_ge(pool_step, steps[0])

            def select(x, compare, fill, base, pattern, by, source=None):
                return pool.affine_select(out=x, in_=x if source is None else source, compare_op=compare, fill=fill,
                                          base=base, pattern=pattern, channel_multiplier=by)

            pool.memset(mean_w[:, :], 1.0 / D)
            pool.memset(eps_col[:, :], 1e-5)
            pool.memset(magic_col[:, :], MAGIC)
            pool.memset(minus_magic[:, :], -MAGIC)
            pool.memset(zero_w[:, :], 0.0)
            link(pool.memset(ones[:, :], 1.0))
            select(ident[:, :], ALU.is_equal, 0.0, 0, [[-1, 128]], 1, ones[:, :])
            link(select(in_block[:, :], ALU.is_ge, 0.0, 0, [[-4, 32]], 1, ones[:, 0:32]))
            select(in_block[:, :], ALU.is_ge, 0.0, 3, [[4, 32]], -1).then_inc(consts, 1)
            link(select(head_col[:, :], ALU.is_ge, 0.0, 0, [[-HD1, H1C]], 1, ones[:, 0:H1C]))
            select(head_col[:, :], ALU.is_ge, 0.0, HD1 - 1, [[HD1, H1C]], -1)
            pool.tensor_copy(ident_h[:, :], ident[:, :])
            pool.tensor_tensor(expert_sel[:, :], ident[:, 0:E], ident[:, E:2 * E], ALU.add)
            link(pool.memset(ones_h[:, :], 1.0))
            link(pool.memset(sel3[:, :, :], 0.0))
            for part in range(3):
                link(select(sel3[:, :, :], ALU.not_equal, 1.0, -32 * part, [[-1, INNER_C], [0, 128]], 1))
            link(pool.memset(a3[:, :], 0.0))
            link(pool.memset(m3[:, :], 0.0))
            pool.tensor_copy(ident_b[:, :], ident[0:GT, :])
            pool.memset(c_hl[:, :, :, :], 0.0)
            link(pool.memset(causal[:, :, :], 0.0))
            link(select(causal[:, :, :], ALU.is_ge, NEG, 0, [[0, INNER_C], [1, GT]], -1))
            link(select(causal[:, :, POS:GT], ALU.is_ge, NEG, -POS, [[0, INNER_C], [0, POS]], 1))
            pool.memset(restart_mul[:, :, :], 1.0)
            link(pool.memset(restart_add[:, :, :], 0.0))
            pool.memset(restart_mul[:, :, 0:1], 0.0)
            link(pool.memset(restart_add[:, :, 0:1], NEG))
            pool.drain().then_inc(consts, 2)

            pool.wait_ge(up_hi_done, 1)
            pool.tensor_tensor(up_hl[:, 1, :, :], wup[:, :, :], up_hl[:, 0, :, :], ALU.subtract).then_inc(up_lo_done, 1)

            pool.wait_ge(ld_attn, 64)
            for dst, src in ((bd_t, blk_t), (bd, blk)):
                pool.tensor_tensor(dst.rearrange("p n (a b) -> p n a b", b=4),
                                   src[:, :, :].unsqueeze(2).broadcast_to([128, 12, 32, 4]),
                                   in_block[:, :].unsqueeze(1).unsqueeze(3).broadcast_to([128, 12, 32, 4]),
                                   ALU.mult).then_inc(bd_done, 1)

            c = INNER_C - 1
            pool.wait_ge(tok_mm, 4)
            pool.wait_ge(conv_first, c + 1)
            for back in range(1, CONV):
                into, tap = images(cacc[:, c, :])[:, :, back:POS], images(conv_tap)[:, :, 0:POS - back]
                link(pool.tensor_scalar(tap, images(xm[:, c, :])[:, :, 0:POS - back],
                                        col("conv_w", c * CONV + CONV - 1 - back), None, ALU.mult))
                ins = pool.tensor_tensor(into, into, tap, ALU.add)
                if back < CONV - 1:
                    link(ins)
            ins.then_inc(conv_pool, 1)

            pool.wait_ge(zs_done, 8)
            pool.wait_ge(qk_mm, 16)
            pool.wait_ge(gates_mm, 2)
            for c in range(INNER_C):
                link(pool.tensor_scalar(xc[:, c, :], xc[:, c, :], col("skip", c), None, ALU.mult))
                link(pool.tensor_tensor(xc[:, c, :], xc[:, c, :], zs[:, c, :], ALU.mult))
                pool.tensor_scalar(zs[:, c, :], zs[:, c, :], col("ln_w", c), None, ALU.mult).then_inc(skip_done, 1)

            for i, (raw, ints) in enumerate(((wraw1, w1q), (wraw2, w2q))):
                pool.wait_ge(wscaled, 4 * i + 4)
                link(pool.tensor_scalar(raw[:, :, :], raw[:, :, :], MAGIC, 1.0, ALU.subtract, ALU.min))
                pool.tensor_scalar(ints[:, :, :], raw[:, :, :], -1.0, None, ALU.max).then_inc(wq_done, 1)

            def split_low(w, slot, n):
                pool.wait_ge(whi_done, n + 1)
                pool.tensor_tensor(wlo[:, slot, :], w, whi[:, slot, :], ALU.subtract).then_inc(wlo_done, 1)

            split_low(shared_w[:, :], 3, 0)
            for e in range(3):
                split_low(stage[:, e, :], e, e + 1)
            with pool.Fori(0, LOOPS) as it:
                for j in range(4):
                    s = (j + 3) % 4
                    split_low(stage[:, s, :], s, it * 4 + (j + 4))
            split_low(stage[:, 3, :], 3, E)
            for i in range(3):
                pool.wait_ge(l1hi_done, i + 1)
                at = slice(2 * i, 2 * i + 2)
                pool.tensor_tensor(l1lo[:, at], l1w[:, at, :, :], l1hi[:, at], ALU.subtract).then_inc(l1lo_done, 1)
            pool.wait_ge(xn_ready, 6)
            pool.memset(xd_flat[:, 2 * REP * DC * T:2 * REP * DC * T + SPILL], 0.0)
            pool.memset(qm_flat[:, 2 * DC * B * QH * POS:2 * DC * B * QH * POS + SPILL], 0.0)
            pool.memset(qm[:, :, :, :, H1C, :].rearrange("p w c b t -> p (w c b) t"), 0.0)
            for n in range(8):
                pool.wait_ge(rope_t, n + 1)
                if n >= 2:
                    pool.wait_ge(rope_done, n - 1)
                pool.tensor_tensor(rsum[:, n % 2, :], rt[:, n % 2, 0, :], rt[:, n % 2, 1, :], ALU.add).then_inc(rope_sum, 1)
                if n < 4:
                    pool.wait_ge(xdlo_done, 2)
                    im = slice(4 * n, 4 * n + 4)
                    pool.tensor_copy(xdup[:, 1, :, im, 1, :], xdup[:, 1, :, im, 0, :]).then_inc(xdup_done, 1)

            def mask_queries(part, head):
                for w in range(2):
                    pool.tensor_scalar(queries_at(qm[:, w], part, head), queries_at(q1_hl[:, w], part), head_col[:, head:head + 1],
                                       None, ALU.mult).then_inc(qm_pool, 1)

            mask_queries(0, 3)
            mask_queries(1, 2)
            mask_queries(1, 3)
            U = 3 * POS
            for n in range(G):
                pool.wait_ge(p_high, n + 1)
                pool.tensor_tensor(ph[0:U, n % 2, :, 2, :], pr[0:U, n % 2, :, :], ph[0:U, n % 2, :, 0, :],
                                   ALU.subtract).then_inc(p_done, 1)
                if n == 0:
                    mask_queries(1, 4)
            for c in POOL_TAPS:
                pool.wait_ge(fconv_first, c + 1)
                for k in (0, 2):
                    to, of = (slice(1, POS), slice(0, POS - 1)) if k == 0 else (slice(0, POS - 1), slice(1, POS))
                    into, tap = images(h2[:, c, :])[:, :, to], images(tapped)[:, :, 0:POS - 1]
                    link(pool.tensor_scalar(tap, images(hid[:, c, :])[:, :, of], col("ffn_conv_w", 3 * c + k), None, ALU.mult))
                    ins = pool.tensor_tensor(into, into, tap, ALU.add)
                    if k == 0:
                        link(ins)
                ins.then_inc(fconv_pool, 1)
                pool.wait_ge(fconv_pool, POOL_TAPS.index(c) + 1)

        @block.tensor
        def _(pe):
            def mean(n, hf):
                pe.wait_ge(h_ready, 4 * n + 2 * hf + 2)
                for c in range(DC):
                    mm = pe.matmul(bank[4 + hf][:, 0:HT], mean_w[:, :], half(h, c, hf), start=c == 0, stop=c == DC - 1)
                mm.then_inc(ln_mean, 1)

            def layer_norm(n, first=True):
                if first:
                    mean(n, 0)
                mean(n, 1)
                for hf in range(2):
                    pe.wait_ge(ln_sq, 2 * n + hf + 1)
                    for g in range(4):
                        at = (4 * hf + g) * GT
                        for c in range(DC):
                            mm = pe.matmul(bank[6 + hf][0:GT, g:g + 1], sq[:, c, at:at + GT], mean_w[:, 0:1],
                                           start=c == 0, stop=c == DC - 1)
                    mm.then_inc(ln_var, 1)
                for hf in range(2):
                    pe.wait_ge(ln_diag, 2 * n + hf + 1)
                    pe.matmul(bank[4 + hf][:, 0:HT], ones[0:GT, :], rstd[:, 4 * hf:4 * hf + 4, :].rearrange("p g t -> p (g t)"),
                              start=True, stop=True).then_inc(ln_rstd, 1)

            for i in range(3):
                pe.wait_ge(ld_patch[i], 32)
                for hf in range(2):
                    for m in range(DC):
                        for k in (2 * i, 2 * i + 1):
                            mm = pe.matmul(bank[2 * hf + m][:, 0:HB * PATCHES], tokw[:, k, m * 128:(m + 1) * 128],
                                           patch_sb[:, k, hf * HB * PATCHES:(hf + 1) * HB * PATCHES],
                                           start=k == 0, stop=k == TOK_K - 1)
                        if i == 2:
                            mm.then_inc(tok_mm, 1)
            pe.wait_ge(consts, 3)
            layer_norm(0)

            pe.wait_ge(ld_attn, 64)
            for n in range(16):
                hf, m = n // 8, (n % 8) // 2 + 4 * (n % 2)
                if n % 8 == 0:
                    pe.wait_ge(xulo_done, hf + 1)
                    pe.wait_ge(up_lo_done, 1)
                if n >= 4:
                    pe.wait_ge((xm_done, zs_done)[n % 2], n // 2 - 1)
                for k in range(DC):
                    for i, (ww, xw) in enumerate(PARTS):
                        mm = pe.matmul(bank[n % 4][:, 0:HT], up_hl[:, ww, k, m * 128:(m + 1) * 128],
                                       xu_hl[:, xw, k, hf * HT:(hf + 1) * HT], start=k + i == 0, stop=k == DC - 1 and i == 2)
                mm.then_inc(up_mm, 1)

            pe.wait_ge(bd_done, 1)
            for c in range(INNER_C):
                pe.matmul(bank[6][:, c * 64:(c + 1) * 64], bd_t[:, c, :], wg[:, c, :], start=True, stop=False)
                pe.matmul(bank[6][:, c * 64:(c + 1) * 64], bd_t[:, 4 + c, :], wg[:, 4 + c, :], start=False, stop=True)
            for c in range(INNER_C):
                mm = pe.matmul(bank[6][:, (4 + c) * 64:(5 + c) * 64], bd_t[:, 8 + c, :], wg[:, 8 + c, :],
                               start=True, stop=True)
            mm.then_inc(geff_mm, 1)

            pe.wait_ge(geff_done, 1)
            pe.wait_ge(xm_done, 8)
            pe.wait_ge(bd_done, 2)
            pe.wait_ge(zs_done, 8)
            for step in range(INNER_C + 1):
                for g in (2 * step, 2 * step + 1):
                    if g >= G:
                        continue
                    if g >= 3:
                        pe.wait_ge(vlo_done, g - 2)
                    for c in range(INNER_C):
                        mm = pe.matmul(bank[(6, 7, 3)[g % 3]][0:GT, c * DH:(c + 1) * DH], xm[:, c, g * GT:(g + 1) * GT],
                                       bd[:, 8 + c, :], start=True, stop=True)
                    mm.then_inc(v_mm, 1)
                if step == 0:
                    continue
                c = step - 1
                for hf in range(2):
                    pe.matmul(bank[4 + hf][0:64, 0:HT], geff[:, 4 + c, :], half(xm, c, hf), start=c == 0, stop=False)
                pe.wait_ge(xc_ready, c + 1)
                for hf in range(2):
                    mm = pe.matmul(bank[4 + hf][0:64, 0:HT], geff[:, c, :], half(xc, c, hf),
                                   start=False, stop=c == INNER_C - 1)
                    if c == INNER_C - 1:
                        mm.then_inc(gates_mm, 1)
            pe.wait_ge(vlo_done, 8)
            for n in range(16):
                c, hf, kind = n // 4, (n // 2) % 2, n % 2
                if n >= 4:
                    pe.wait_ge((qlo_done, klo_done)[kind], n // 2 - 1)
                pe.matmul(bank[n % 4][:, 0:HT], bd[:, 4 * kind + c, :], half(xc, c, hf),
                          start=True, stop=True).then_inc(qk_mm, 1)

            def scores(g):
                if g == 0:
                    pe.wait_ge(qlo_done, 8)
                    pe.wait_ge(klo_done, 8)
                if g >= 2:
                    pe.wait_ge(c_done, g - 1)
                tok = slice(g * GT, (g + 1) * GT)
                for c in range(INNER_C):
                    for i, (kw, qw) in enumerate(PARTS):
                        k_at = (kw * INNER_C + c) * T + g * GT
                        q_at = (qw * INNER_C + c) * T + g * GT
                        mm = pe.matmul(bank[g % 2][:, c * GT:(c + 1) * GT], k_hl[:, k_at:k_at + 128],
                                       q_hl[:, q_at:q_at + GT], start=i == 0, stop=i == 2)
                mm.then_inc(s_mm, 1)
                if g == 0:
                    pe.wait_ge(wabs_done, 2)
                    pe.matmul(bank[7][:, 64:66], ones[:, :], wabs[:, :], start=True, stop=True).then_inc(wmean_mm, 1)
                    pe.wait_ge(arow_done, 2)
                    pe.wait_ge(mid_placed, 2)
                dst = bank[2 + g % 2]
                pe.matmul(dst[:, 0:INNER_C * GT], a3[0:68, g * GT:g * GT + 128], sel3[0:68, :, 0:GT], start=True, stop=False)
                for c in range(INNER_C):
                    pe.matmul(dst[:, c * GT:(c + 1) * GT], sel3[0:68, c, :], m3[0:68, tok], start=False, stop=False)
                pe.matmul(dst[:, 0:INNER_C * GT], ident_b[:, :], causal[:, :, :],
                          start=False, stop=True).then_inc(e_mm, 1)

            pe.wait_ge(consts, 2)
            scores(0)
            for g in range(G):
                if g + 1 < G:
                    scores(g + 1)
                if g == 0:
                    pe.wait_ge(nrow_done, 1)
                    pe.wait_ge(wmean_done, 1)
                    for gg in range(G):
                        mm = pe.matmul(bank[7][0:GT, gg * INNER_C:(gg + 1) * INNER_C], nrow[:, gg * GT:(gg + 1) * GT],
                                       ident[0:INNER_C, 0:INNER_C], start=True, stop=True)
                    mm.then_inc(floor_mm, 1)
                    pe.wait_ge(gts_done, 2)
                pe.wait_ge(c_split, g + 1)
                if g >= 2:
                    pe.wait_ge(hstat_done, g - 1)
                    pe.wait_ge(hraw_done, g - 1)
                for c in range(INNER_C):
                    high, low = (c_hl[:, g % 2, w, c * GT:c * GT + 128] for w in range(2))
                    total = bank[6][:, g * INNER_C + c:g * INNER_C + c + 1]
                    pe.matmul(total, high, ones_h[0:GT, :], start=True, stop=False)
                    pe.matmul(total, low, ones_h[0:GT, :], start=False, stop=True)
                    for i, (cw, vw) in enumerate(PARTS):
                        mm = pe.matmul(bank[4 + g % 2][:, c * DH:(c + 1) * DH], (high, low)[cw],
                                       v[0:GT, vw, g, c * DH:(c + 1) * DH], start=i == 0, stop=i == 2)
                mm.then_inc(hv_mm, 1)
            for g in range(G):
                pe.wait_ge(hn_done, g + 1)
                pe.wait_ge(hnv_done, g + 1)
                if g >= 2:
                    pe.wait_ge(hst_done, g - 1)
                for c in range(INNER_C):
                    mm = pe.transpose(bank[g % 2][:, c * GT:(c + 1) * GT], hraw[0:GT, g, c * DH:(c + 1) * DH],
                                      ident[0:GT, 0:GT])
                mm.then_inc(ht_mm, 1)
            for hf in range(2):
                pe.wait_ge(hst_done, G // 2 * (hf + 1))
                for m in range(DC):
                    for k in range(INNER_C):
                        mm = pe.matmul(bank[(2, 3, 6, 7)[2 * hf + m]][:, 0:HT], wdn[:, k, m * 128:(m + 1) * 128], half(hst, k, hf),
                                       start=k == 0, stop=k == INNER_C - 1)
                    mm.then_inc(down0_mm, 1)

            layer_norm(1)

            pe.wait_ge(ld_ffn, 32)
            for g in range(G):
                if g % 4 == 0:
                    pe.wait_ge(xn_ready, 2 + g // 4 + 1)
                for k in range(DC):
                    mm = pe.matmul(bank[7][0:GT, g * E:(g + 1) * E], xn[:, k, g * GT:(g + 1) * GT], wrt[:, k, :],
                                   start=k == 0, stop=k == DC - 1)
            mm.then_inc(route_mm, 1)

            def into_hidden(dst, slot, at, hf, done):
                n = 0
                for k in range(DC):
                    w_at = slice(at + k * 128, at + (k + 1) * 128)
                    for w, x in ((whi, xhi), (whi, xlo), (wlo, xhi)):
                        mm = pe.matmul(dst[:, 0:HT], w[:, slot, w_at], half(x, k, hf), start=n == 0, stop=n == 5)
                        n += 1
                mm.then_inc(done, 1)

            def down(slot, hf, n, last=False):
                pe.wait_ge(alo_done, n + 1)
                s = hf
                for m in range(DC):
                    w_at = slice(512 + m * 128, 512 + (m + 1) * 128)
                    for i, (w, x) in enumerate(((whi, ahi), (whi, alo), (wlo, ahi))):
                        mm = pe.matmul(bank[2 * hf + m][:, 0:HT], w[:, slot, w_at], x[:, s, :],
                                       start=False, stop=last and i == 2, skip_group_check=True)
                mm.then_inc(down_mm, 1)

            pe.wait_ge(wlo_done, 1)
            pe.wait_ge(xlo_done, 2)
            for i in range(4):
                pe.matmul(bank[i][:, 0:HT], zero_w[:, :], half(xhi, 0, 0), start=True, stop=False, skip_group_check=True)
            into_hidden(bank[4], 3, 0, 0, gate_mm)
            into_hidden(bank[5], 3, 256, 0, uproj_mm)
            pe.wait_ge(aff_done, 1)
            into_hidden(bank[6], 3, 0, 1, gate_mm)
            into_hidden(bank[7], 3, 256, 1, uproj_mm)
            down(3, 0, 0)
            pe.wait_ge(mask_done, 1)
            pe.wait_ge(act_done, 1)
            for g in range(G):
                mm = pe.transpose(bank[4][:, g * 64:g * 64 + 64].bitcast(F16)[:, 0:GT], mask_hl[:, g, :], ident_h[0:GT, 0:GT])
            mm.then_inc(maskt_mm, 1)
            pe.wait_ge(maskt_done, 1)

            def four_experts(it, last=False):
                r = 0
                for j in range(4):
                    for hf in range(2):
                        n = it * 8 + (2 * j + hf + 2)
                        if hf == 0:
                            pe.wait_ge(wlo_done, it * 4 + (j + 2))
                        for kind in range(3):
                            old = r - 4
                            steps = n - (2 * j + hf) + old // 3
                            pe.wait_ge((silu_done, gu_done, act_done)[old % 3], steps + 1)
                            b = bank[4 + r % 4]
                            if kind == 0:
                                into_hidden(b, j, 0, hf, gate_mm)
                            elif kind == 1:
                                into_hidden(b, j, 256, hf, uproj_mm)
                            else:
                                e = it * 4 + j
                                pe.matmul(b[:, 0:HT], expert_sel[:, bass.ds(e, 1)].broadcast_to([128, 128]),
                                          maskT[:, hf * HT:(hf + 1) * HT], start=True, stop=True).then_inc(mask_mm, 1)
                            r += 1
                        down((j - 1 + hf) % 4, 1 - hf, n - 1, last=last and j == 3 and hf == 1)

            with pe.Fori(0, LOOPS) as it:
                four_experts(it)
            four_experts(LOOPS, last=True)
            down(3, 1, 2 * E + 1, last=True)

            layer_norm(2)

            pe.wait_ge(ld_bit, 48)
            n = 0
            pe.wait_ge(l1lo_done, 3)
            for qk in range(2):
                for hf in range(2):
                    pe.wait_ge(xdlo_done, hf + 1)
                    for m in range(DC):
                        if n >= 2:
                            pe.wait_ge(rope_t, n - 1)
                        for sw in range(2):
                            b = bank[2 * (n % 2) + sw]
                            for k in range(DC):
                                for i, (ww, xw) in enumerate(PARTS):
                                    mm = pe.matmul(b[:, 0:HT], (l1hi, l1lo)[ww][:, 2 * qk + sw, k, m * 128:(m + 1) * 128],
                                                   xdup[:, xw, k, hf * HB:(hf + 1) * HB, 0, :],
                                                   start=k + i == 0, stop=k == DC - 1 and i == 2)
                        mm.then_inc(rope_mm, 1)
                        n += 1
            pe.wait_ge(xdhi_done, 6)
            pe.wait_ge(xdlast_done, 1)
            pe.wait_ge(xdup_done, 4)
            for n in range(G):
                if n >= 4:
                    pe.wait_ge(v1lo_done, n - 3)
                for i in range(2):
                    b = 2 * n + i
                    for k in range(DC):
                        for j, (xw, ww) in enumerate(PARTS):
                            at = ((xw * DC + k) * B + b) * UK
                            mm = pe.matmul(bank[4 + n % 4][:, i * D:(i + 1) * D], xd_flat[:, at:at + 128],
                                           (l1hi, l1lo)[ww][:, 4, k, :], start=k + j == 0, stop=k == DC - 1 and j == 2)
                mm.then_inc(vb_mm, 1)

            U = 3 * POS

            def att_scores(n):
                if n == 0:
                    pe.wait_ge(qm_done, 4)
                    pe.wait_ge(qm_act, 6)
                    pe.wait_ge(qm_pool, 2)
                    pe.wait_ge(rope_done, 8)
                if 2 * n == HB:
                    pe.wait_ge(qm_done, 7)
                    pe.wait_ge(qm_act, 10)
                    pe.wait_ge(qm_pool, 8)
                if n >= 2:
                    pe.wait_ge(sc_sub, n - 1)
                for i in range(2):
                    b = 2 * n + i
                    for c in range(DC):
                        for u in range(3):
                            o = (i * 6 + c * 3 + u) * POS
                            for j, (qw, kw) in enumerate(PARTS):
                                at = ((qw * DC + c) * B + b) * QH * POS + u * U
                                mm = pe.matmul(bank[n % 2][:, o:o + POS], qm_flat[:, at:at + 128],
                                               k1_hl[:, kw, c, b * POS:(b + 1) * POS], start=j == 0, stop=j == 2)
                mm.then_inc(sc_mm, 1)

            def turn(b):
                pe.wait_ge(p_done, b // 2 + 1)
                pe.wait_ge(p_again, b // 2 + 1)
                if b >= 2:
                    pe.wait_ge(pt_done, b - 1)
                for u in range(6):
                    mm = pe.transpose(bank[2 + b % 2][0:UK, 56 * u:56 * (u + 1)].bitcast(F16)[:, 0:U],
                                      ph[0:U, (b // 2) % 2, (b % 2) * 6 + u, :, :].rearrange("p w t -> p (w t)"),
                                      ident_h[0:U, 0:U])
                mm.then_inc(pt_mm, 1)

            def outputs_back(hf):
                if hf == 0:
                    pe.wait_ge(v1lo_done, 8)
                else:
                    pe.wait_ge(pt_done, B)
                for c in range(DC):
                    for b in range(HB):
                        if c == 0:
                            pe.wait_ge(ot_done, hf * HB + b + 1)
                        mm = pe.transpose(bank[6 - 4 * hf + c][:, b * POS:(b + 1) * POS],
                                          otok[0:POS, hf * HB + b, c * 128:(c + 1) * 128], ident[0:POS, 0:POS])
                    mm.then_inc(ott_mm, 1)

            def project(hf, m):
                pe.wait_ge(oT_done, 2 * hf + 2)
                for k in range(DC):
                    mm = pe.matmul(bank[6 - 6 * hf + m][:, 0:HT], l1w[:, 5, k, m * 128:(m + 1) * 128], half(oT, k, hf),
                                   start=k == 0, stop=k == DC - 1)
                mm.then_inc(wo_mm, 1)

            att_scores(0)
            att_scores(1)
            att_scores(2)
            pe.wait_ge(v1lo_done, 6)
            turn(0)
            for b in range(B):
                if b % 2 == 1 and b // 2 + 3 < G:
                    att_scores(b // 2 + 3)
                if b == B - 3:
                    project(0, 0)
                if b + 1 < B:
                    turn(b + 1)
                if b == B - 2:
                    project(0, 1)
                pe.wait_ge(pt_done, b + 1)
                if b >= 2:
                    pe.wait_ge(ot_done, b - 1)
                for hh in range(H1):
                    c, q = hh // H1C, hh % H1C
                    at = (3 * c + q // 3) * PTW + q % 3 * POS
                    dst = bank[4 + b % 2][0:POS, hh * HD1:(hh + 1) * HD1]
                    feat = slice(hh * HD1, (hh + 1) * HD1)
                    mm = pe.matmul(dst, pT[0:UK, b % 2, at:at + POS], v1[0:UK, b, feat], start=True, stop=True)
                mm.then_inc(pv_mm, 1)
                if b == 4:
                    pe.wait_ge(v1lo_done, 8)
                if b == HB:
                    outputs_back(0)
            outputs_back(1)
            mean(3, 0)
            for m in range(DC):
                project(1, m)

            layer_norm(3, first=False)

            def token_scales(n):
                pe.wait_ge(amax_done, n + 1)
                for g in range(G):
                    b = bank[(4, 5)[g // 4]]
                    mm = pe.transpose(b[0:GT, (g % 4) * 128:(g % 4 + 1) * 128], amax[:, g * GT:(g + 1) * GT], ident[:, :])
                mm.then_inc(amaxt_mm, 1)
                pe.wait_ge(tsc_done, n + 1)
                pe.transpose(bank[6][0:2 * G, 0:GT], tsc[:, :, :].rearrange("p a g -> p (a g)"),
                             ident[0:GT, 0:GT]).then_inc(tsct_mm, 1)
                for kind in range(2):
                    pe.wait_ge(tsct_done, 2 * n + kind + 1)
                    for hf in range(2):
                        pe.matmul(bank[4 + 2 * kind + hf][:, 0:HT], ones[0:2 * G, :],
                                  spread[:, kind, 4 * hf:4 * hf + 4, :].rearrange("p g t -> p (g t)"),
                                  start=True, stop=True).then_inc(bc_mm, 1)

            token_scales(0)
            pe.wait_ge(wq_done, 2)
            for n in range(16):
                m, hf = n // 2, n % 2
                pe.wait_ge(xq_done, 2 * hf + 2)
                if n >= 4:
                    pe.wait_ge(hid_done, n - 3)
                for k in range(DC):
                    mm = pe.matmul(bank[n % 4][:, 0:HT], w1q[:, k, m * 128:(m + 1) * 128], half(x4q, k, hf),
                                   start=k == 0, stop=k == DC - 1)
                mm.then_inc(w1_mm, 1)
            token_scales(1)
            for hf in range(2):
                for ks in (0, 4):
                    if (hf, ks) != (1, 4):
                        pe.wait_ge(h2q_done, 2 * hf + ks // 4 + 1)
                    else:
                        pe.wait_ge(last_rounded, 1)
                    for m in range(DC):
                        for k in range(ks, ks + 4):
                            mm = pe.matmul(bank[2 * hf + m][:, 0:HT], w2q[:, k, m * 128:(m + 1) * 128], half(h2q, k, hf),
                                           start=k == 0, stop=k == FC - 1)
                        if ks:
                            mm.then_inc(w2_mm, 1)

        @block.scalar
        def _(a):
            def layer_norm(n):
                a.activation(root_warm[:, n:n + 1], eps_col[:, :], ACT.Sqrt)
                for hf in range(2):
                    a.wait_ge(ln_cent, 2 * n + hf + 1)
                    a.activation(sq[:, :, hf * HT:(hf + 1) * HT], xn[:, :, hf * HT:(hf + 1) * HT], ACT.Square).then_inc(ln_sq, 1)
                for hf in range(2):
                    a.wait_ge(ln_var, 2 * n + hf + 1)
                    a.activation(var8[:, 0, 4 * hf:4 * hf + 4], bank[6 + hf][0:GT, 0:4], ACT.Sqrt,
                                 bias=eps_col[0:GT, :]).then_inc(ln_std, 1)

            a.wait_ge(ld_up, 16)
            a.activation(up_hl[:, 0, :, :], wup[:, :, :], ACT.Copy).then_inc(up_hi_done, 1)
            a.wait_ge(consts, 1)
            layer_norm(0)
            for hf in range(2):
                tok = slice(hf * HT, (hf + 1) * HT)
                a.wait_ge(xn_ready, hf + 1)
                a.activation(xu_hl[:, 0, :, tok], xn[:, :, tok], ACT.Copy).then_inc(xuhi_done, 1)
            for n in range(8):
                a.wait_ge(up_mm, 2 * n + 2)
                hf, c = n // 4, n % 4
                a.activation(half(zs, c, hf), bank[(2 * n + 1) % 4][:, 0:HT], ACT.Silu).then_inc(zs_done, 1)
            for c in range(INNER_C):
                a.wait_ge(xm_done, 5 + c)
                a.activation(cacc[:, c, :], xm[:, c, :], ACT.Identity, bias=col("conv_b", c),
                             scale=col("conv_w", c * CONV + CONV - 1)).then_inc(conv_first, 1)

            def magnitudes(i):
                a.wait_ge((ld_bit, ld_w2)[i], (48, 16)[i])
                a.activation((sq, xn)[i][:, :, :].rearrange("p c t -> p (c t)").bitcast(F16)[:, 0:2048],
                             (wraw1, wraw2)[i][:, :, :].rearrange("p a b -> p (a b)"), ACT.Abs,
                             accum_out=wabs[:, i:i + 1]).then_inc(wabs_done, 1)

            magnitudes(0)
            a.wait_ge(tok_mm, 4)

            def values_high(pair):
                for g in (2 * pair, 2 * pair + 1):
                    a.wait_ge(v_mm, g + 1)
                    a.activation(v[0:GT, 0, g, :], bank[(6, 7, 3)[g % 3]][0:GT, :], ACT.Copy).then_inc(v_done, 1)

            values_high(0)
            for c in range(INNER_C):
                if c + 1 < G // 2:
                    values_high(c + 1)
                if c < INNER_C - 1:
                    a.wait_ge(conv_done, c + 1)
                else:
                    a.wait_ge(conv_pool, 1)
                a.activation(xc[:, c, :], cacc[:, c, :], ACT.Silu).then_inc(xc_ready, 1)
            magnitudes(1)
            a.activation(root_warm[:, 5:6], eps_col[:, :], ACT.Exp)

            def parts_high(*which):
                for n in which:
                    c, hf, kind = n // 4, (n // 2) % 2, n % 2
                    at = c * T + hf * HT
                    a.wait_ge(qk_mm, n + 1)
                    a.activation((q_hl, k_hl)[kind][:, at:at + HT], bank[n % 4][:, 0:HT], ACT.Copy,
                                 scale=(QK_SCALE, 1.0)[kind]).then_inc(qkhi_done, 1)

            parts_high(0, 1, 2, 3)
            a.wait_ge(absf_done, 1)
            a.activation(lf[:, 1, :], lf[:, 0, :], ACT.Exp, scale=-1.0).then_inc(act_step, 1)
            a.wait_ge(act_step, 1)
            a.activation(lf[:, 1, :], lf[:, 1, :], ACT.Ln, bias=ones[0:INNER_C, 0:1]).then_inc(lnf_done, 1)
            parts_high(4, 5)
            a.wait_ge(arow_in, 1)
            a.activation(a3[0:INNER_C, 0:T], arow[:, :], ACT.Copy).then_inc(gate_hi, 1)
            a.wait_ge(mrow_in, 1)
            a.activation(m3[0:INNER_C, 0:T], mrow[:, :], ACT.Copy, scale=-1.0).then_inc(gate_hi, 1)
            parts_high(6, 7)
            for i, parts in enumerate((a3, m3)):
                a.wait_ge(gate_rest, i + 1)
                a.activation(mid[:, i, :], rrow[:, i, :], ACT.Copy).then_inc(gate_mid, 1)
            for i, parts in enumerate((a3, m3)):
                a.wait_ge(gate_mid, i + 1)
                a.activation(parts[32:32 + INNER_C, 0:T], mid[:, i, :], ACT.Copy).then_inc(mid_placed, 1)
            parts_high(*range(8, 16))
            a.wait_ge(nrow_in, 1)
            a.activation(nrow[:, :], nrow[:, :], ACT.Exp, scale=-1.0).then_inc(nrow_done, 1)

            def decay(g):
                a.wait_ge(e_mm, g + 1)
                if g >= 2:
                    a.wait_ge(c_done, g - 1)
                a.activation(dmat[:, g % 2, :, :], bank[2 + g % 2][0:GT, 0:INNER_C * GT], ACT.Exp).then_inc(d_done, 1)

            def weights_high(g):
                a.wait_ge(c_done, g + 1)
                if g >= 2:
                    a.wait_ge(hv_mm, g - 1)
                    a.wait_ge(c_split, g - 1)
                a.activation(c_hl[:, g % 2, 0, 0:INNER_C * GT], cmat[:, g % 2, :], ACT.Copy).then_inc(c_high, 1)

            decay(0)
            weights_high(0)
            decay(1)
            for g in range(G):
                if g + 1 < G:
                    weights_high(g + 1)
                if g + 2 < G:
                    decay(g + 2)
                a.wait_ge(hstat_done, g + 1)
                a.activation(hraw[0:GT, g, :], bank[4 + g % 2][0:GT, :], ACT.Copy).then_inc(hraw_done, 1)
                if g == 0:
                    a.wait_ge(wmean_done, 1)
                i, raw = ((0, wraw1), (1, wraw2))[g // 4]
                piece = raw[:, :, :].rearrange("p a b -> p (a b)")[:, g % 4 * 512:(g % 4 + 1) * 512]
                a.activation(piece, piece, ACT.Identity, bias=magic_col[:, :], scale=wscale[:, i:i + 1]).then_inc(wscaled, 1)
            a.activation(root_warm[:, 4:5], eps_col[:, :], ACT.Sqrt)
            a.wait_ge(hvar_done, 1)
            a.activation(tiny[:, 3, :], tiny[:, 2, :], ACT.Sqrt, bias=eps_col[0:GT, :]).then_inc(hstd_done, 1)
            a.wait_ge(hcoef_done, 1)
            for g in range(G):
                for c in range(INNER_C - 1):
                    n = g * INNER_C + c
                    head = hraw[0:GT, g, c * DH:(c + 1) * DH]
                    ins = a.activation(head, head, ACT.Identity, bias=tiny[:, 1, n:n + 1], scale=tiny[:, 5, n:n + 1])
                ins.then_inc(hn_done, 1)
            def split_high(slot):
                a.activation(whi[:, slot, :], stage[:, slot, :], ACT.Copy).then_inc(whi_done, 1)

            a.wait_ge(ld_ffn, 32)
            a.activation(whi[:, 3, :], shared_w[:, :], ACT.Copy).then_inc(whi_done, 1)
            for e in range(3):
                if e % 2 == 0:
                    a.wait_ge(ld_stage[e // 2], 16)
                split_high(e)
            layer_norm(1)
            for hf in range(2):
                a.wait_ge(xn_ready, 2 + hf + 1)
                a.activation(xhi[:, :, hf * HT:(hf + 1) * HT], xn[:, :, hf * HT:(hf + 1) * HT], ACT.Copy).then_inc(xhi_done, 1)
            a.wait_ge(route_mm, 1)
            a.activation(aff[:, :, :].rearrange("p g e -> p (g e)"), bank[7][0:GT, :], ACT.Sigmoid).then_inc(aff_done, 1)

            def silu(b, s, n):
                a.wait_ge(gate_mm, n + 1)
                a.activation(sg[:, s, :], b[:, 0:HT], ACT.Silu).then_inc(silu_done, 1)

            silu(bank[4], 0, 0)
            silu(bank[6], 1, 1)

            def four_experts(it, last=False):
                for j in range(4):
                    for hf in range(2):
                        n = it * 8 + (2 * j + hf + 2)
                        r = 3 * (2 * j + hf)
                        a.wait_ge(gu_done, n - 1)
                        silu(bank[4 + r % 4], hf, n)
                    if last and j > 0:
                        at = slice(2 * j - 2, 2 * j)
                        a.activation(l1hi[:, at], l1w[:, at, :, :], ACT.Copy).then_inc(l1hi_done, 1)
                        continue
                    s = (j + 3) % 4
                    if s == 0:
                        a.wait_ge(ld_stage[0], it * 16 + 32)
                    if s == 2:
                        a.wait_ge(ld_stage[1], it * 16 + 32)
                    a.wait_ge(down_mm, it * 8 + (2 * j + 2))
                    split_high(s)

            with a.Fori(0, LOOPS) as it:
                four_experts(it)
            a.wait_ge(ld_bit, 48)
            a.wait_ge(wq_done, 2)
            four_experts(LOOPS, last=True)

            layer_norm(2)
            for i in range(REP):
                for hf in range(2):
                    a.wait_ge(xn_ready, 4 + hf + 1)
                    a.activation(xdup[:, 0, :, hf * HB:(hf + 1) * HB, i, :],
                                 xn[:, :, hf * HT:(hf + 1) * HT].rearrange("p c (b t) -> p c b t", t=POS),
                                 ACT.Copy).then_inc(xdhi_done, 1)
            n = 0
            for qk in range(2):
                for hf in range(2):
                    for m in range(DC):
                        a.wait_ge(rope_sum, n + 1)
                        a.activation(half((q1_hl, k1_hl)[qk][:, 0], m, hf), rsum[:, n % 2, :], ACT.Copy).then_inc(rope_hi, 1)
                        n += 1
            a.wait_ge(rope_done, 4)

            def mask_queries(part, head, w):
                a.activation(queries_at(qm[:, w], part, head), queries_at(q1_hl[:, w], part), ACT.Copy,
                             scale=head_col[:, head:head + 1]).then_inc(qm_act, 1)

            for n in range(G):
                if n < 6:
                    mask_queries(0, n // 2, n % 2)
                a.wait_ge(vb_mm, n + 1)
                a.activation(v1[0:UK, 2 * n:2 * n + 2, :], bank[4 + n % 4][0:UK, :].rearrange("p (b m) -> p b m", b=2),
                             ACT.Copy).then_inc(v1hi_done, 1)
            U = 3 * POS

            def exps(n):
                a.wait_ge(sc_sub, n + 1)
                a.activation(pr[0:U, n % 2, :, :], pr[0:U, n % 2, :, :], ACT.Exp, scale=1.0 / 16.0).then_inc(sc_exp, 1)

            def outputs(b):
                a.wait_ge(pv_mm, b + 1)
                a.activation(otok[0:POS, b, :], bank[4 + b % 2][0:POS, 0:D], ACT.Copy).then_inc(ot_done, 1)

            def quotients_high(n):
                a.wait_ge(quot_done, n + 1)
                if n >= 2:
                    a.wait_ge(pt_mm, 2 * (n - 1))
                a.activation(ph[0:U, n % 2, :, 0, :], pr[0:U, n % 2, :, :], ACT.Copy).then_inc(p_high, 1)

            def outputs_back(hf):
                for c in range(DC):
                    a.wait_ge(ott_mm, 2 * hf + c + 1)
                    a.activation(half(oT, c, hf), bank[6 - 4 * hf + c][:, 0:HT], ACT.Identity, bias=col("bv", c)).then_inc(oT_done, 1)

            exps(0)
            exps(1)
            quotients_high(0)
            for b in range(B):
                if b == HB + 3:
                    outputs_back(0)
                if b >= 2:
                    a.wait_ge(pv_mm, b - 1)
                a.wait_ge(pt_mm, b + 1)
                a.activation(pT[0:UK, b % 2, :].rearrange("p (u m) -> p u m", u=6)[:, :, 0:U],
                             bank[2 + b % 2][0:UK, 0:336].bitcast(F16).rearrange("p (u m) -> p u m", u=6)[:, :, 0:U],
                             ACT.Copy).then_inc(pt_done, 1)
                if b >= 1:
                    outputs(b - 1)
                if b % 2 == 0 and b // 2 + 1 < G:
                    quotients_high(b // 2 + 1)
                if b < 3:
                    for i in ((0, 1), (2,), (3,))[b]:
                        mask_queries(1, i // 2, i % 2)
                if b % 2 == 1 and b // 2 + 2 < G:
                    exps(b // 2 + 2)
            outputs(B - 1)
            outputs_back(1)

            layer_norm(3)
            a.wait_ge(xn_ready, 8)
            a.activation(habs[:, 1, :], xn[:, 1, :], ACT.Abs).then_inc(habs_done, 1)
            for s in range(FC + 2):
                if s < FC:
                    a.wait_ge(hid_done, 2 * s + 2)
                    a.activation(h2[:, s, :], hid[:, s, :], ACT.Identity, bias=col("ffn_conv_b", s),
                                 scale=col("ffn_conv_w", 3 * s + 1)).then_inc(fconv_first, 1)
                if s >= 2:
                    c = TAP_ORDER[s - 2]
                    if c in POOL_TAPS:
                        a.wait_ge(fconv_pool, POOL_TAPS.index(c) + 1)
                    else:
                        a.wait_ge(fconv_done, [x for x in range(FC) if x not in POOL_TAPS].index(c) + 1)
                    a.activation(h2[:, c, :], h2[:, c, :], ACT.Silu).then_inc(h2_done, 1)
                    a.wait_ge(h2_done, s - 1)
                    if s == 2:
                        a.wait_ge(amax_done, 1)
                    a.activation(habs[:, c, :], h2[:, c, :], ACT.Abs).then_inc(habs_done, 1)
            for i in range(3):
                hf, c = i // 2, i % 2 * 4
                block_of = h2[:, c:c + 4, hf * HT:(hf + 1) * HT]
                a.wait_ge(clipped, i + 1)
                a.activation(block_of, block_of, ACT.Identity, bias=magic_col[:, :]).then_inc(rounded, 1)
                a.wait_ge(rounded, i + 1)
                a.activation(h2q[:, c:c + 4, hf * HT:(hf + 1) * HT], block_of, ACT.Identity,
                             bias=minus_magic[:, :]).then_inc(h2q_done, 1)

        @block.vector
        def _(d):
            steps = [0]

            def link(ins):
                steps[0] += 1
                ins.then_inc(vec_step, 1)
                d.wait_ge(vec_step, steps[0])

            def magnitude(out, x):
                return d.scalar_tensor_tensor(out=out, in0=x, scalar=-1.0, in1=x, op0=ALU.mult, op1=ALU.max)

            def centre(n, hf):
                tok = slice(hf * HT, (hf + 1) * HT)
                d.wait_ge(h_ready, 4 * n + 2 * hf + 2)
                d.wait_ge(ln_mean, 2 * n + hf + 1)
                d.tensor_tensor(xn[:, :, tok], h[:, :, tok],
                                bank[4 + hf][:, 0:HT].unsqueeze(1).broadcast_to([128, DC, HT]), ALU.subtract).then_inc(ln_cent, 1)

            def layer_norm(n):
                centre(n, 1)
                for hf in range(2):
                    gs = slice(4 * hf, 4 * hf + 4)
                    d.wait_ge(ln_std, 2 * n + hf + 1)
                    link(d.reciprocal(var8[:, 1, gs], var8[:, 0, gs]))
                    d.tensor_tensor(rstd[:, gs, :], ident[0:GT, 0:GT].unsqueeze(1).broadcast_to([GT, 4, GT]),
                                    var8[:, 1, gs].unsqueeze(2).broadcast_to([GT, 4, GT]), ALU.mult).then_inc(ln_diag, 1)
                for hf in range(2):
                    tok = slice(hf * HT, (hf + 1) * HT)
                    d.wait_ge(ln_rstd, 2 * n + hf + 1)
                    d.tensor_tensor(xn[:, :, tok], xn[:, :, tok],
                                    bank[4 + hf][:, 0:HT].unsqueeze(1).broadcast_to([128, DC, HT]), ALU.mult).then_inc(xn_ready, 1)

            def add_to_h(n, banks, done, early):
                for hf in range(2):
                    for m in range(DC):
                        d.wait_ge(done, 2 * hf + m + 1)
                        d.tensor_tensor(half(h, m, hf), half(h, m, hf), banks[2 * hf + m][:, 0:HT], ALU.add).then_inc(h_ready, 1)
                    if hf == early:
                        centre(n, 0)

            d.wait_ge(consts, 3)
            d.wait_ge(ld_first, 32)
            for m in range(DC):
                d.tensor_scalar(posb[:, m, :], posw[:, m, :], col("tok_b", m), None, ALU.add)
                link(d.tensor_tensor(cls0[:, m:m + 1], col("cls", m), posw[:, m, 0:1], ALU.add))
                d.tensor_copy(images(h[:, m, :])[:, :, 0:1], cls0[:, m:m + 1].unsqueeze(1).broadcast_to([128, B, 1]))
            for hf in range(2):
                for m in range(DC):
                    d.wait_ge(tok_mm, 2 * hf + m + 1)
                    d.tensor_tensor(images(half(h, m, hf))[:, :, 1:POS],
                                    bank[2 * hf + m][:, 0:HB * PATCHES].rearrange("p (b t) -> p b t", t=PATCHES),
                                    posb[:, m, 1:POS].unsqueeze(1).broadcast_to([128, HB, PATCHES]), ALU.add).then_inc(h_ready, 1)
            centre(0, 0)
            layer_norm(0)
            for hf in range(2):
                tok = slice(hf * HT, (hf + 1) * HT)
                d.wait_ge(xuhi_done, hf + 1)
                d.tensor_tensor(xu_hl[:, 1, :, tok], xn[:, :, tok], xu_hl[:, 0, :, tok], ALU.subtract).then_inc(xulo_done, 1)

            for n in range(8):
                hf, c = n // 4, n % 4
                d.wait_ge(up_mm, 2 * n + 1)
                d.tensor_copy(half(xm, c, hf), bank[(2 * n) % 4][:, 0:HT]).then_inc(xm_done, 1)
            d.wait_ge(geff_mm, 1)
            d.tensor_copy(geff[:, :, :].rearrange("p a b -> p (a b)"), bank[6][:, :]).then_inc(geff_done, 1)
            for c in range(INNER_C):
                if c < INNER_C - 1:
                    d.wait_ge(conv_first, c + 1)
                    for back in range(1, CONV):
                        into = images(cacc[:, c, :])[:, :, back:POS]
                        ins = d.scalar_tensor_tensor(out=into, in0=images(xm[:, c, :])[:, :, 0:POS - back],
                                                     scalar=col("conv_w", c * CONV + CONV - 1 - back), in1=into,
                                                     op0=ALU.mult, op1=ALU.add)
                        if back < CONV - 1:
                            link(ins)
                    ins.then_inc(conv_done, 1)
                for n in (2 * c, 2 * c + 1):
                    d.wait_ge(v_done, n + 1)
                    d.tensor_tensor(v[0:GT, 1, n, :], bank[(6, 7, 3)[n % 3]][0:GT, :], v[0:GT, 0, n, :], ALU.subtract).then_inc(vlo_done, 1)
            d.memset(k_hl[:, 2 * INNER_C * T:2 * INNER_C * T + SPILL], 0.0)

            def parts_low(*which):
                for n in which:
                    c, hf = n // 2, n % 2
                    hi, lo = c * T + hf * HT, (INNER_C + c) * T + hf * HT
                    d.wait_ge(qkhi_done, 2 * n + 1)
                    d.scalar_tensor_tensor(out=q_hl[:, lo:lo + HT], in0=bank[2 * n % 4][:, 0:HT], scalar=QK_SCALE,
                                           in1=q_hl[:, hi:hi + HT], op0=ALU.mult, op1=ALU.subtract).then_inc(qlo_done, 1)
                    d.wait_ge(qkhi_done, 2 * n + 2)
                    d.tensor_tensor(k_hl[:, lo:lo + HT], bank[(2 * n + 1) % 4][:, 0:HT], k_hl[:, hi:hi + HT],
                                    ALU.subtract).then_inc(klo_done, 1)

            for hf in range(2):
                d.wait_ge(gates_mm, hf + 1)
                d.tensor_scalar(gts[:, hf * HT:(hf + 1) * HT], bank[4 + hf][0:64, 0:HT], col("gate_b", 0, slice(0, 64)),
                                None, ALU.add).then_inc(gts_done, 1)
            d.wait_ge(gts_done, 2)
            d.tensor_scalar(lf[:, 2, :], gts[32:32 + INNER_C, :], 0.0, None, ALU.min)
            magnitude(lf[:, 0, :], gts[32:32 + INNER_C, :]).then_inc(absf_done, 1)
            parts_low(0, 1)
            d.wait_ge(lnf_done, 1)
            link(d.tensor_tensor(lf[:, 3, :], lf[:, 2, :], lf[:, 1, :], ALU.subtract))
            d.wait_ge(consts, 2)
            link(d.tensor_tensor_scan(lcum[:, :], restart_mul[:, :, :].rearrange("p b t -> p (b t)"), lf[:, 3, :], 0.0,
                                      ALU.mult, ALU.add))
            d.tensor_tensor(arow[:, :], gts[0:INNER_C, :], lcum[:, :], ALU.subtract).then_inc(arow_in, 1)
            d.wait_ge(arow_in, 1)
            d.tensor_tensor_scan(mrow[:, :], restart_add[:, :, :].rearrange("p b t -> p (b t)"), arow[:, :], NEG,
                                 ALU.add, ALU.max).then_inc(mrow_in, 1)
            parts_low(2)
            d.wait_ge(gate_hi, 1)
            d.tensor_tensor(rrow[:, 0, :], arow[:, :], a3[0:INNER_C, 0:T], ALU.subtract).then_inc(gate_rest, 1)
            d.wait_ge(mrow_in, 1)
            d.wait_ge(gate_hi, 2)
            d.scalar_tensor_tensor(out=rrow[:, 1, :], in0=mrow[:, :], scalar=-1.0, in1=m3[0:INNER_C, 0:T],
                                   op0=ALU.mult, op1=ALU.subtract).then_inc(gate_rest, 1)
            parts_low(3)
            d.tensor_tensor(nrow[:, :], mrow[:, :], lcum[:, :], ALU.add).then_inc(nrow_in, 1)
            for i, parts in enumerate((a3, m3)):
                d.wait_ge(gate_rest, i + 1)
                d.wait_ge(gate_mid, i + 1)
                d.tensor_tensor(parts[64:64 + INNER_C, 0:T], rrow[:, i, :], mid[:, i, :], ALU.subtract).then_inc(arow_done, 1)
            parts_low(*range(4, 8))
            d.wait_ge(wmean_mm, 1)
            link(d.tensor_scalar(wmean[:, :], bank[7][:, 64:66], 1.0 / (D * 1024), 1e-5, ALU.mult, ALU.max))
            d.reciprocal(wscale[:, :], wmean[:, :]).then_inc(wmean_done, 1)

            def weights(g):
                d.wait_ge(d_done, g + 1)
                d.wait_ge(s_mm, g + 1)
                if g >= 2:
                    d.wait_ge(c_split, g - 1)
                d.tensor_tensor(cmat[:, g % 2, :], bank[g % 2][0:GT, 0:INNER_C * GT],
                                dmat[:, g % 2, :, :].rearrange("p c s -> p (c s)"), ALU.mult).then_inc(c_done, 1)

            def weights_low(g):
                d.wait_ge(c_done, g + 1)
                d.wait_ge(c_high, g + 1)
                high, low = (c_hl[:, g % 2, w, 0:INNER_C * GT] for w in range(2))
                d.tensor_tensor(low, cmat[:, g % 2, :], high, ALU.subtract).then_inc(c_split, 1)

            def aggregate(g):
                d.wait_ge(hstat_done, g + 1)
                for n in range(g * INNER_C, (g + 1) * INNER_C):
                    ins = d.bn_aggr(mv[:, n, :], stat[:, n, :])
                return ins

            weights(0)
            weights_low(0)
            for g in range(G):
                if g + 1 < G:
                    weights(g + 1)
                if g >= 1:
                    aggregate(g - 1)
                if g + 1 < G:
                    weights_low(g + 1)
                d.wait_ge(hv_mm, g + 1)
                for c in range(INNER_C):
                    ins = d.bn_stats(stat[:, g * INNER_C + c, :], bank[4 + g % 2][0:GT, c * DH:(c + 1) * DH])
                ins.then_inc(hstat_done, 1)
            ins = aggregate(G - 1)
            d.wait_ge(floor_mm, 1)
            d.tensor_copy(floor_t[:, :], bank[7][0:GT, 0:G * INNER_C])
            link(d.tensor_copy(csum[:, :], bank[6][0:GT, 0:G * INNER_C]))
            link(magnitude(csum[:, :], csum[:, :]))
            link(d.tensor_tensor(csum[:, :], csum[:, :], floor_t[:, :], ALU.max))
            link(d.tensor_scalar(csum[:, :], csum[:, :], 1e-6, None, ALU.add))
            link(d.reciprocal(tiny[:, 0, :], csum[:, :]))
            link(d.tensor_tensor(tiny[:, 1, :], tiny[:, 0, :], tiny[:, 0, :], ALU.mult))
            d.tensor_tensor(tiny[:, 2, :], tiny[:, 1, :], mv[:, :, 1], ALU.mult).then_inc(hvar_done, 1)
            d.wait_ge(hstd_done, 1)
            link(d.reciprocal(tiny[:, 4, :], tiny[:, 3, :]))
            link(d.tensor_tensor(tiny[:, 5, :], tiny[:, 4, :], tiny[:, 0, :], ALU.mult))
            d.scalar_tensor_tensor(out=tiny[:, 1, :], in0=mv[:, :, 0], scalar=-1.0, in1=tiny[:, 5, :],
                                   op0=ALU.mult, op1=ALU.mult).then_inc(hcoef_done, 1)
            d.wait_ge(hraw_done, G)
            c = INNER_C - 1
            for g in range(G):
                n = g * INNER_C + c
                d.tensor_scalar(hraw[0:GT, g, c * DH:(c + 1) * DH], hraw[0:GT, g, c * DH:(c + 1) * DH],
                                mv[:, n, 0:1], tiny[:, 5, n:n + 1], ALU.subtract, ALU.mult).then_inc(hnv_done, 1)
            d.wait_ge(skip_done, INNER_C)
            for g in range(G):
                d.wait_ge(ht_mm, g + 1)
                tok = slice(g * GT, (g + 1) * GT)
                link(d.tensor_tensor(hst[:, :, tok], bank[g % 2][:, 0:INNER_C * GT].rearrange("p (c t) -> p c t", c=INNER_C),
                                     zs[:, :, tok], ALU.mult))
                d.tensor_tensor(hst[:, :, tok], hst[:, :, tok], xc[:, :, tok], ALU.add).then_inc(hst_done, 1)
            add_to_h(1, bank[2:4] + bank[6:8], down0_mm, 1)
            layer_norm(1)

            for hf in range(2):
                tok = slice(hf * HT, (hf + 1) * HT)
                d.wait_ge(xhi_done, hf + 1)
                d.tensor_tensor(xlo[:, :, tok], xn[:, :, tok], xhi[:, :, tok], ALU.subtract).then_inc(xlo_done, 1)
            def hidden(up_bank, mask_bank, s, n):
                d.wait_ge(silu_done, n + 1)
                d.wait_ge(uproj_mm, n + 1)
                d.tensor_tensor(gu[:, s, :], sg[:, s, :], up_bank[:, 0:HT], ALU.mult).then_inc(gu_done, 1)
                d.wait_ge(gu_done, n + 1)
                if mask_bank is None:
                    d.tensor_copy(act[:, s, :], gu[:, s, :]).then_inc(act_done, 1)
                else:
                    d.wait_ge(mask_mm, n - 1)
                    d.tensor_tensor(act[:, s, :], gu[:, s, :], mask_bank[:, 0:HT], ALU.mult).then_inc(act_done, 1)
                    d.wait_ge(down_mm, n - 1)
                d.wait_ge(act_done, n + 1)
                d.tensor_copy(ahi[:, s, :], act[:, s, :]).then_inc(ahi_done, 1)
                d.wait_ge(ahi_done, n + 1)
                d.tensor_tensor(alo[:, s, :], act[:, s, :], ahi[:, s, :], ALU.subtract).then_inc(alo_done, 1)

            hidden(bank[5], None, 0, 0)
            d.wait_ge(aff_done, 1)
            for g in range(G):
                ins = d.max(top[:, g, :], aff[:, g, :])
            link(ins)
            for g in range(G):
                d.match_replace(rest[:, g, :], top[:, g, :], aff[:, g, :], 0.0)
            link(d.tensor_reduce(den[:, 0, :], top[:, :, :], AX, ALU.add))
            link(d.tensor_scalar(den[:, 1, :], den[:, 0, :], 1e-9, None, ALU.add))
            link(d.reciprocal(den[:, 2, :], den[:, 1, :]))
            link(d.tensor_tensor(rest[:, :, :], aff[:, :, :], rest[:, :, :], ALU.subtract))
            link(d.tensor_tensor(rest[:, :, :], rest[:, :, :], den[:, 2, :].unsqueeze(2).broadcast_to([GT, G, E]), ALU.mult))
            link(d.tensor_copy(mask_hl[:, :, 0:E], rest[:, :, :]))
            d.tensor_tensor(mask_hl[:, :, E:2 * E], rest[:, :, :], mask_hl[:, :, 0:E], ALU.subtract).then_inc(mask_done, 1)

            d.wait_ge(maskt_mm, 1)
            d.tensor_copy(maskT[:, :].rearrange("p (g t) -> p g t", g=G),
                          bank[4][:, :].bitcast(F16).rearrange("p (g t) -> p g t", g=G)[:, :, 0:GT]).then_inc(maskt_done, 1)
            hidden(bank[7], None, 1, 1)

            def four_experts(it):
                for j in range(4):
                    for hf in range(2):
                        r = 3 * (2 * j + hf)
                        hidden(bank[4 + (r + 1) % 4], bank[4 + (r + 2) % 4], hf, it * 8 + (2 * j + hf + 2))

            with d.Fori(0, LOOPS) as it:
                four_experts(it)
            four_experts(LOOPS)
            for hf in range(2):
                d.wait_ge(down_mm, 2 * E + 1 + hf)
                for m in range(DC):
                    d.tensor_tensor(half(h, m, hf), half(h, m, hf), bank[2 * hf + m][:, 0:HT], ALU.add).then_inc(h_ready, 1)
            centre(2, 0)
            layer_norm(2)

            def low_part(n):
                qk, hf, m = n // 4, n // 2 % 2, n % 2
                hl = (q1_hl, k1_hl)[qk]
                d.wait_ge(rope_hi, n + 1)
                d.tensor_tensor(half(hl[:, 1], m, hf), rsum[:, n % 2, :], half(hl[:, 0], m, hf), ALU.subtract).then_inc(rope_done, 1)

            for hf in range(2):
                d.wait_ge(xdhi_done, hf + 1)
                im = slice(hf * HB, (hf + 1) * HB)
                d.tensor_tensor(xdup[:, 1, :, im, 0, :], xn[:, :, hf * HT:(hf + 1) * HT].rearrange("p c (b t) -> p c b t", t=POS),
                                xdup[:, 0, :, im, 0, :], ALU.subtract).then_inc(xdlo_done, 1)

            n = 0
            for qk in range(2):
                for hf in range(2):
                    for m in range(DC):
                        d.wait_ge(rope_mm, n + 1)
                        if n >= 2:
                            d.wait_ge(rope_sum, n - 1)
                        for sw in range(2):
                            if n + sw == 0:
                                d.wait_ge(ld_bit, 48)
                            ins = d.scalar_tensor_tensor(
                                out=images(rt[:, n % 2, sw, :]), in0=images(bank[2 * (n % 2) + sw][:, 0:HT]),
                                scalar=col(("bq", "bq_swap", "bk", "bk_swap")[2 * qk + sw], m),
                                in1=ropew[:, sw, :].unsqueeze(1).broadcast_to([128, HB, POS]), op0=ALU.add, op1=ALU.mult)
                        ins.then_inc(rope_t, 1)
                        if n >= 1:
                            low_part(n - 1)
                        if n == 2:
                            d.wait_ge(xdlo_done, 2)
                            d.tensor_copy(xdup[:, 1, :, :, 2, :].rearrange("p c b t -> p (c b) t"),
                                          xdup[:, 1, :, :, 0, :].rearrange("p c b t -> p (c b) t")).then_inc(xdlast_done, 1)
                        n += 1
            low_part(7)
            d.wait_ge(rope_done, 8)
            def v1_low(n):
                d.wait_ge(v1hi_done, n + 1)
                d.tensor_tensor(v1[0:POS, 2 * n:2 * n + 2, :], bank[4 + n % 4][0:POS, :].rearrange("p (b m) -> p b m", b=2),
                                v1[0:POS, 2 * n:2 * n + 2, :], ALU.subtract).then_inc(v1lo_done, 1)

            def mask_queries(part, head):
                for w in range(2):
                    ins = d.tensor_scalar(queries_at(qm[:, w], part, head), queries_at(q1_hl[:, w], part),
                                          head_col[:, head:head + 1], None, ALU.mult)
                ins.then_inc(qm_done, 1)

            for n in range(4):
                v1_low(n)
                mask_queries(0, 4 + n)
            v1_low(4)
            v1_low(5)
            U = 3 * POS

            def scores_of(n):
                return bank[n % 2][0:U, 0:12 * POS].rearrange("p (n t) -> p n t", t=POS)

            def maxima(n):
                d.wait_ge(sc_mm, n + 1)
                d.tensor_reduce(smx[0:U, n % 2, 0, :], scores_of(n), AX, ALU.max).then_inc(max_done, 1)

            def subtract_max(n):
                d.wait_ge(max_done, n + 1)
                d.tensor_tensor(pr[0:U, n % 2, :, :], scores_of(n),
                                smx[0:U, n % 2, 0, :].unsqueeze(2).broadcast_to([U, 12, POS]), ALU.subtract).then_inc(sc_sub, 1)

            maxima(0)
            subtract_max(0)
            maxima(1)
            subtract_max(1)
            maxima(2)

            def quotients(n):
                d.wait_ge(sc_exp, n + 1)
                e = pr[0:U, n % 2, :, :]
                link(d.tensor_reduce(smx[0:U, n % 2, 1, :], e, AX, ALU.add))
                link(d.reciprocal(smx[0:U, n % 2, 2, :], smx[0:U, n % 2, 1, :]))
                d.tensor_tensor(e, e, smx[0:U, n % 2, 2, :].unsqueeze(2).broadcast_to([U, 12, POS]), ALU.mult).then_inc(quot_done, 1)
                d.wait_ge(quot_done, n + 1)
                if n >= 2:
                    d.wait_ge(pt_mm, 2 * (n - 1))
                d.tensor_copy(ph[0:U, n % 2, :, 1, :], e).then_inc(p_again, 1)

            quotients(0)
            for n in range(G):
                if n + 1 < G:
                    quotients(n + 1)
                if n < 2:
                    v1_low(6 + n)
                if n + 2 < G:
                    d.wait_ge(p_done, n + 1)
                    subtract_max(n + 2)
                if n < 2:
                    for head in ((5, 6), (7,))[n]:
                        mask_queries(1, head)
                if n + 3 < G:
                    maxima(n + 3)
            add_to_h(3, bank[6:8] + bank[0:2], wo_mm, 0)
            layer_norm(3)

            def token_scales(n):
                for i in range(2):
                    if i == 0:
                        d.wait_ge(amaxt_mm, n + 1)
                    ins = d.tensor_reduce(tmx[:, 4 * i:4 * i + 4], bank[4 + i][0:GT, :].rearrange("p (g f) -> p g f", g=4), AX, ALU.max)
                link(ins)
                link(d.tensor_scalar(tsc[:, 1, :], tmx[:, :], 1e-5, 1.0 / 127.0, ALU.max, ALU.mult))
                d.reciprocal(tsc[:, 0, :], tsc[:, 1, :]).then_inc(tsc_done, 1)
                d.wait_ge(tsct_mm, n + 1)
                for kind in range(2):
                    d.tensor_tensor(spread[:, kind, :, :], bank[6][0:2 * G, 0:GT].unsqueeze(1).broadcast_to([2 * G, G, GT]),
                                    ident[0:2 * G, kind * G:(kind + 1) * G].unsqueeze(2).broadcast_to([2 * G, G, GT]),
                                    ALU.mult).then_inc(tsct_done, 1)

            def inverse_scales(n):
                d.wait_ge(bc_mm, 4 * n + 4)
                for i in range(2):
                    ins = d.tensor_scalar(binv[:, i * HT:(i + 1) * HT], bank[6 + i][:, 0:HT], wmean[:, n:n + 1], None, ALU.mult)
                ins.then_inc(bc_done, 1)

            def quantize(dst, src, hf, done, by):
                n = src.shape[1]
                link(d.tensor_tensor(src, src, bank[4 + hf][:, 0:HT].unsqueeze(1).broadcast_to([128, n, HT]), ALU.mult))
                link(d.tensor_scalar(src, src, 127.0, -128.0, ALU.min, ALU.max))
                d.tensor_scalar(dst, src, MAGIC, MAGIC, ALU.add, ALU.subtract).then_inc(done, by)

            d.wait_ge(xn_ready, 8)
            link(magnitude(habs[:, 0, :], xn[:, 0, :]))
            d.wait_ge(habs_done, 1)
            d.tensor_tensor(amax, habs[:, 0, :], habs[:, 1, :], ALU.max).then_inc(amax_done, 1)
            token_scales(0)
            for hf in range(2):
                d.wait_ge(bc_mm, hf + 1)
                tok = slice(hf * HT, (hf + 1) * HT)
                quantize(x4q[:, :, tok], xn[:, :, tok], hf, xq_done, 2)
            inverse_scales(0)
            d.wait_ge(bc_done, 1)
            def outer_taps(c):
                d.wait_ge(fconv_first, c + 1)
                for k in (0, 2):
                    to, of = (slice(1, POS), slice(0, POS - 1)) if k == 0 else (slice(0, POS - 1), slice(1, POS))
                    into = images(h2[:, c, :])[:, :, to]
                    ins = d.scalar_tensor_tensor(out=into, in0=images(hid[:, c, :])[:, :, of],
                                                 scalar=col("ffn_conv_w", 3 * c + k), in1=into,
                                                 op0=ALU.mult, op1=ALU.add)
                    if k == 0:
                        link(ins)
                ins.then_inc(fconv_done, 1)

            def maximum(i):
                d.wait_ge(habs_done, i + 2)
                ins = d.tensor_tensor(amax, amax if i > 1 else habs[:, TAP_ORDER[0], :], habs[:, TAP_ORDER[i], :], ALU.max)
                if i < FC - 1:
                    link(ins)
                else:
                    ins.then_inc(amax_done, 1)

            for s in range(FC + 1):
                if s < FC:
                    for hf in range(2):
                        d.wait_ge(w1_mm, 2 * s + hf + 1)
                        d.tensor_tensor(half(hid, s, hf), bank[(2 * s + hf) % 4][:, 0:HT], binv[:, hf * HT:(hf + 1) * HT],
                                        ALU.mult).then_inc(hid_done, 1)
                if s >= 1 and s - 1 not in POOL_TAPS:
                    outer_taps(s - 1)
                if s >= 5:
                    maximum(s - 4)
            for i in range(FC - 3, FC):
                maximum(i)
            token_scales(1)
            for hf in range(2):
                d.wait_ge(bc_mm, 4 + hf + 1)
                for c in (0, 4):
                    src = h2[:, c:c + 4, hf * HT:(hf + 1) * HT]
                    link(d.tensor_tensor(src, src, bank[4 + hf][:, 0:HT].unsqueeze(1).broadcast_to([128, 4, HT]), ALU.mult))
                    if (hf, c) != (1, 4):
                        d.tensor_scalar(src, src, 127.0, -128.0, ALU.min, ALU.max).then_inc(clipped, 1)
                    else:
                        link(d.tensor_scalar(src, src, 127.0, -128.0, ALU.min, ALU.max))
                        d.tensor_scalar(h2q[:, c:c + 4, HT:2 * HT], src, MAGIC, MAGIC, ALU.add, ALU.subtract).then_inc(last_rounded, 1)
            inverse_scales(1)
            d.wait_ge(bc_done, 2)
            for hf in range(2):
                for m in range(DC):
                    tok = slice(hf * HT, (hf + 1) * HT)
                    d.wait_ge(w2_mm, 2 * hf + m + 1)
                    link(d.tensor_tensor(half(sq, m, hf), bank[2 * hf + m][:, 0:HT], binv[:, tok], ALU.mult))
                    d.tensor_tensor(half(h, m, hf), half(h, m, hf), half(sq, m, hf), ALU.add).then_inc(h_ready, 1)


def _kmajor(w):
    k, m = w.shape
    return w.reshape(k // 128, 128, m).transpose(1, 0, 2)


def _columns(v):
    return v.reshape(-1, 128).T


def _rope_tables():
    import numpy as np
    freqs = np.float32(10000.0) ** (-np.arange(0, HD1, 2).astype(np.float32) / np.float32(HD1))
    ang = np.arange(POS, dtype=np.float32)[None, :] * freqs[:, None].astype(np.float32)
    f = (np.arange(128) % HD1) // 2
    sign = np.where(np.arange(128) % 2 == 0, -1.0, 1.0).astype(np.float32)[:, None]
    return np.stack([np.cos(ang)[f], np.sin(ang)[f] * sign], axis=1).astype(np.float32)


def _layouts(i):
    import numpy as np
    x = i["x"].reshape(B, 3, 6, 16, 6, 16).transpose(1, 3, 5, 0, 2, 4).reshape(TOK_K * 128, B * PATCHES)
    swap = np.arange(D) ^ 1
    gate_b = np.zeros((128, 1), np.float32)
    gate_b[0:4, 0], gate_b[32:36, 0] = i["L0_attn_b_ig"], i["L0_attn_b_fg"]
    w_gates = np.zeros((1536, 64), np.float32)
    w_gates[:, 0:4], w_gates[:, 32:36] = i["L0_attn_w_ig"].T, i["L0_attn_w_fg"].T
    cw = i["L0_attn_conv_w"].reshape(INNER_C, 128, CONV).transpose(1, 0, 2).reshape(128, -1)
    fw = i["L1_ffn_conv_w"].reshape(FC, 128, 3).transpose(1, 0, 2).reshape(128, -1)
    cols = np.concatenate([
        _columns(i["L0_tok_b"]), _columns(i["L0_tok_cls_token"].reshape(-1)), cw, _columns(i["L0_attn_conv_b"]),
        _columns(i["L0_attn_ln_w"].reshape(-1)), _columns(i["L0_attn_skip"]), gate_b,
        _columns(i["L1_attn_bq"]), _columns(i["L1_attn_bq"][swap]), _columns(i["L1_attn_bk"]),
        _columns(i["L1_attn_bk"][swap]), _columns(i["L1_attn_bv"]), fw, _columns(i["L1_ffn_conv_b"])], axis=1)
    heads = [i[f"L0_attn_w_{n}"] for n in "qkv"]
    blocks = np.concatenate([_kmajor(w.transpose(0, 2, 1).reshape(512, 4)) for w in heads], axis=1)
    blocks_t = np.concatenate([_kmajor(w.reshape(512, 4)) for w in heads], axis=1)

    def expert(gate, up, down):
        n = gate.shape[0]
        rows = [w.reshape(n, 2, 128, 128).transpose(0, 2, 1, 3).reshape(n, 128, 256) for w in (gate, up)]
        return np.concatenate([*rows, down], axis=2)

    shared = expert(*(i[f"L0_ffn_shared_{n}_w"][None] for n in ("gate", "up", "down")))[0]
    experts = expert(*(i[f"L0_ffn_expert_{n}_k"] for n in ("gate", "up", "down"))).transpose(1, 0, 2)
    wq, wk = i["L1_attn_Wq"], i["L1_attn_Wk"]
    l1_w = np.stack([_kmajor(w.T) for w in (wq, wq[swap], wk, wk[swap], i["L1_attn_Wv"], i["L1_attn_Wo"])], axis=1)
    return {
        "patches": _kmajor(x), "tok_w": _kmajor(i["L0_tok_W"].T), "pos": _kmajor(i["L0_tok_pos_enc"][0].T),
        "cols": cols, "w_up": _kmajor(i["L0_attn_w_up"].T), "blocks": blocks, "blocks_t": blocks_t,
        "w_gates": _kmajor(w_gates), "w_down": _kmajor(i["L0_attn_w_down"].T),
        "w_router": _kmajor(i["L0_ffn_router_w"]), "w_shared": shared, "w_experts": experts, "l1_w": l1_w,
        "rope": _rope_tables(), "ffn_w1": _kmajor(i["L1_ffn_w1"].T), "ffn_w2": _kmajor(i["L1_ffn_w2"].T),
    }


def kernel(**inputs):
    import numpy as np
    import concourse.bacc as bacc
    from concourse.bass_utils import run_bass_kernel_spmd

    nc = bacc.Bacc("TRN2", target_bir_lowering=False, num_devices=1)
    arrays = {k: np.ascontiguousarray(v) for k, v in _layouts({k: np.asarray(v) for k, v in inputs.items()}).items()}
    args = {k: nc.dram_tensor(k, v.shape, mybir.dt.from_np(v.dtype), kind="ExternalInput").ap() for k, v in arrays.items()}
    out = nc.dram_tensor("out", (128, DC, T), F32, kind="ExternalOutput").ap()
    vit_tower(nc, out=out, **args)
    r = run_bass_kernel_spmd(nc, [arrays], core_ids=[0])
    return r.results[0]["out"].transpose(2, 1, 0).reshape(B, POS, D)
```
